# Optimizing a Trainium2 kernel written in Bass

```python
import numpy as np
import jax
import jax.numpy as jnp

def _softmax(x, axis=-1):
    return jax.nn.softmax(x, axis=axis)

def _gelu(x):
    return jax.nn.gelu(x, approximate=True)

def _silu(x):
    return jax.nn.silu(x)

def _sigmoid(x):
    return jax.nn.sigmoid(x)

def _layernorm(x, axis=-1, eps=1e-05):
    m = jnp.mean(x, axis=axis, keepdims=True)
    v = jnp.var(x, axis=axis, keepdims=True)
    return (x - m) / jnp.sqrt(v + eps)

def _scatter_add(tgt, idx, src, axis=0):
    return tgt.at[idx].add(src)

def _segment_sum(src, seg, n):
    return jax.ops.segment_sum(src, seg, n)
kernel_name = 'mk_audio_tower_d2_tok_audfeat768_r4_840298'

def setup_inputs(seed: int=0):
    np.random.seed(seed)
    _w = jnp.asarray

    def _rec_inputs():
        import jax
        import jax.numpy as jnp
        _rk = jax.random.key(seed)
        x = -0.000253961 + 1 * jax.random.normal(jax.random.fold_in(_rk, 1), (64, 90, 375), jnp.float32)
        return x
    x = _rec_inputs()

    def _L0_tok_setup():
        import jax, jax.numpy as jnp
        import numpy as np
        CHANNELS = 90
        PATCH = 16
        EMBED = 192
        key = jax.random.key(seed)
        k_x, k_w, k_b = jax.random.split(key, 3)
        in_feat = CHANNELS * PATCH
        x = jax.random.normal(k_x, (128, CHANNELS, 512), dtype=jnp.float32)
        bound = 1.0 / np.sqrt(in_feat)
        W = jax.random.uniform(k_w, (EMBED, in_feat), dtype=jnp.float32, minval=-bound, maxval=bound)
        b = jax.random.uniform(k_b, (EMBED,), dtype=jnp.float32, minval=-bound, maxval=bound)
        return {'x': x, 'W': W, 'b': b}
    _L0_tok_all = _L0_tok_setup()
    _L0_tok_in = {k: v for k, v in _L0_tok_all.items() if k in ('W', 'b')}
    del _L0_tok_all

    def _L0_attn_setup():
        import jax, jax.numpy as jnp
        import numpy as np
        NUM_HEADS = 12

        def rotate_every_two(x):
            x1 = x[..., ::2]
            x2 = x[..., 1::2]
            return jnp.stack((-x2, x1), axis=-1).reshape(x.shape)

        def rope_cos_sin(seq_len, dim):
            inv_freq = 1.0 / 10000.0 ** (jnp.arange(0, dim, 2, dtype=jnp.float32) / dim)
            t = jnp.arange(seq_len, dtype=jnp.float32)
            freqs = t[:, None] * inv_freq[None, :]
            emb = jnp.concatenate([freqs, freqs], axis=-1)
            return (jnp.cos(emb)[None, None], jnp.sin(emb)[None, None])
        key = jax.random.key(seed)
        kx, k1, k2, k3, k4 = jax.random.split(key, 5)
        B, S, D = (1, 1024, 192)
        scale = 1.0 / np.sqrt(D)
        x = jax.random.normal(kx, (B, S, D), dtype=jnp.float32)
        W_qkv = jax.random.normal(k1, (D, 3 * D), dtype=jnp.float32) * scale
        b_qkv = jax.random.normal(k2, (3 * D,), dtype=jnp.float32) * 0.01
        W_out = jax.random.normal(k3, (D, D), dtype=jnp.float32) * scale
        b_out = jax.random.normal(k4, (D,), dtype=jnp.float32) * 0.01
        return {'x': x, 'W_qkv': W_qkv, 'b_qkv': b_qkv, 'W_out': W_out, 'b_out': b_out}
    _L0_attn_all = _L0_attn_setup()
    _L0_attn_in = {k: v for k, v in _L0_attn_all.items() if k in ('W_qkv', 'b_qkv', 'W_out', 'b_out')}
    del _L0_attn_all

    def _L0_ffn_setup():
        import jax, jax.numpy as jnp
        import numpy as np
        import math
        B, S, D = (4, 1024, 192)
        E = 8
        TOP_K = 2
        H = 512
        CAP_F = 1.25
        EPS = 1e-06
        ALPHA = 1.0
        key = jax.random.key(seed)
        k0, k1, k2, k3 = jax.random.split(key, 4)
        x = jax.random.normal(k0, (B, S, D), jnp.float32)
        gate_w = jax.random.normal(k1, (E, D), jnp.float32) * 0.02
        w13 = jax.random.normal(k2, (E, 2 * H, D), jnp.float32) * 0.02
        w2 = jax.random.normal(k3, (E, D, H), jnp.float32) * 0.02
        norm_w = jnp.ones((E, D), jnp.float32)
        return {'x': x, 'gate_w': gate_w, 'w13': w13, 'w2': w2, 'norm_w': norm_w}
    _L0_ffn_all = _L0_ffn_setup()
    _L0_ffn_in = {k: v for k, v in _L0_ffn_all.items() if k in ('gate_w', 'w13', 'w2', 'norm_w')}
    del _L0_ffn_all

    def _L1_attn_setup():
        import jax, jax.numpy as jnp
        import numpy as np
        D_MODEL = 192
        N_LAYER = 4
        D_INNER = 2 * D_MODEL
        D_STATE = 16
        D_CONV = 4
        DT_RANK = (D_MODEL + 15) // 16
        EPS = 1e-05

        def _ln(x, w, b):
            mu = jnp.mean(x, axis=-1, keepdims=True)
            var = jnp.mean(jnp.square(x - mu), axis=-1, keepdims=True)
            return (x - mu) * jax.lax.rsqrt(var + EPS) * w + b

        def _mixer(u, p):
            B, L, _ = u.shape
            xz = jnp.einsum('bld,ed->ble', u, p['in_proj_w'])
            x, z = jnp.split(xz, 2, axis=-1)
            xp = jnp.pad(x, ((0, 0), (D_CONV - 1, 0), (0, 0)))
            x = sum((p['conv_w'][:, k] * xp[:, k:k + L, :] for k in range(D_CONV))) + p['conv_b']
            x = jax.nn.silu(x)
            x_dbl = jnp.einsum('bld,ed->ble', x, p['x_proj_w'])
            dt, Bm, Cm = jnp.split(x_dbl, [DT_RANK, DT_RANK + D_STATE], axis=-1)
            dt = jax.nn.softplus(jnp.einsum('blr,dr->bld', dt, p['dt_proj_w']) + p['dt_proj_b'])
            A = -jnp.exp(p['A_log'])

            def step(h, xs):
                dt_t, B_t, C_t, x_t = xs
                dA = jnp.exp(dt_t[:, :, None] * A)
                h = dA * h + (dt_t * x_t)[:, :, None] * B_t[:, None, :]
                y = jnp.einsum('bds,bs->bd', h, C_t)
                return (h, y)
            h0 = jnp.zeros((B, D_INNER, D_STATE), x.dtype)
            xs = (dt.transpose(1, 0, 2), Bm.transpose(1, 0, 2), Cm.transpose(1, 0, 2), x.transpose(1, 0, 2))
            _, ys = jax.lax.scan(step, h0, xs)
            y = ys.transpose(1, 0, 2) + x * p['D_skip']
            y = y * jax.nn.silu(z)
            return jnp.einsum('bld,ed->ble', y, p['out_proj_w'])
        key = jax.random.key(seed)
        ks = jax.random.split(key, 8)
        s = 0.02
        n, dm, di = (N_LAYER, D_MODEL, D_INNER)
        return {'embeddings': jax.random.normal(ks[0], (2, 256, dm), jnp.float32), 'norm_w': jnp.ones((n, dm), jnp.float32), 'norm_b': jnp.zeros((n, dm), jnp.float32), 'in_proj_w': jax.random.normal(ks[1], (n, 2 * di, dm), jnp.float32) * s, 'conv_w': jax.random.normal(ks[2], (n, di, D_CONV), jnp.float32) * s, 'conv_b': jnp.zeros((n, di), jnp.float32), 'x_proj_w': jax.random.normal(ks[3], (n, DT_RANK + 2 * D_STATE, di), jnp.float32) * s, 'dt_proj_w': jax.random.normal(ks[4], (n, di, DT_RANK), jnp.float32) * s, 'dt_proj_b': jnp.full((n, di), float(np.log(np.expm1(0.01))), jnp.float32), 'A_log': jnp.broadcast_to(jnp.log(jnp.arange(1, D_STATE + 1, dtype=jnp.float32)), (n, di, D_STATE)) + jnp.zeros((n, di, D_STATE), jnp.float32), 'D_skip': jnp.ones((n, di), jnp.float32), 'out_proj_w': jax.random.normal(ks[5], (n, dm, di), jnp.float32) * s, 'norm_f_w': jnp.ones((dm,), jnp.float32), 'norm_f_b': jnp.zeros((dm,), jnp.float32)}
    _L1_attn_all = _L1_attn_setup()
    _L1_attn_in = {k: v for k, v in _L1_attn_all.items() if k in ('norm_w', 'norm_b', 'in_proj_w', 'conv_w', 'conv_b', 'x_proj_w', 'dt_proj_w', 'dt_proj_b', 'A_log', 'D_skip', 'out_proj_w', 'norm_f_w', 'norm_f_b')}
    del _L1_attn_all

    def _L1_ffn_setup():
        import jax, jax.numpy as jnp
        import numpy as np
        B, T, D, H, E = (4, 512, 192, 768, 8)
        key = jax.random.key(seed)
        ks = jax.random.split(key, 7)
        s_d = 1.0 / np.sqrt(D)
        s_h = 1.0 / np.sqrt(H)
        return {'x': jax.random.normal(ks[0], (B, T, D), dtype=jnp.float32), 'Wg': jax.random.normal(ks[1], (E, D), dtype=jnp.float32) * s_d, 'bg': jax.random.normal(ks[2], (E,), dtype=jnp.float32) * 0.01, 'W1': jax.random.normal(ks[3], (E, D, H), dtype=jnp.float32) * s_d, 'b1': jax.random.normal(ks[4], (E, H), dtype=jnp.float32) * s_d, 'W2': jax.random.normal(ks[5], (E, H, D), dtype=jnp.float32) * s_h, 'b2': jax.random.normal(ks[6], (E, D), dtype=jnp.float32) * s_h}
    _L1_ffn_all = _L1_ffn_setup()
    _L1_ffn_in = {k: v for k, v in _L1_ffn_all.items() if k in ('Wg', 'bg', 'W1', 'b1', 'W2', 'b2')}
    del _L1_ffn_all
    return {'x': x, 'L0_tok_W': _L0_tok_in['W'], 'L0_tok_b': _L0_tok_in['b'], 'L0_attn_W_qkv': _L0_attn_in['W_qkv'], 'L0_attn_b_qkv': _L0_attn_in['b_qkv'], 'L0_attn_W_out': _L0_attn_in['W_out'], 'L0_attn_b_out': _L0_attn_in['b_out'], 'L0_ffn_gate_w': _L0_ffn_in['gate_w'], 'L0_ffn_w13': _L0_ffn_in['w13'], 'L0_ffn_w2': _L0_ffn_in['w2'], 'L0_ffn_norm_w': _L0_ffn_in['norm_w'], 'L1_attn_norm_w': _L1_attn_in['norm_w'], 'L1_attn_norm_b': _L1_attn_in['norm_b'], 'L1_attn_in_proj_w': _L1_attn_in['in_proj_w'], 'L1_attn_conv_w': _L1_attn_in['conv_w'], 'L1_attn_conv_b': _L1_attn_in['conv_b'], 'L1_attn_x_proj_w': _L1_attn_in['x_proj_w'], 'L1_attn_dt_proj_w': _L1_attn_in['dt_proj_w'], 'L1_attn_dt_proj_b': _L1_attn_in['dt_proj_b'], 'L1_attn_A_log': _L1_attn_in['A_log'], 'L1_attn_D_skip': _L1_attn_in['D_skip'], 'L1_attn_out_proj_w': _L1_attn_in['out_proj_w'], 'L1_attn_norm_f_w': _L1_attn_in['norm_f_w'], 'L1_attn_norm_f_b': _L1_attn_in['norm_f_b'], 'L1_ffn_Wg': _L1_ffn_in['Wg'], 'L1_ffn_bg': _L1_ffn_in['bg'], 'L1_ffn_W1': _L1_ffn_in['W1'], 'L1_ffn_b1': _L1_ffn_in['b1'], 'L1_ffn_W2': _L1_ffn_in['W2'], 'L1_ffn_b2': _L1_ffn_in['b2']}

def reference(x, L0_tok_W, L0_tok_b, L0_attn_W_qkv, L0_attn_b_qkv, L0_attn_W_out, L0_attn_b_out, L0_ffn_gate_w, L0_ffn_w13, L0_ffn_w2, L0_ffn_norm_w, L1_attn_norm_w, L1_attn_norm_b, L1_attn_in_proj_w, L1_attn_conv_w, L1_attn_conv_b, L1_attn_x_proj_w, L1_attn_dt_proj_w, L1_attn_dt_proj_b, L1_attn_A_log, L1_attn_D_skip, L1_attn_out_proj_w, L1_attn_norm_f_w, L1_attn_norm_f_b, L1_ffn_Wg, L1_ffn_bg, L1_ffn_W1, L1_ffn_b1, L1_ffn_W2, L1_ffn_b2):
    import jax
    import jax.numpy as jnp

    def _L0_tok_ref(x, W, b):
        import jax, jax.numpy as jnp
        import numpy as np
        CHANNELS = 90
        PATCH = 16
        EMBED = 192
        B, C, T = x.shape
        n = T // PATCH
        patches = x[:, :, :n * PATCH].reshape(B, C, n, PATCH)
        patches = patches.transpose(0, 2, 1, 3).reshape(B, n, C * PATCH)
        return jnp.einsum('bnf,ef->bne', patches, W) + b

    def _L0_attn_ref(x, W_qkv, b_qkv, W_out, b_out):
        import jax, jax.numpy as jnp
        import numpy as np
        NUM_HEADS = 12

        def rotate_every_two(x):
            x1 = x[..., ::2]
            x2 = x[..., 1::2]
            return jnp.stack((-x2, x1), axis=-1).reshape(x.shape)

        def rope_cos_sin(seq_len, dim):
            inv_freq = 1.0 / 10000.0 ** (jnp.arange(0, dim, 2, dtype=jnp.float32) / dim)
            t = jnp.arange(seq_len, dtype=jnp.float32)
            freqs = t[:, None] * inv_freq[None, :]
            emb = jnp.concatenate([freqs, freqs], axis=-1)
            return (jnp.cos(emb)[None, None], jnp.sin(emb)[None, None])
        B, S, D = x.shape
        H = NUM_HEADS
        hd = D // H
        qkv = x @ W_qkv + b_qkv
        qkv = qkv.reshape(B, S, 3, H, hd).transpose(2, 0, 3, 1, 4)
        q, k, v = (qkv[0], qkv[1], qkv[2])
        cos, sin = rope_cos_sin(S, hd)
        q = q * cos + rotate_every_two(q) * sin
        k = k * cos + rotate_every_two(k) * sin
        scores = jnp.einsum('bhqd,bhkd->bhqk', q, k) / np.float32(np.sqrt(hd))
        probs = jax.nn.softmax(scores, axis=-1)
        ctx = jnp.einsum('bhqk,bhkd->bhqd', probs, v)
        ctx = ctx.transpose(0, 2, 1, 3).reshape(B, S, D)
        return ctx @ W_out + b_out

    def _L0_ffn_ref(x, gate_w, w13, w2, norm_w):
        import jax, jax.numpy as jnp
        import numpy as np
        import math
        B, S, D = (4, 1024, 192)
        E = 8
        TOP_K = 2
        H = 512
        CAP_F = 1.25
        EPS = 1e-06
        ALPHA = 1.0
        Bx, Sx, Dx = x.shape
        N = Bx * Sx
        cap = int(math.ceil(CAP_F * TOP_K * N / E))
        xf = x.reshape(N, Dx)
        logits = xf.astype(jnp.float32) @ gate_w.T
        probs = jax.nn.softmax(logits, axis=-1)
        top_p, top_i = jax.lax.top_k(probs, TOP_K)
        w = top_p / jnp.sum(top_p, axis=-1, keepdims=True)
        flat_e = top_i.reshape(-1)
        onehot = jax.nn.one_hot(flat_e, E, dtype=jnp.int32)
        pos = jnp.take_along_axis(jnp.cumsum(onehot, axis=0) - 1, flat_e[:, None], axis=1)[:, 0]
        keep = pos < cap
        didx = flat_e * cap + jnp.minimum(pos, cap - 1)
        safe = jnp.where(keep, didx, E * cap)
        x_rep = jnp.repeat(xf, TOP_K, axis=0)
        buf = jnp.zeros((E * cap + 1, Dx), x.dtype).at[safe].set(x_rep)
        buf = buf[:-1].reshape(E, cap, Dx)
        z = 2.0 * buf
        z = z * jax.lax.rsqrt(jnp.mean(z * z, axis=-1, keepdims=True) + EPS)
        z = z * norm_w[:, None, :]
        gu = jnp.einsum('ecd,ehd->ech', z, w13)
        g, u = jnp.split(gu, 2, axis=-1)
        y = buf + ALPHA * jnp.einsum('ech,edh->ecd', jax.nn.silu(g) * u, w2)
        y_tok = y.reshape(E * cap, Dx)[didx]
        cw = (w.reshape(-1) * keep.astype(w.dtype)).astype(x.dtype)
        out = (cw[:, None] * y_tok).reshape(N, TOP_K, Dx).sum(axis=1)
        return out.reshape(Bx, Sx, Dx)

    def _L1_attn_ref(embeddings, norm_w, norm_b, in_proj_w, conv_w, conv_b, x_proj_w, dt_proj_w, dt_proj_b, A_log, D_skip, out_proj_w, norm_f_w, norm_f_b):
        import jax, jax.numpy as jnp
        import numpy as np
        D_MODEL = 192
        N_LAYER = 4
        D_INNER = 2 * D_MODEL
        D_STATE = 16
        D_CONV = 4
        DT_RANK = (D_MODEL + 15) // 16
        EPS = 1e-05

        def _ln(x, w, b):
            mu = jnp.mean(x, axis=-1, keepdims=True)
            var = jnp.mean(jnp.square(x - mu), axis=-1, keepdims=True)
            return (x - mu) * jax.lax.rsqrt(var + EPS) * w + b

        def _mixer(u, p):
            B, L, _ = u.shape
            xz = jnp.einsum('bld,ed->ble', u, p['in_proj_w'])
            x, z = jnp.split(xz, 2, axis=-1)
            xp = jnp.pad(x, ((0, 0), (D_CONV - 1, 0), (0, 0)))
            x = sum((p['conv_w'][:, k] * xp[:, k:k + L, :] for k in range(D_CONV))) + p['conv_b']
            x = jax.nn.silu(x)
            x_dbl = jnp.einsum('bld,ed->ble', x, p['x_proj_w'])
            dt, Bm, Cm = jnp.split(x_dbl, [DT_RANK, DT_RANK + D_STATE], axis=-1)
            dt = jax.nn.softplus(jnp.einsum('blr,dr->bld', dt, p['dt_proj_w']) + p['dt_proj_b'])
            A = -jnp.exp(p['A_log'])

            def step(h, xs):
                dt_t, B_t, C_t, x_t = xs
                dA = jnp.exp(dt_t[:, :, None] * A)
                h = dA * h + (dt_t * x_t)[:, :, None] * B_t[:, None, :]
                y = jnp.einsum('bds,bs->bd', h, C_t)
                return (h, y)
            h0 = jnp.zeros((B, D_INNER, D_STATE), x.dtype)
            xs = (dt.transpose(1, 0, 2), Bm.transpose(1, 0, 2), Cm.transpose(1, 0, 2), x.transpose(1, 0, 2))
            _, ys = jax.lax.scan(step, h0, xs)
            y = ys.transpose(1, 0, 2) + x * p['D_skip']
            y = y * jax.nn.silu(z)
            return jnp.einsum('bld,ed->ble', y, p['out_proj_w'])
        params = dict(norm_w=norm_w, norm_b=norm_b, in_proj_w=in_proj_w, conv_w=conv_w, conv_b=conv_b, x_proj_w=x_proj_w, dt_proj_w=dt_proj_w, dt_proj_b=dt_proj_b, A_log=A_log, D_skip=D_skip, out_proj_w=out_proj_w)

        def layer_step(carry, p):
            hidden, residual = carry
            residual = hidden + residual
            h = _ln(residual, p['norm_w'], p['norm_b'])
            h = _mixer(h, p)
            return ((h, residual), None)
        carry = (embeddings, jnp.zeros_like(embeddings))
        (hidden, residual), _ = jax.lax.scan(layer_step, carry, params)
        residual = hidden + residual
        return _ln(residual, norm_f_w, norm_f_b)

    def _L1_ffn_ref(x, Wg, bg, W1, b1, W2, b2):
        import jax, jax.numpy as jnp
        import numpy as np
        B, T, D, H, E = (4, 512, 192, 768, 8)
        b, t, d = x.shape
        xf = x.reshape(-1, d)
        n = xf.shape[0]
        logits = xf @ Wg.T + bg
        probs = jax.nn.softmax(logits, axis=-1)
        top2_vals, top2_idx = jax.lax.top_k(probs, 2)
        cw = jnp.zeros((n, Wg.shape[0]), dtype=x.dtype)
        cw = cw.at[jnp.arange(n)[:, None], top2_idx].set(top2_vals)
        h = jax.nn.gelu(jnp.einsum('nd,edh->neh', xf, W1) + b1[None], approximate=False)
        y = jnp.einsum('neh,ehd->ned', h, W2) + b2[None]
        out = jnp.einsum('ne,ned->nd', cw, y)
        return out.reshape(b, t, d)
    h = _L0_tok_ref(x, L0_tok_W, L0_tok_b)
    h = h + _L0_attn_ref(_layernorm(h, axis=-1), L0_attn_W_qkv, L0_attn_b_qkv, L0_attn_W_out, L0_attn_b_out)
    h = h + _L0_ffn_ref(_layernorm(h, axis=-1), L0_ffn_gate_w, L0_ffn_w13, L0_ffn_w2, L0_ffn_norm_w)
    h = h + _L1_attn_ref(_layernorm(h, axis=-1), L1_attn_norm_w, L1_attn_norm_b, L1_attn_in_proj_w, L1_attn_conv_w, L1_attn_conv_b, L1_attn_x_proj_w, L1_attn_dt_proj_w, L1_attn_dt_proj_b, L1_attn_A_log, L1_attn_D_skip, L1_attn_out_proj_w, L1_attn_norm_f_w, L1_attn_norm_f_b)
    h = h + _L1_ffn_ref(_layernorm(h, axis=-1), L1_ffn_Wg, L1_ffn_bg, L1_ffn_W1, L1_ffn_b1, L1_ffn_W2, L1_ffn_b2)
    return h

_drawn_inputs = setup_inputs


def setup_inputs(seed=0):
    import zlib

    import numpy as np

    out = dict(_drawn_inputs(seed))
    spreads = {'L0_ffn_norm_w': (1.0, 0.6),
     'L1_attn_norm_w': (1.0, 0.6),
     'L1_attn_norm_b': (0.0, 0.8),
     'L1_attn_conv_b': (0.0, 0.8),
     'L1_attn_dt_proj_b': (-4.600165843963623, 0.6),
     'L1_attn_D_skip': (1.0, 0.6),
     'L1_attn_norm_f_w': (1.0, 0.6),
     'L1_attn_norm_f_b': (0.0, 0.626)}
    factors = {'L0_attn_b_qkv': 2.997,
     'L0_attn_b_out': 3.455,
     'L0_ffn_gate_w': 6.391,
     'L0_ffn_w13': 5.772,
     'L0_ffn_w2': 5.835,
     'L1_attn_in_proj_w': 8.0,
     'L1_attn_conv_w': 8.0,
     'L1_attn_x_proj_w': 8.0,
     'L1_attn_dt_proj_w': 8.0,
     'L1_attn_A_log': 8.0,
     'L1_attn_out_proj_w': 8.0,
     'L1_ffn_bg': 64.0,
     'L1_ffn_b1': 20.724,
     'L1_ffn_b2': 27.219}
    for name, (base, spread) in spreads.items():
        noise = np.random.default_rng([zlib.crc32(name.encode()), seed]).standard_normal(out[name].shape)
        drawn = base * np.exp(spread * noise) if base else spread * noise
        out[name] = jnp.asarray(drawn.astype(out[name].dtype))
    for name, factor in factors.items():
        out[name] = (out[name] * factor).astype(out[name].dtype)
    return out
```

```python
from contextlib import ExitStack

import numpy as np
import concourse.bass as bass
from concourse import mybir

ALU = mybir.AluOpType
ACT = mybir.ActivationFunctionType
AX = mybir.AxisListType
F32 = mybir.dt.float32
BF16 = mybir.dt.bfloat16
U32 = mybir.dt.uint32

SEQS, CHANNELS, SAMPLES, PATCH = 64, 90, 375, 16
T = SAMPLES // PATCH
N = SEQS * T
D = 192
DH = D // 2
CB = 16
CT = CB * T
NC = N // CT
GB = 4
GT = GB * T
NG = N // GT
GC = CT // GT
HEADS, HD = 12, 16
QT = 3
E = 8
H0 = 512
H1 = 768
CAP = -(-5 * 2 * N // (4 * E))
LAYERS, DI, DS, DCONV, DTR = 4, 384, 16, 4, 12
DT3 = DI // 128
TAPS = DCONV - 1
MASKED = -1e30
LN_EPS, RMS_EPS = 1e-5, 1e-6


class Semaphores:

    def __init__(self, nc, prefix=""):
        self.nc, self.prefix, self.taken = nc, prefix, []

    def __enter__(self):
        return self

    def __call__(self, name):
        self.taken.append(self.nc.alloc_semaphore(self.prefix + name))
        return self.taken[-1]

    def __exit__(self, *error):
        if error[0] is None:
            self.nc.clear_and_free_semaphores(self.taken)
            self.nc.all_engine_barrier()


def start_at_one(eng, *semaphores):
    for semaphore in semaphores:
        eng.sem_inc(semaphore, 1)


class Norm:

    def __init__(self, nc, sb, sem, name, consts, mean_bank, var_bank, rep_bank, eps, gain=1.0):
        self.nc, self.consts, self.eps, self.gain = nc, consts, eps, gain
        self.mean_bank, self.var_bank, self.rep_bank = mean_bank, var_bank, rep_bank
        self.ve = sb(name + "_var_eps", [GT, GC])
        self.std = sb(name + "_std", [GT, GC])
        self.inv = sb(name + "_inv", [GT, GC])
        if gain != 1.0:
            self.inv_gain = sb(name + "_inv_gain", [GT, GC])
        else:
            self.inv_gain = self.inv
        self.meaned = sem(name + "_meaned")
        self.centred = sem(name + "_centred")
        self.squared = sem(name + "_squared")
        self.summed = sem(name + "_summed")
        self.eps_added = sem(name + "_eps_added")
        self.rooted = sem(name + "_rooted")
        self.inverted = sem(name + "_inverted")
        self.gained = sem(name + "_gained")
        self.spread = sem(name + "_spread")
        self.scaled = sem(name + "_scaled")

    def pe_mean(self, pe, src):
        for k in range(2):
            mm = pe.matmul(self.mean_bank[0:DH, 0:CT], self.consts["mean"][:, 0:DH], src[:, k], start=(k == 0), stop=(k == 1))
        mm.then_inc(self.meaned, 1)

    def pe_square(self, pe, n, sq):
        pe.wait_ge(self.squared, n + 1)
        for g in range(GC):
            for k in range(2):
                mm = pe.matmul(self.var_bank[0:GT, g:g + 1], sq[:, k, g * GT:(g + 1) * GT], self.consts["mean"][:, 0:1],
                               start=(k == 0), stop=(k == 1))
        mm.then_inc(self.summed, 1)

    def pe_spread(self, pe, n):
        pe.wait_ge(self.inverted if self.gain == 1.0 else self.gained, n + 1)
        for g in range(GC):
            mm = pe.matmul(self.rep_bank[0:DH, g * GT:(g + 1) * GT], self.inv_gain[:, g:g + 1].broadcast_to([GT, DH]),
                           self.consts["ident"][0:GT, 0:GT], start=True, stop=True)
        mm.then_inc(self.spread, 1)

    def dve_centre(self, dve, n, xc, src):
        dve.wait_ge(self.meaned, n + 1)
        dve.tensor_tensor(xc, src, self.mean_bank[0:DH, 0:CT].unsqueeze(1).broadcast_to([DH, 2, CT]),
                          ALU.subtract).then_inc(self.centred, 1)

    def act_square(self, act, n, sq, xc):
        act.wait_ge(self.centred, n + 1)
        act.activation(sq, xc, ACT.Square).then_inc(self.squared, 1)

    def dve_eps(self, dve, n):
        dve.wait_ge(self.summed, n + 1)
        dve.tensor_scalar(self.ve[:], self.var_bank[0:GT, 0:GC], self.gain * self.gain, self.eps,
                          ALU.mult, ALU.add).then_inc(self.eps_added, 1)

    def act_root(self, act, n):
        act.wait_ge(self.eps_added, n + 1)
        act.activation(self.std[:], self.ve[:], ACT.Sqrt).then_inc(self.rooted, 1)

    def dve_invert(self, dve, n):
        dve.wait_ge(self.rooted, n + 1)
        dve.reciprocal(self.inv[:], self.std[:]).then_inc(self.inverted, 1)
        if self.gain != 1.0:
            dve.wait_ge(self.inverted, n + 1)
            dve.tensor_scalar(self.inv_gain[:], self.inv[:], self.gain, None, ALU.mult).then_inc(self.gained, 1)

    def dve_scale(self, dve, n, dst, xc):
        dve.wait_ge(self.spread, n + 1)
        dve.tensor_tensor(dst, xc, self.rep_bank[0:DH, 0:CT].unsqueeze(1).broadcast_to([DH, 2, CT]),
                          ALU.mult).then_inc(self.scaled, 1)


def chunk(tile, c):
    return tile[:, :, bass.ds(c * CT, CT)]


def whole_norm(norm, src, xc, sq, dst, centred=True, n0=0, first=None):

    def on_pe(pe):
        for c in range(NC):
            if centred:
                if first is not None:
                    first(pe, c)
                if c >= 1:
                    pe.wait_ge(norm.centred, n0 + c)
                norm.pe_mean(pe, chunk(src, c))
            norm.pe_square(pe, n0 + c, chunk(sq, c))
            norm.pe_spread(pe, n0 + c)

    def on_dve(dve):
        for c in range(NC):
            if centred:
                norm.dve_centre(dve, n0 + c, chunk(xc, c), chunk(src, c))
            norm.dve_eps(dve, n0 + c)
            norm.dve_invert(dve, n0 + c)
            if centred:
                dve.wait_ge(norm.centred, n0 + c + 1)
            norm.dve_scale(dve, n0 + c, chunk(dst, c), chunk(xc, c))

    def on_act(act):
        for c in range(NC):
            if centred:
                norm.act_square(act, n0 + c, chunk(sq, c), chunk(xc, c))
            else:
                act.activation(chunk(sq, c), chunk(xc, c), ACT.Square).then_inc(norm.squared, 1)
            norm.act_root(act, n0 + c)

    return on_pe, on_dve, on_act


def embed(nc, banks, stream, x, tok_w, tok_b):
    with ExitStack() as ctx:
        sb = lambda name, shape, dt=F32: ctx.enter_context(nc.sbuf_tensor(name, shape, dt))
        sem = ctx.enter_context(Semaphores(nc))
        xs = [sb(f"signal{u}", [CHANNELS, CB, SAMPLES]) for u in range(2)]
        w = sb("patch_w", [CHANNELS, PATCH, D])
        b = sb("patch_b", [DH, 2])
        w_landed = sem("patch_w_landed")
        x_landed = [sem(f"signal{u}_landed") for u in range(2)]
        summed = [sem(f"patch_half{k}_summed") for k in range(2)]
        stored = [sem(f"patch_half{k}_stored") for k in range(2)]
        block = ctx.enter_context(nc.Block())

        @block.sync
        def _(sp):
            sp.dma_start(w[:], tok_w).then_inc(w_landed, 16)
            sp.dma_start(b[:], tok_b).then_inc(w_landed, 16)
            with sp.Fori(0, NC // 2) as i:
                for u in range(2):
                    if u == 0:
                        sp.wait_ge(summed[1], 2 * i + 1)
                    sp.dma_start(xs[u][:], x[bass.ds((2 * i + u) * CB, CB)].rearrange("b c t -> c b t")).then_inc(x_landed[u], 16)

        @block.tensor
        def _(pe):
            start_at_one(pe, *summed)
            pe.wait_ge(w_landed, 32)
            with pe.Fori(0, NC // 2) as i:
                for u in range(2):
                    pe.wait_ge(x_landed[u], 16 * i + 16)
                    for k in range(2):
                        pe.wait_ge(stored[k], 2 * i + u + 1)
                        for p in range(PATCH):
                            mm = pe.matmul(banks[k][0:DH, 0:CT], w[:, p, k * DH:(k + 1) * DH],
                                           xs[u][:, :, p:p + PATCH * (T - 1) + 1:PATCH], start=(p == 0), stop=(p == PATCH - 1))
                        mm.then_inc(summed[k], 1)

        @block.scalar
        def _(act):
            start_at_one(act, *stored)
            act.wait_ge(w_landed, 32)
            with act.Fori(0, NC) as c:
                for k in range(2):
                    act.wait_ge(summed[k], c + 2)
                    act.activation(stream[:, k, bass.ds(c * CT, CT)], banks[k][0:DH, 0:CT], ACT.Identity,
                                   bias=b[:, k:k + 1]).then_inc(stored[k], 1)


def attention(nc, banks, stream, consts, qk_w, qk_b, v_w, v_b, out_w, out_b, rope):
    with ExitStack() as ctx:
        sb = lambda name, shape, dt=F32: ctx.enter_context(nc.sbuf_tensor(name, shape, dt))
        sem = ctx.enter_context(Semaphores(nc))
        wqk = sb("wqk", [DH, 2, 2 * QT, 128])
        bqk = sb("bqk", [128, 2 * QT])
        wv = sb("wv", [DH, 2, D])
        bv = sb("bv", [GT, D])
        wo = sb("wo", [DH, 2, D])
        bo = sb("bo", [DH, 2])
        cos_sin = sb("cos_sin", [128, 2, CT])
        xc = sb("at_xc", [DH, 2, N])
        sq = sb("at_sq", [DH, 2, N])
        xn = sb("at_xn", [DH, 2, N])
        xl = sb("at_chunk", [DH, 2, CT])
        biased_t = sb("qk_biased", [128, 2, CT])
        t1 = sb("rope_cos_part", [128, 2, CT])
        t2 = sb("rope_sin_part", [128, 2, CT])
        qm = sb("q_one_head", [128, HEADS, CT])
        kt = sb("k_heads", [128, QT, CT])
        va = sb("v_and_one", [GT, GC, HEADS, HD + 1])
        sm = sb("scores", [GT, 2, 4, GT])
        sx = sb("scores_less_max", [GT, 2, 4, GT])
        ex = sb("exps", [GT, 2, 4, GT])
        pt = sb("exps_turned", [GT, 2, 4, GT])
        mx = sb("score_max", [GT, 2, 4])
        rec = sb("inverse_sums", [GT, HEADS])
        cn = sb("context", [GT, HEADS, HD])
        cx = sb("context_turned", [DH, 2, CT])
        norm = Norm(nc, sb, sem, "at", consts, banks[0], banks[1], banks[2], LN_EPS)
        on_pe, on_dve, on_act = whole_norm(norm, stream, xc, sq, xn)
        landed = sem("at_weights_landed")
        zeroed = sem("at_zeroed")
        copied = sem("chunk_copied")
        projected = sem("qk_projected")
        biased = sem("qk_biased_done")
        turned = sem("qk_rotated")
        cos_done = sem("cos_done")
        sin_done = sem("sin_done")
        roped = sem("qk_roped")
        v_summed = sem("v_summed")
        v_stored = sem("v_stored")
        scored = sem("scored")
        masked = sem("scores_masked")
        maxed = sem("scores_maxed")
        lessened = sem("scores_lessened")
        exped = sem("scores_exped")
        exps_turned = sem("exps_turned_done")
        exps_stored = sem("exps_stored")
        mixed = sem("values_mixed")
        inverted = sem("sums_inverted")
        normed = sem("context_normed")
        ctx_turned = sem("context_turned_done")
        ctx_stored = sem("context_stored")
        out_summed = sem("out_summed")
        added = sem("attention_added")
        block = ctx.enter_context(nc.Block())
        U = QT * GC
        J = 2 * QT

        @block.sync
        def _(sp):
            for dst, src in ((wqk, qk_w), (bqk, qk_b), (wv, v_w), (bv, v_b), (wo, out_w), (bo, out_b), (cos_sin, rope)):
                sp.dma_start(dst[:], src).then_inc(landed, 16)

        @block.gpsimd
        def _(pool):
            pool.memset(qm[:], 0.0).then_inc(zeroed, 1)
            pool.memset(va[:], 1.0).then_inc(zeroed, 1)
            pool.wait_ge(landed, 16 * 7)
            with pool.Fori(0, NC) as c:
                for j in range(J):
                    pool.wait_ge(biased, J * c + j + 1)
                    if j >= 2:
                        pool.wait_ge(roped, J * c + j)
                    else:
                        pool.wait_ge(roped, J * c + 1)
                    pool.tensor_tensor(t1[:, j % 2], biased_t[:, j % 2], cos_sin[:, 0], ALU.mult).then_inc(cos_done, 1)
                for u in range(U):
                    b = u % 2
                    pool.wait_ge(maxed, U * c + u + 1)
                    pool.wait_ge(masked, U * c + u + 1)
                    if u >= 2:
                        pool.wait_ge(exped, U * c + u - 1)
                    pool.tensor_tensor(sx[:, b], sm[:, b], mx[:, b].unsqueeze(2).broadcast_to([GT, 4, GT]),
                                       ALU.subtract).then_inc(lessened, 1)

        @block.tensor
        def _(pe):
            start_at_one(pe, v_summed, mixed)
            on_pe(pe)
            pe.wait_ge(landed, 16 * 7)
            with pe.Fori(0, NC) as c:
                pe.wait_ge(copied, c + 1)
                pe.wait_ge(added, 2 * c + 1)

                def rotate(j):
                    pe.wait_ge(biased, J * c + j + 1)
                    if j >= 2:
                        pe.wait_ge(sin_done, J * c + j - 1)
                    pe.matmul(banks[2 + j % 2][:, 0:CT], consts["rotate"][:], biased_t[:, j % 2], start=True,
                              stop=True).then_inc(turned, 1)

                for j in range(J):
                    if j >= 2:
                        pe.wait_ge(biased, J * c + j - 1)
                    for k in range(2):
                        mm = pe.matmul(banks[j % 2][:, 0:CT], wqk[:, k, j], xl[:, k], start=(k == 0), stop=(k == 1))
                    mm.then_inc(projected, 1)
                    if j >= 1:
                        rotate(j - 1)
                rotate(J - 1)
                for g in range(GC):
                    for k in range(2):
                        mm = pe.matmul(banks[4 + g][0:GT, 0:D], xl[:, k, g * GT:(g + 1) * GT], wv[:, k],
                                       start=(k == 0), stop=(k == 1))
                    mm.then_inc(v_summed, 1)
                pe.wait_ge(roped, J * c + J + 1)
                pe.wait_ge(v_stored, GC * c + GC)

                def score(u):
                    g, j = divmod(u, QT)
                    if u >= 2:
                        pe.wait_ge(masked, U * c + u - 1)
                    for i in range(4):
                        mm = pe.matmul(banks[u % 2][0:GT, i * GT:(i + 1) * GT], qm[:, 4 * j + i, g * GT:(g + 1) * GT],
                                       kt[:, j, g * GT:(g + 1) * GT], start=True, stop=True)
                    mm.then_inc(scored, 1)

                def turn(u):
                    pe.wait_ge(exped, U * c + u + 1)
                    if u >= 2:
                        pe.wait_ge(exps_stored, U * c + u - 1)
                    for i in range(4):
                        mm = pe.transpose(banks[2 + u % 2][0:GT, i * GT:(i + 1) * GT], ex[:, u % 2, i], consts["ident"][0:GT, 0:GT])
                    mm.then_inc(exps_turned, 1)

                def mix(u):
                    g, j = divmod(u, QT)
                    pe.wait_ge(exps_stored, U * c + u + 1)
                    if j == 0 and g >= 1:
                        pe.wait_ge(normed, GC * c + g)
                    for i in range(4):
                        h = 4 * j + i
                        mm = pe.matmul(banks[6][0:GT, h * (HD + 1):(h + 1) * (HD + 1)], pt[:, u % 2, i], va[:, g, h],
                                       start=True, stop=True)
                    mm.then_inc(mixed, 1)

                def turn_context(g):
                    pe.wait_ge(normed, GC * c + g + 1)
                    if g >= 1:
                        pe.wait_ge(ctx_stored, GC * c + g)
                    for k in range(2):
                        mm = pe.transpose(banks[7][0:DH, k * GT:(k + 1) * GT],
                                          cn[:].rearrange("p h d -> p (h d)")[:, k * DH:(k + 1) * DH], consts["ident"][0:GT, 0:GT])
                    mm.then_inc(ctx_turned, 1)

                for u in range(U + 4):
                    if u < U:
                        score(u)
                    if 1 <= u <= U:
                        turn(u - 1)
                    if 2 <= u < U + 2:
                        mix(u - 2)
                    if u >= 5 and (u - 5) % QT == 0:
                        turn_context((u - 5) // QT)
                pe.wait_ge(ctx_stored, GC * c + GC)
                for m in range(2):
                    for k in range(2):
                        mm = pe.matmul(banks[4 + m][0:DH, 0:CT], wo[:, k, m * DH:(m + 1) * DH], cx[:, k], start=(k == 0), stop=(k == 1))
                    mm.then_inc(out_summed, 1)

        def store_context(act, c, g):
            act.wait_ge(ctx_turned, GC * c + g + 1)
            act.activation(cx[:, :, g * GT:(g + 1) * GT], banks[7][0:DH, 0:2 * GT].rearrange("p (k t) -> p k t", k=2),
                           ACT.Copy).then_inc(ctx_stored, 1)

        @block.scalar
        def _(act):
            on_act(act)
            act.wait_ge(landed, 16 * 7)
            act.wait_ge(norm.scaled, NC)
            with act.Fori(0, NC) as c:
                act.wait_ge(v_summed, GC * c + 1)
                act.activation(xl[:], chunk(xn, c), ACT.Copy).then_inc(copied, 1)
                for j in range(J):
                    act.wait_ge(projected, J * c + j + 1)
                    if j >= 2:
                        act.wait_ge(turned, J * c + j - 1)
                        act.wait_ge(cos_done, J * c + j - 1)
                    act.activation(biased_t[:, j % 2], banks[j % 2][:, 0:CT], ACT.Identity, bias=bqk[:, j:j + 1]).then_inc(biased, 1)
                for u in range(U + 4):
                    if u < U:
                        act.wait_ge(lessened, U * c + u + 1)
                        if u >= 2:
                            act.wait_ge(exps_turned, U * c + u - 1)
                        act.activation(ex[:, u % 2], sx[:, u % 2], ACT.Exp).then_inc(exped, 1)
                    if 1 <= u <= U:
                        v = u - 1
                        act.wait_ge(exps_turned, U * c + v + 1)
                        if v >= 2:
                            act.wait_ge(mixed, U * c + v)
                        act.activation(pt[:, v % 2].rearrange("p a b -> p (a b)"), banks[2 + v % 2][0:GT, 0:4 * GT], ACT.Copy).then_inc(exps_stored, 1)
                    if u >= 6 and (u - 6) % QT == 0:
                        store_context(act, c, (u - 6) // QT)

        @block.vector
        def _(dve):
            start_at_one(dve, roped, added)
            on_dve(dve)
            dve.wait_ge(landed, 16 * 7)
            dve.wait_ge(zeroed, 2)
            with dve.Fori(0, NC) as c:
                dve.wait_ge(mixed, U * c + 1)
                for j in range(J):
                    b = j % 2
                    dve.wait_ge(turned, J * c + j + 1)
                    dve.tensor_tensor(t2[:, b], banks[2 + b][:, 0:CT], cos_sin[:, 1], ALU.mult).then_inc(sin_done, 1)
                    dve.wait_ge(sin_done, J * c + j + 1)
                    dve.wait_ge(cos_done, J * c + j + 1)
                    if j < QT:
                        for i in range(4):
                            q = slice(32 * i, 32 * i + 32)
                            last = dve.tensor_tensor(qm[q, 4 * j + i], t1[q, b], t2[q, b], ALU.add)
                    else:
                        last = dve.tensor_tensor(kt[:, j - QT], t1[:, b], t2[:, b], ALU.add)
                    last.then_inc(roped, 1)
                for g in range(GC):
                    dve.wait_ge(v_summed, GC * c + g + 2)
                    dve.tensor_tensor(va[:, g, :, 0:HD], banks[4 + g][0:GT, 0:D].rearrange("p (h d) -> p h d", h=HEADS),
                                      bv[:].rearrange("p (h d) -> p h d", h=HEADS), ALU.add).then_inc(v_stored, 1)

                def norm_context(g):
                    dve.wait_ge(mixed, U * c + QT * (g + 1) + 1)
                    heads = banks[6][0:GT, 0:HEADS * (HD + 1)].rearrange("p (h d) -> p h d", h=HEADS)
                    dve.reciprocal(rec[:].unsqueeze(2), heads[:, :, HD:HD + 1]).then_inc(inverted, 1)
                    dve.wait_ge(inverted, GC * c + g + 1)
                    if g >= 1:
                        dve.wait_ge(ctx_turned, GC * c + g)
                    dve.tensor_tensor(cn[:], heads[:, :, 0:HD], rec[:].unsqueeze(2).broadcast_to([GT, HEADS, HD]),
                                      ALU.mult).then_inc(normed, 1)

                for u in range(U):
                    b = u % 2
                    dve.wait_ge(scored, U * c + u + 1)
                    if u >= 2:
                        dve.wait_ge(lessened, U * c + u - 1)
                    dve.scalar_tensor_tensor(sm[:, b], banks[b][0:GT, 0:4 * GT].rearrange("p (i t) -> p i t", i=4), HD ** -0.5,
                                             consts["mask"][:].unsqueeze(1).broadcast_to([GT, 4, GT]),
                                             ALU.mult, ALU.add).then_inc(masked, 1)
                    dve.wait_ge(masked, U * c + u + 1)
                    dve.tensor_reduce(mx[:, b], sm[:, b], AX.X, ALU.max).then_inc(maxed, 1)
                    if u >= 5 and (u - 5) % QT == 0:
                        norm_context((u - 5) // QT)
                for g in range((U - 1 - 5) // QT + 1, GC):
                    norm_context(g)
                for m in range(2):
                    dve.wait_ge(out_summed, 2 * c + m + 1)
                    half = stream[:, m, bass.ds(c * CT, CT)]
                    dve.scalar_tensor_tensor(half, banks[4 + m][0:DH, 0:CT], bo[:, m:m + 1], half, ALU.add, ALU.add).then_inc(added, 1)


def route(nc, tag, banks, consts, xn, gate_w, gate_b, weights_rep, weights_t, capacity):
    with ExitStack() as ctx:
        sb = lambda name, shape, dt=F32: ctx.enter_context(nc.sbuf_tensor(f"{tag}_{name}", shape, dt))
        sem = ctx.enter_context(Semaphores(nc, tag + "_"))
        gw = sb("gate_w", [DH, 2, E])
        gb = sb("gate_b", [GT, E])
        lg = sb("logits", [GT, NG, E])
        top = sb("top_values", [GT, NG, 8])
        ti = sb("top_indices", [GT, NG, 8], U32)
        tf = sb("top_indices_f", [GT, NG, 2])
        one = sb("is_first", [GT, NG, E])
        two = sb("is_second", [GT, NG, E])
        chosen = sb("chosen", [GT, NG, E])
        less = sb("logits_less_max", [GT, NG, E])
        ex = sb("logit_exps", [GT, NG, E])
        sel = sb("chosen_exps", [GT, NG, E])
        total = sb("exp_total", [GT, NG])
        inv = sb("exp_total_inverse", [GT, NG])
        pre = [sb(f"group_prefix{u}", [GT, NG, E]) for u in range(2)]
        place = sb("place_in_expert", [GT, NG, E])
        cw = sb("weights_by_token", [GT, NG, E])
        landed = sem("gate_landed")
        logits_summed = sem("logits_summed")
        step = sem("routing_step")
        chosen_ready = sem("chosen_ready")
        counted = sem("chosen_counted")
        less_ready = sem("logits_less_max_ready")
        exped = sem("logits_exped")
        ready = sem("weights_by_token_ready")
        turned = sem("weights_turned")
        turned_stored = sem("weights_turned_stored")
        repeated = sem("weights_repeated")
        stored = sem("weights_rep_stored")
        block = ctx.enter_context(nc.Block())
        last_of = lambda tile, k: tile[:, :, k:k + 1].broadcast_to([GT, NG, E])

        @block.sync
        def _(sp):
            sp.dma_start(gw[:], gate_w).then_inc(landed, 16)
            if gate_b is not None:
                sp.dma_start(gb[:], gate_b).then_inc(landed, 16)

        all_landed = 16 if gate_b is None else 32

        @block.tensor
        def _(pe):
            pe.wait_ge(landed, all_landed)
            for g in range(NG):
                for k in range(2):
                    mm = pe.matmul(banks[0][0:GT, g * E:(g + 1) * E], xn[:, k, g * GT:(g + 1) * GT], gw[:, k], start=(k == 0), stop=(k == 1))
            mm.then_inc(logits_summed, 1)
            if capacity is not None:
                pe.wait_ge(chosen_ready, 1)
                flat = chosen[:].rearrange("p g e -> p (g e)")
                pe.matmul(banks[1][0:GT, 0:NG * E], consts["before"][:], flat, start=True, stop=True)
                pe.matmul(banks[2][0:GT, 0:NG * E], consts["ones"][0:GT, 0:GT], flat, start=True, stop=True).then_inc(counted, 1)
            pe.wait_ge(ready, 1)
            for c in range(NC):
                for i in range(GC):
                    mm = pe.transpose(banks[4 + c][0:E, i * GT:(i + 1) * GT], cw[:, c * GC + i], consts["ident"][0:GT, 0:GT])
                mm.then_inc(turned, 1)
            for c in range(NC):
                pe.wait_ge(turned_stored, c + 1)
                for e in range(E):
                    n = c * E + e
                    if n >= 2:
                        pe.wait_ge(stored, n - 1)
                    pe.matmul(banks[n % 2][0:DH, 0:CT], consts["pick"][:, e], weights_t[:, c * CT:(c + 1) * CT],
                              start=True, stop=True).then_inc(repeated, 1)

        @block.scalar
        def _(act):
            act.wait_ge(less_ready, 1)
            act.activation(ex[:], less[:], ACT.Exp).then_inc(exped, 1)
            for c in range(NC):
                for e in range(E):
                    n = c * E + e
                    act.wait_ge(repeated, n + 1)
                    act.activation(weights_rep[:, e, c * CT:(c + 1) * CT], banks[n % 2][0:DH, 0:CT], ACT.Copy).then_inc(stored, 1)

        @block.vector
        def _(dve):
            steps = [0]

            def then(instruction):
                steps[0] += 1
                instruction.then_inc(step, 1)
                dve.wait_ge(step, steps[0])

            dve.wait_ge(landed, all_landed)
            dve.wait_ge(logits_summed, 1)
            summed = banks[0][0:GT, 0:NG * E].rearrange("p (g e) -> p g e", e=E)
            if gate_b is None:
                then(dve.tensor_copy(lg[:], summed))
            else:
                then(dve.tensor_tensor(lg[:], summed, gb[:].unsqueeze(1).broadcast_to([GT, NG, E]), ALU.add))
            for g in range(NG):
                last = dve.max(top[:, g], lg[:, g])
            then(last)
            dve.tensor_tensor(less[:], lg[:], last_of(top, 0), ALU.subtract).then_inc(less_ready, 1)
            for g in range(NG):
                last = dve.max_index(ti[:, g], top[:, g], lg[:, g])
            then(last)
            then(dve.tensor_copy(tf[:], ti[:, :, 0:2]))
            names = consts["expert_names"][:].unsqueeze(1).broadcast_to([GT, NG, E])
            dve.tensor_tensor(one[:], names, last_of(tf, 0), ALU.is_equal)
            then(dve.tensor_tensor(two[:], names, last_of(tf, 1), ALU.is_equal))
            dve.tensor_tensor(chosen[:], one[:], two[:], ALU.add).then_inc(chosen_ready, 1)
            dve.wait_ge(chosen_ready, 1)
            dve.wait_ge(exped, 1)
            then(dve.tensor_tensor(sel[:], ex[:], chosen[:], ALU.mult))
            then(dve.tensor_reduce(total[:], (sel if capacity is not None else ex)[:], AX.X, ALU.add))
            then(dve.reciprocal(inv[:], total[:]))
            if capacity is None:
                dve.tensor_tensor(cw[:], sel[:], inv[:].unsqueeze(2).broadcast_to([GT, NG, E]), ALU.mult).then_inc(ready, 1)
            else:
                dve.wait_ge(counted, 1)
                totals = banks[2][0:GT, 0:NG * E].rearrange("p (g e) -> p g e", e=E)
                dve.memset(pre[0][:, 0:1], 0.0)
                then(dve.tensor_copy(pre[0][:, 1:NG], totals[:, 0:NG - 1]))
                shift, u = 1, 0
                while shift < NG:
                    dve.tensor_copy(pre[1 - u][:, 0:shift], pre[u][:, 0:shift])
                    then(dve.tensor_tensor(pre[1 - u][:, shift:NG], pre[u][:, shift:NG], pre[u][:, 0:NG - shift], ALU.add))
                    shift, u = 2 * shift, 1 - u
                within = banks[1][0:GT, 0:NG * E].rearrange("p (g e) -> p g e", e=E)
                then(dve.tensor_tensor(place[:], pre[u][:], within, ALU.add))
                then(dve.scalar_tensor_tensor(sel[:], place[:], float(capacity), sel[:], ALU.is_lt, ALU.mult))
                dve.tensor_tensor(cw[:], sel[:], inv[:].unsqueeze(2).broadcast_to([GT, NG, E]), ALU.mult).then_inc(ready, 1)
            for c in range(NC):
                dve.wait_ge(turned, c + 1)
                dve.tensor_copy(weights_t[:, c * CT:(c + 1) * CT], banks[4 + c][0:E, 0:CT]).then_inc(turned_stored, 1)


def experts(nc, tag, banks, consts, stream, xn, xf, weights_rep, weights_t, w_in, w_out, hidden, b_in=None, b_out=None, norm_w=None):
    gated = norm_w is not None
    tiles = hidden // 128
    with ExitStack() as ctx:
        sb = lambda name, shape, dt=F32: ctx.enter_context(nc.sbuf_tensor(f"{tag}_{name}", shape, dt))
        sem = ctx.enter_context(Semaphores(nc, tag + "_"))
        width = hidden * (2 if gated else 1)
        wi = [sb(f"expert_in{u}", [DH, 2, width]) for u in range(2)]
        wo = [sb(f"expert_out{u}", [128, tiles, D]) for u in range(2)]
        small = [sb(f"expert_small{u}", [DH, 2] if gated else [128, tiles]) for u in range(2)]
        act_out = sb("gate_silu", [128, 2, CT])
        hid = sb("expert_hidden", [128, 2, tiles, CT])
        weighed = sb("expert_weighed", [DH, 2, 2, CT])
        bo = sb("experts_b_out", [E, D])
        b_landed = sem("experts_b_landed")
        landed = [sem(f"expert{u}_landed") for u in range(2)]
        scaled = sem("expert_in_scaled")
        base_summed = sem("base_summed")
        weighed_base = sem("weighed_base")
        base_added = sem("base_added")
        first_summed = sem("hidden_summed")
        silued = sem("gate_silued")
        hid_ready = sem("hidden_ready")
        second_summed = [sem(f"expert{u}_summed") for u in range(2)]
        weighed_ready = sem("expert_weighed_ready")
        added = sem("expert_added")
        block = ctx.enter_context(nc.Block())
        K = NC * tiles

        def hidden_used(eng, i, u, c):
            if c >= 2:
                eng.wait_ge(second_summed[u], NC * i + c)
            elif c == 0:
                eng.wait_ge(second_summed[1 - u], NC * i + NC * u + 1)

        @block.sync
        def _(sp):
            if not gated:
                sp.dma_start(bo[:], b_out).then_inc(b_landed, 16)
            with sp.Fori(0, E // 2) as i:
                for u in range(2):
                    sp.wait_ge(second_summed[u], NC * i + 1)
                    e = 2 * i + u
                    sp.dma_start(wi[u][:], w_in[bass.ds(e, 1)].rearrange("a p k h -> (a p) k h")).then_inc(landed[u], 16)
                    sp.dma_start(small[u][:], (norm_w if gated else b_in)[bass.ds(e, 1)].rearrange("a p k -> (a p) k")).then_inc(landed[u], 16)
                    sp.dma_start(wo[u][:], w_out[bass.ds(e, 1)].rearrange("a p k h -> (a p) k h")).then_inc(landed[u], 16)

        @block.tensor
        def _(pe):
            start_at_one(pe, *second_summed)
            if not gated:
                pe.wait_ge(b_landed, 16)
            for c in range(NC):
                if c >= 1:
                    pe.wait_ge(base_added, c)
                for k in range(1 if gated else 2):
                    lhs = consts["ones"][0:E, 0:DH] if gated else bo[:, k * DH:(k + 1) * DH]
                    mm = pe.matmul(banks[k][0:DH, 0:CT], lhs, weights_t[:, c * CT:(c + 1) * CT], start=True, stop=True)
                mm.then_inc(base_summed, 1)
            pe.wait_ge(base_added, NC)
            with pe.Fori(0, E // 2) as i:
                for u in range(2):
                    e = 2 * i + u
                    if gated:
                        pe.wait_ge(scaled, e + 1)
                    pe.wait_ge(landed[u], 48 * i + 48)

                    def first(c):
                        for h in range(tiles):
                            n = c * tiles + h
                            b = 2 * (n % 2) if gated else n % 4
                            behind = 2 if gated else 4
                            if n >= behind:
                                pe.wait_ge(hid_ready, K * e + n - behind + 2)
                            elif n == 0:
                                pe.wait_ge(hid_ready, K * e + 1)
                            for part in range(2 if gated else 1):
                                o = part * hidden + h * 128
                                for k in range(2):
                                    mm = pe.matmul(banks[b + part][:, 0:CT], wi[u][:, k, o:o + 128], xn[:, k, c * CT:(c + 1) * CT],
                                                   start=(k == 0), stop=(k == 1))
                            mm.then_inc(first_summed, 1)

                    def second(c):
                        pe.wait_ge(hid_ready, K * e + (c + 1) * tiles + 1)
                        if c >= 2:
                            pe.wait_ge(weighed_ready, NC * e + c)
                        elif c == 0:
                            pe.wait_ge(weighed_ready, NC * e + 1)
                        for m in range(2):
                            for h in range(tiles):
                                mm = pe.matmul(banks[4 + 2 * (c % 2) + m][0:DH, 0:CT], wo[u][:, h, m * DH:(m + 1) * DH], hid[:, c % 2, h],
                                               start=(h == 0), stop=(h == tiles - 1))
                        mm.then_inc(second_summed[u], 1)

                    for c in range(NC):
                        first(c)
                        if c >= 1:
                            second(c - 1)
                    second(NC - 1)

        @block.scalar
        def _(act):
            if not gated:
                start_at_one(act, hid_ready)
            with act.Fori(0, E // 2) as i:
                for u in range(2):
                    e = 2 * i + u
                    act.wait_ge(landed[u], 48 * i + 48)
                    if gated:
                        for k in range(2):
                            last = act.activation(wi[u][:, k], wi[u][:, k], ACT.Copy, scale=small[u][:, k:k + 1])
                        last.then_inc(scaled, 1)
                    for c in range(NC):
                        if not gated:
                            hidden_used(act, i, u, c)
                        for h in range(tiles):
                            n = c * tiles + h
                            act.wait_ge(first_summed, K * e + n + 1)
                            if gated:
                                if n >= 2:
                                    act.wait_ge(hid_ready, K * e + n)
                                act.activation(act_out[:, n % 2], banks[2 * (n % 2)][:, 0:CT], ACT.Silu).then_inc(silued, 1)
                            else:
                                act.activation(hid[:, c % 2, h], banks[n % 4][:, 0:CT], ACT.Gelu, bias=small[u][:, h:h + 1]).then_inc(hid_ready, 1)

        @block.vector
        def _(dve):
            start_at_one(dve, weighed_ready)
            if gated:
                start_at_one(dve, hid_ready)
            for c in range(NC):
                dve.wait_ge(base_summed, c + 1)
                part = chunk(stream, c)
                if gated:
                    rep = banks[0][0:DH, 0:CT].unsqueeze(1).broadcast_to([DH, 2, CT])
                    dve.tensor_tensor(weighed[:, c % 2], chunk(xf, c), rep, ALU.mult).then_inc(weighed_base, 1)
                    dve.wait_ge(weighed_base, c + 1)
                    dve.tensor_tensor(part, part, weighed[:, c % 2], ALU.add).then_inc(base_added, 1)
                else:
                    for k in range(2):
                        last = dve.tensor_tensor(stream[:, k, c * CT:(c + 1) * CT], stream[:, k, c * CT:(c + 1) * CT],
                                                 banks[k][0:DH, 0:CT], ALU.add)
                    last.then_inc(base_added, 1)
            with dve.Fori(0, E // 2) as i:
                for u in range(2):
                    e = 2 * i + u

                    def weigh(c):
                        dve.wait_ge(second_summed[u], NC * i + c + 2)
                        if c >= 2:
                            dve.wait_ge(added, NC * e + c)
                        elif c == 0:
                            dve.wait_ge(added, NC * e + 1)
                        for m in range(2):
                            last = dve.tensor_tensor(weighed[:, c % 2, m], banks[4 + 2 * (c % 2) + m][0:DH, 0:CT],
                                                     weights_rep[:, bass.ds(e, 1), c * CT:(c + 1) * CT].rearrange("p a t -> p (a t)"), ALU.mult)
                        last.then_inc(weighed_ready, 1)

                    for c in range(NC):
                        if gated:
                            hidden_used(dve, i, u, c)
                            for h in range(tiles):
                                n = c * tiles + h
                                dve.wait_ge(silued, K * e + n + 1)
                                dve.tensor_tensor(hid[:, c % 2, h], act_out[:, n % 2], banks[2 * (n % 2) + 1][:, 0:CT],
                                                  ALU.mult).then_inc(hid_ready, 1)
                        if c >= 1:
                            weigh(c - 1)
                    weigh(NC - 1)

        @block.gpsimd
        def _(pool):
            start_at_one(pool, added)
            pool.wait_ge(base_added, NC)
            with pool.Fori(0, E) as e:
                for c in range(NC):
                    pool.wait_ge(weighed_ready, NC * e + c + 2)
                    part = chunk(stream, c)
                    pool.tensor_tensor(part, part, weighed[:, c % 2], ALU.add).then_inc(added, 1)


def state_space(nc, banks, consts, resid, params96, params128, dt_w):
    with ExitStack() as ctx:
        sb = lambda name, shape, dt=F32: ctx.enter_context(nc.sbuf_tensor(name, shape, dt))
        sem = ctx.enter_context(Semaphores(nc))
        p96 = sb("layer_p96", [DH, 2 * 2 * DI + 4])
        p128 = sb("layer_p128", [128, params128.shape[2]])
        dtw = sb("layer_dt_w", [64, DI])
        in_w = p96[:, 0:4 * DI].rearrange("p (k e) -> p k e", k=2)
        norm_w, norm_b = p96[:, 4 * DI:4 * DI + 2], p96[:, 4 * DI + 2:4 * DI + 4]
        cut, o = {}, 0
        for name, size in (("conv_w", DT3 * DCONV), ("conv_b", DT3), ("dt_b", DT3), ("skip", DT3), ("a_log", DT3 * DS),
                           ("x_w", DT3 * (2 * DS + DTR)), ("out_w", DT3 * D)):
            cut[name] = p128[:, o:o + size]
            o += size
        conv_w = cut["conv_w"].rearrange("p (d k) -> p d k", d=DT3)
        x_w = cut["x_w"].rearrange("p (d e) -> p d e", d=DT3)
        out_w = cut["out_w"].rearrange("p (d e) -> p d e", d=DT3)
        a_exp = sb("a_exp", [128, DT3 * DS])
        a_neg = sb("a_neg", [128, DT3 * DS])
        xc = sb("ss_xc", [DH, 2, CT])
        sq = sb("ss_sq", [DH, 2, CT])
        xn = sb("ss_xn", [DH, 2, CT])
        un = sb("ss_un", [DH, 2, CT])
        padded = sb("conv_in", [128, DT3, CB, T + DCONV - 1])
        conv = sb("conv_sum", [128, DT3, CT])
        xa = sb("conv_silu", [128, 2, DT3, CT])
        zs = sb("gate_silu_z", [128, 2, DT3, CT])
        dtr = sb("dt_low_rank", [64, CT])
        rest1 = sb("bc_rest1", [2 * DS, CT])
        mid = sb("bc_mid", [2 * DS, CT], BF16)
        rest2 = sb("bc_rest2", [2 * DS, CT])
        bc = sb("bc_parts", [3 * 2 * DS, 2, CT], BF16)
        xb = sb("dt_in", [128, DT3, CT])
        ab = sb("dt_abs", [128, DT3, CT])
        eb = sb("dt_exp", [128, DT3, CT])
        ub = sb("dt_exp_plus_one", [128, DT3, CT])
        lost = sb("dt_rounding", [128, DT3, CT])
        lb = sb("dt_log", [128, DT3, CT])
        dt = sb("dt", [128, 2, DT3, CT])
        dtx = sb("dt_x", [128, 2, DT3, CT])
        da = sb("decay", [128, 2, DT3, CB, T])
        dbx = sb("state_in", [128, 3, DT3 * CT])
        hs = sb("states", [128, 2, DT3 * CT])
        cs = sb("c_repeated", [128, 2, CT])
        prod = sb("c_states", [128, 2, DT3 * CT])
        yt = sb("y_skip", [128, DT3, CT])
        yg = sb("y_gated", [128, DT3, CT])
        norm = Norm(nc, sb, sem, "ss", consts, banks[6], banks[7], banks[6], LN_EPS)
        params_landed = sem("layer_params_landed")
        a_exped = sem("a_exped")
        a_ready = sem("a_ready")
        zeroed = sem("ss_zeroed")
        affined = sem("norm_affined")
        in_summed = sem("in_summed")
        in_stored = sem("in_stored")
        tap0 = sem("conv_tap0")
        tapped = sem("conv_tapped")
        conv_silued = sem("conv_silued")
        x_summed = sem("x_proj_summed")
        dtr_stored = sem("dt_low_rank_stored")
        bc_step = sem("bc_step")
        bc_mid_stored = sem("bc_mid_stored")
        dt_summed = sem("dt_summed")
        dt_stored = sem("dt_in_stored")
        dt_absed = sem("dt_absed")
        dt_exped = sem("dt_exped")
        dt_one = sem("dt_plus_one")
        dt_lost = sem("dt_rounding_ready")
        dt_logged = sem("dt_logged")
        dt_fixed = sem("dt_log_fixed")
        dt_ready = sem("dt_ready")
        dtx_ready = sem("dtx_ready")
        b_spread = sem("b_spread")
        c_spread = sem("c_spread")
        c_stored = sem("c_stored")
        decayed = sem("decay_ready")
        fed = sem("state_in_ready")
        scanned = sem("scanned")
        produced = sem("c_states_ready")
        reduced = sem("c_states_summed")
        skipped = sem("y_skip_ready")
        gated = sem("y_gated_ready")
        out_summed = sem("mixer_summed")
        added = sem("mixer_added")
        block = ctx.enter_context(nc.Block())

        @block.sync
        def _(sp):
            with sp.Fori(0, LAYERS) as l:
                sp.wait_ge(added, NC * l + 1)
                sp.dma_start(p96[:], params96[bass.ds(l, 1)].rearrange("a p c -> (a p) c")).then_inc(params_landed, 16)
                sp.dma_start(p128[:], params128[bass.ds(l, 1)].rearrange("a p c -> (a p) c")).then_inc(params_landed, 16)
                sp.dma_start(dtw[2 * DS:2 * DS + DTR, :], dt_w[bass.ds(l, 1)].rearrange("a p c -> (a p) c")).then_inc(params_landed, 16)

        @block.tensor
        def _(pe):
            start_at_one(pe, dt_summed, in_summed, out_summed, reduced)
            with pe.Fori(0, LAYERS) as l:
                pe.wait_ge(params_landed, 48 * l + 48)

                def normalise(c, part):
                    n = NC * l + c
                    if part == 0:
                        pe.wait_ge(added, n + 1 if c == 0 else n)
                        pe.wait_ge(dt_stored, DT3 * n + 1)
                        norm.pe_mean(pe, chunk(resid, c))
                    elif part == 1:
                        norm.pe_square(pe, n, sq)
                    else:
                        norm.pe_spread(pe, n)

                def project_in(c, m):
                    n = NC * l + c
                    if m == 0:
                        pe.wait_ge(affined, n + 2)
                    if m >= 2:
                        pe.wait_ge(in_stored, 2 * DT3 * n + m - 1)
                    for k in range(2):
                        mm = pe.matmul(banks[6 + m % 2][:, 0:CT], in_w[:, k, m * 128:(m + 1) * 128], un[:, k], start=(k == 0), stop=(k == 1))
                    mm.then_inc(in_summed, 1)

                def project_x(c):
                    n = NC * l + c
                    pe.wait_ge(in_stored, 2 * DT3 * (n + 1))
                    pe.wait_ge(conv_silued, n + 1)
                    for d in range(DT3):
                        mm = pe.matmul(banks[6][0:2 * DS + DTR, 0:CT], x_w[:, d], xa[:, c % 2, d], start=(d == 0), stop=(d == DT3 - 1))
                    mm.then_inc(x_summed, 1)

                def project_dt(c, d):
                    n = NC * l + c
                    if d == 0:
                        pe.wait_ge(dtr_stored, n + 1)
                    if d == 1:
                        pe.wait_ge(bc_step, 4 * n + 2)
                    if d == 2:
                        pe.wait_ge(dt_stored, DT3 * n + 2)
                    low = slice(2 * DS, 2 * DS + DTR)
                    pe.matmul(banks[7 - d % 2][:, 0:CT], dtw[low, d * 128:(d + 1) * 128], dtr[low, :], start=True,
                              stop=True).then_inc(dt_summed, 1)

                def spread(c, s):
                    n = DS * (NC * l + c)
                    if s >= 2:
                        pe.wait_ge(fed, n + s)
                    elif s == 0:
                        pe.wait_ge(fed, n + 1)
                    pe.matmul(banks[3 + s % 2][:, 0:CT], consts["spread"][:, s], bc[:, c % 2], start=True, stop=True).then_inc(b_spread, 1)
                    pe.wait_ge(c_stored, n + s + 1)
                    pe.matmul(banks[5][:, 0:CT], consts["spread"][:, DS + s], bc[:, c % 2], start=True, stop=True).then_inc(c_spread, 1)

                def reduce(c, s):
                    n = NC * l + c
                    if s == 0:
                        pe.wait_ge(skipped, DT3 * n + 1)
                    pe.wait_ge(produced, DS * n + s + 2)
                    for d in range(DT3):
                        mm = pe.matmul(banks[d][:, 0:CT], consts["ident"][:], prod[:, s % 2, d * CT:(d + 1) * CT],
                                       start=(s == 0), stop=(s == DS - 1))
                    mm.then_inc(reduced, 1)

                def project_out(c):
                    n = NC * l + c
                    pe.wait_ge(gated, n + 2)
                    if c + 1 < NC:
                        pe.wait_ge(dt_stored, DT3 * (n + 2) + 1)
                    else:
                        pe.wait_ge(added, n + 1)
                    for k in range(2):
                        for d in range(DT3):
                            mm = pe.matmul(banks[6 + k][0:DH, 0:CT], out_w[:, d, k * DH:(k + 1) * DH], yg[:, d], start=(d == 0), stop=(d == DT3 - 1))
                    mm.then_inc(out_summed, 1)

                def start(c, s):
                    if s in (0, 2, 4):
                        normalise(c, s // 2)
                    elif s in (6, 7, 8):
                        project_in(c, 2 * (s - 6))
                        project_in(c, 2 * (s - 6) + 1)
                    elif s == 11:
                        project_x(c)
                    elif s == 12:
                        for d in range(DT3):
                            project_dt(c, d)

                for s in range(DS):
                    start(0, s)
                for c in range(NC):
                    pe.wait_ge(bc_step, 4 * (NC * l + c) + 4)
                    pe.wait_ge(bc_mid_stored, NC * l + c + 2)
                    for s in range(DS + 2):
                        if s < DS:
                            spread(c, s)
                        if s >= 2:
                            reduce(c, s - 2)
                        if c + 1 < NC and s < DS:
                            start(c + 1, s)
                    project_out(c)

        @block.scalar
        def _(act):
            start_at_one(act, dt_stored, c_stored, affined, bc_mid_stored)
            with act.Fori(0, LAYERS) as l:
                act.wait_ge(params_landed, 48 * l + 48)
                act.activation(a_exp[:], cut["a_log"], ACT.Exp).then_inc(a_exped, 1)

                def store_in(c, m):
                    n = NC * l + c
                    act.wait_ge(in_summed, 2 * DT3 * n + m + 2)
                    d = m % DT3
                    bank = banks[6 + m % 2][:, 0:CT]
                    if m < DT3:
                        if m == 0:
                            act.wait_ge(tapped, TAPS * DT3 * n + 1)
                        act.activation(padded[:, d, :, DCONV - 1:], bank.rearrange("p (b t) -> p b t", t=T), ACT.Copy).then_inc(in_stored, 1)
                    else:
                        if m == DT3 and c < 2:
                            act.wait_ge(gated, NC * l + 1)
                        elif m == DT3:
                            act.wait_ge(gated, n)
                        act.activation(zs[:, c % 2, d], bank, ACT.Silu).then_inc(in_stored, 1)

                def conv_silu(c):
                    n = NC * l + c
                    act.wait_ge(tapped, TAPS * DT3 * (n + 1) + 1)
                    act.activation(xa[:, c % 2], conv[:], ACT.Silu).then_inc(conv_silued, 1)

                def low_rank(c):
                    n = NC * l + c
                    low = slice(2 * DS, 2 * DS + DTR)
                    act.wait_ge(x_summed, n + 1)
                    act.wait_ge(dt_summed, DT3 * n + 1)
                    act.activation(dtr[low, :], banks[6][low, 0:CT], ACT.Copy).then_inc(dtr_stored, 1)

                def store_mid(c):
                    n = NC * l + c
                    act.wait_ge(bc_step, 4 * n + 3)
                    act.activation(bc[2 * DS:4 * DS, c % 2], mid[:], ACT.Copy).then_inc(bc_mid_stored, 1)

                def soften(c):
                    n = NC * l + c
                    act.wait_ge(dt_ready, n + 1)
                    for d in range(DT3):
                        act.wait_ge(dt_summed, DT3 * n + d + 2)
                        act.activation(xb[:, d], banks[7 - d % 2][:, 0:CT], ACT.Identity, bias=cut["dt_b"][:, d:d + 1]).then_inc(dt_stored, 1)
                    act.wait_ge(dt_stored, DT3 * (n + 1) + 1)
                    act.activation(ab[:], xb[:], ACT.Abs).then_inc(dt_absed, 1)
                    act.wait_ge(dt_absed, n + 1)
                    act.activation(eb[:], ab[:], ACT.Exp, scale=-1.0).then_inc(dt_exped, 1)

                def soften_log(c):
                    n = NC * l + c
                    act.wait_ge(dt_one, n + 1)
                    act.activation(lb[:], ub[:], ACT.Ln).then_inc(dt_logged, 1)

                def affine(c):
                    n = NC * l + c
                    act.wait_ge(norm.scaled, n + 1)
                    act.wait_ge(in_summed, 2 * DT3 * n + 1)
                    for k in range(2):
                        last = act.activation(un[:, k], xn[:, k], ACT.Identity, bias=norm_b[:, k:k + 1], scale=norm_w[:, k:k + 1])
                    last.then_inc(affined, 1)

                def first_tap(c, d):
                    n = NC * l + c
                    act.wait_ge(in_stored, 2 * DT3 * n + d + 1)
                    act.activation(conv[:, d].rearrange("p (b t) -> p b t", t=T), padded[:, d, :, 0:T], ACT.Identity,
                                   bias=cut["conv_b"][:, d:d + 1], scale=conv_w[:, d, 0:1]).then_inc(tap0, 1)

                def start(c, s):
                    if s == 1:
                        norm.act_square(act, NC * l + c, sq[:], xc[:])
                    elif s == 3:
                        norm.act_root(act, NC * l + c)
                    elif s == 4:
                        affine(c)
                    elif s in (6, 7, 8):
                        store_in(c, 2 * (s - 6))
                        store_in(c, 2 * (s - 6) + 1)
                        if s == 7:
                            for d in range(DT3):
                                first_tap(c, d)
                    elif s == 10:
                        conv_silu(c)
                    elif s == 11:
                        low_rank(c)
                    elif s == 12:
                        store_mid(c)
                        soften(c)
                    elif s == 14:
                        soften_log(c)

                for s in range(DS):
                    start(0, s)
                act.wait_ge(a_ready, l + 1)
                for c in range(NC):
                    n = NC * l + c
                    act.wait_ge(dt_ready, n + 2)
                    for s in range(DS):
                        i = DS * n + s
                        if s >= 2:
                            act.wait_ge(scanned, i)
                        elif s == 0:
                            act.wait_ge(scanned, i + 1)
                        for d in range(DT3):
                            last = act.activation(da[:, s % 2, d, :, 1:], dt[:, c % 2, d].rearrange("p (b t) -> p b t", t=T)[:, :, 1:],
                                                  ACT.Exp, scale=a_neg[:, d * DS + s:d * DS + s + 1])
                        last.then_inc(decayed, 1)
                        act.wait_ge(c_spread, i + 1)
                        if s >= 2:
                            act.wait_ge(produced, i)
                        elif s == 0:
                            act.wait_ge(produced, i + 1)
                        act.activation(cs[:, s % 2], banks[5][:, 0:CT], ACT.Copy).then_inc(c_stored, 1)
                        if c + 1 < NC:
                            start(c + 1, s)

        @block.vector
        def _(dve):
            start_at_one(dve, added, fed, skipped, tapped, gated, dt_ready, scanned)
            dve.memset(da[:, :, :, :, 0:1], 0.0)
            dve.memset(padded[:, :, :, 0:DCONV - 1], 0.0).then_inc(zeroed, 1)
            dve.wait_ge(zeroed, 1)
            with dve.Fori(0, LAYERS) as l:
                dve.wait_ge(params_landed, 48 * l + 48)
                dve.wait_ge(a_exped, l + 1)
                dve.tensor_scalar(a_neg[:], a_exp[:], -1.0, None, ALU.mult).then_inc(a_ready, 1)

                def convolve(c, d):
                    n = NC * l + c
                    dve.wait_ge(tap0, DT3 * n + d + 1)
                    out = conv[:, d].rearrange("p (b t) -> p b t", t=T)
                    for k in range(1, DCONV):
                        if k > 1:
                            dve.wait_ge(tapped, TAPS * (DT3 * n + d) + k)
                        dve.scalar_tensor_tensor(out, padded[:, d, :, k:k + T], conv_w[:, d, k:k + 1], out, ALU.mult,
                                                 ALU.add).then_inc(tapped, 1)

                def split_bc(c):
                    n = NC * l + c
                    dve.wait_ge(x_summed, n + 1)
                    summed = banks[6][0:2 * DS, 0:CT]
                    high = bc[0:2 * DS, c % 2]
                    dve.tensor_copy(high, summed).then_inc(bc_step, 1)
                    dve.wait_ge(bc_step, 4 * n + 1)
                    dve.tensor_tensor(rest1[:], summed, high, ALU.subtract).then_inc(bc_step, 1)
                    dve.wait_ge(bc_step, 4 * n + 2)
                    dve.wait_ge(bc_mid_stored, n + 1)
                    dve.tensor_copy(mid[:], rest1[:]).then_inc(bc_step, 1)
                    dve.wait_ge(bc_step, 4 * n + 3)
                    dve.tensor_tensor(bc[4 * DS:6 * DS, c % 2], rest1[:], mid[:], ALU.subtract).then_inc(bc_step, 1)

                def soften(c, part):
                    n = NC * l + c
                    if part == 0:
                        dve.wait_ge(dt_exped, n + 1)
                        dve.tensor_scalar(ub[:], eb[:], 1.0, None, ALU.add).then_inc(dt_one, 1)
                        dve.wait_ge(dt_one, n + 1)
                        dve.scalar_tensor_tensor(lost[:], ub[:], -1.0, eb[:], ALU.add, ALU.subtract).then_inc(dt_lost, 1)
                    else:
                        dve.wait_ge(dt_logged, n + 1)
                        dve.wait_ge(dt_lost, n + 1)
                        dve.tensor_tensor(lost[:], lb[:], lost[:], ALU.subtract).then_inc(dt_fixed, 1)
                        dve.wait_ge(dt_fixed, n + 1)
                        dve.scalar_tensor_tensor(dt[:, c % 2], xb[:], 0.0, lost[:], ALU.max, ALU.add).then_inc(dt_ready, 1)
                        dve.wait_ge(dt_ready, n + 2)
                        dve.tensor_tensor(dtx[:, c % 2], dt[:, c % 2], xa[:, c % 2], ALU.mult).then_inc(dtx_ready, 1)

                def start(c, s):
                    n = NC * l + c
                    if s == 0:
                        norm.dve_centre(dve, n, xc[:], chunk(resid, c))
                    elif s == 2:
                        norm.dve_eps(dve, n)
                    elif s == 3:
                        norm.dve_invert(dve, n)
                    elif s == 4:
                        dve.wait_ge(affined, n + 1)
                        norm.dve_scale(dve, n, xn[:], xc[:])
                    elif s in (7, 8, 9):
                        convolve(c, s - 7)
                    elif s == 11:
                        split_bc(c)
                    elif s == 13:
                        soften(c, 0)
                    elif s == 14:
                        soften(c, 1)

                for s in range(DS):
                    start(0, s)
                for c in range(NC):
                    n = NC * l + c
                    dve.wait_ge(dtx_ready, n + 1)

                    def feed(s):
                        i = DS * n + s
                        dve.wait_ge(b_spread, i + 1)
                        if s >= 3:
                            dve.wait_ge(scanned, i - 1)
                        dve.tensor_tensor(dbx[:, s % 3].rearrange("p (d t) -> p d t", d=DT3), dtx[:, c % 2],
                                          banks[3 + s % 2][:, 0:CT].unsqueeze(1).broadcast_to([128, DT3, CT]), ALU.mult).then_inc(fed, 1)

                    feed(0)
                    for s in range(DS):
                        i = DS * n + s
                        if s + 1 < DS:
                            feed(s + 1)
                        dve.wait_ge(fed, i + 2)
                        dve.wait_ge(decayed, i + 1)
                        if s >= 2:
                            dve.wait_ge(produced, i)
                        elif s == 0:
                            dve.wait_ge(produced, i + 1)
                        dve.tensor_tensor_scan(hs[:, s % 2], da[:, s % 2].rearrange("p d b t -> p (d b t)"), dbx[:, s % 3], 0.0,
                                               ALU.mult, ALU.add).then_inc(scanned, 1)
                        if c + 1 < NC:
                            start(c + 1, s)
                    dve.wait_ge(reduced, DS * (n + 1) + 1)
                    for d in range(DT3):
                        dve.scalar_tensor_tensor(yt[:, d], xa[:, c % 2, d], cut["skip"][:, d:d + 1], banks[d][:, 0:CT],
                                                 ALU.mult, ALU.add).then_inc(skipped, 1)
                    dve.wait_ge(skipped, DT3 * (n + 1) + 1)
                    dve.wait_ge(out_summed, n + 1)
                    dve.tensor_tensor(yg[:], yt[:], zs[:, c % 2], ALU.mult).then_inc(gated, 1)
                    dve.wait_ge(out_summed, n + 2)
                    for k in range(2):
                        last = dve.tensor_tensor(resid[:, k, c * CT:(c + 1) * CT], resid[:, k, c * CT:(c + 1) * CT],
                                                 banks[6 + k][0:DH, 0:CT], ALU.add)
                    last.then_inc(added, 1)

        @block.gpsimd
        def _(pool):
            start_at_one(pool, produced)
            with pool.Fori(0, LAYERS) as l:
                for c in range(NC):
                    n = NC * l + c
                    for s in range(DS):
                        i = DS * n + s
                        pool.wait_ge(scanned, i + 2)
                        pool.wait_ge(c_stored, i + 2)
                        if s >= 2:
                            pool.wait_ge(reduced, i)
                        elif s == 0:
                            pool.wait_ge(reduced, i + 1)
                        pool.tensor_tensor(prod[:, s % 2].rearrange("p (d t) -> p d t", d=DT3), hs[:, s % 2].rearrange("p (d t) -> p d t", d=DT3),
                                           cs[:, s % 2].unsqueeze(1).broadcast_to([128, DT3, CT]), ALU.mult).then_inc(produced, 1)


def normalise_tokens(nc, tag, banks, consts, src, dst, eps=LN_EPS):
    with ExitStack() as ctx:
        sb = lambda name, shape, dt=F32: ctx.enter_context(nc.sbuf_tensor(f"{tag}_{name}", shape, dt))
        sem = ctx.enter_context(Semaphores(nc, tag + "_"))
        xc, sq = sb("nt_xc", [DH, 2, N]), sb("nt_sq", [DH, 2, N])
        norm = Norm(nc, sb, sem, "nt", consts, banks[0], banks[1], banks[2], eps)
        on_pe, on_dve, on_act = whole_norm(norm, src, xc, sq, dst)
        block = ctx.enter_context(nc.Block())
        block.tensor(on_pe)
        block.vector(on_dve)
        block.scalar(on_act)


def normalise_roots(nc, tag, banks, consts, src, dst):
    with ExitStack() as ctx:
        sb = lambda name, shape, dt=F32: ctx.enter_context(nc.sbuf_tensor(f"{tag}_{name}", shape, dt))
        sem = ctx.enter_context(Semaphores(nc, tag + "_"))
        sq = sb("nr_sq", [DH, 2, N])
        norm = Norm(nc, sb, sem, "nr", consts, banks[0], banks[1], banks[2], RMS_EPS, gain=2.0)
        on_pe, on_dve, on_act = whole_norm(norm, None, src, sq, dst, centred=False)
        block = ctx.enter_context(nc.Block())
        block.tensor(on_pe)
        block.vector(on_dve)
        block.scalar(on_act)


def add_last_norm(nc, banks, consts, stream, resid, last_wb):
    with ExitStack() as ctx:
        sb = lambda name, shape, dt=F32: ctx.enter_context(nc.sbuf_tensor(name, shape, dt))
        sem = ctx.enter_context(Semaphores(nc))
        xc, sq, xn = sb("ln_xc", [DH, 2, N]), sb("ln_sq", [DH, 2, N]), sb("ln_xn", [DH, 2, N])
        wb = sb("ln_wb", [DH, 2, 2])
        wb_landed, affined = sem("last_wb_landed"), sem("last_affined")
        norm = Norm(nc, sb, sem, "ln", consts, banks[0], banks[1], banks[2], LN_EPS)
        on_pe, on_dve, on_act = whole_norm(norm, resid, xc, sq, xn)
        block = ctx.enter_context(nc.Block())
        block.tensor(on_pe)
        block.scalar(on_act)

        @block.sync
        def _(sp):
            sp.dma_start(wb[:], last_wb).then_inc(wb_landed, 16)

        @block.vector
        def _(dve):
            on_dve(dve)
            dve.wait_ge(norm.scaled, NC)
            dve.wait_ge(wb_landed, 16)
            for k in range(2):
                dve.tensor_scalar(xn[:, k], xn[:, k], wb[:, 0, k:k + 1], wb[:, 1, k:k + 1], ALU.mult, ALU.add).then_inc(affined, 1)
                dve.wait_ge(affined, k + 1)
                dve.tensor_tensor(stream[:, k], stream[:, k], xn[:, k], ALU.add)


def store(nc, banks, consts, stream, out):
    with ExitStack() as ctx:
        sb = lambda name, shape, dt=F32: ctx.enter_context(nc.sbuf_tensor(name, shape, dt))
        sem = ctx.enter_context(Semaphores(nc))
        rows = sb("out_rows", [GT, NG, D])
        turned, copied, written = sem("out_turned"), sem("out_copied"), sem("out_written")
        block = ctx.enter_context(nc.Block())

        @block.tensor
        def _(pe):
            for g in range(NG):
                if g >= 4:
                    pe.wait_ge(copied, g - 3)
                for k in range(2):
                    mm = pe.transpose(banks[g % 4][0:GT, k * DH:(k + 1) * DH], stream[:, k, g * GT:(g + 1) * GT],
                                      consts["ident"][0:DH, 0:DH])
                mm.then_inc(turned, 1)

        @block.vector
        def _(dve):
            for g in range(NG):
                dve.wait_ge(turned, g + 1)
                dve.tensor_copy(rows[:, g], banks[g % 4][0:GT, 0:D]).then_inc(copied, 1)

        @block.sync
        def _(sp):
            for q in range(NC):
                sp.wait_ge(copied, GC * (q + 1))
                sp.dma_start(out.rearrange("b t d -> (b t) d").rearrange("(g p) d -> p g d", p=GT)[:, q * GC:(q + 1) * GC],
                             rows[:, q * GC:(q + 1) * GC]).then_inc(written, 16)
            sp.wait_ge(written, 16 * NC)


CONSTS = {"mean": ([DH, DH], F32), "ident": ([128, 128], F32), "ones": ([128, 128], F32), "rotate": ([128, 128], F32),
          "mask": ([GT, GT], F32), "before": ([GT, GT], F32), "expert_names": ([GT, E], F32), "pick": ([E, E, DH], F32),
          "part_rows": ([6 * DS, 2 * DS], F32)}


def constants():
    f = np.float32
    rotate = np.zeros((128, 128), f)
    for h in range(4):
        for i in range(0, HD, 2):
            rotate[32 * h + i + 1, 32 * h + i] = -1.0
            rotate[32 * h + i, 32 * h + i + 1] = 1.0
    seq = np.arange(GT) // T
    pick = np.zeros((E, E, DH), f)
    for e in range(E):
        pick[e, e] = 1.0
    freq = (1.0 / 10000.0 ** (np.arange(0, HD, 2, dtype=f) / f(HD))).astype(f)
    angle = np.arange(T, dtype=f)[:, None] * freq[None]
    angle = np.concatenate([angle, angle], -1).T
    rope = np.zeros((128, 2, CB, T), f)
    for h in range(4):
        rope[32 * h:32 * h + HD, 0] = np.cos(angle)[:, None]
        rope[32 * h:32 * h + HD, 1] = np.sin(angle)[:, None]
    return {
        "mean": np.full((DH, DH), 1.0 / D, f), "ident": np.eye(128, dtype=f), "ones": np.ones((128, 128), f), "rotate": rotate,
        "mask": np.where(seq[:, None] == seq[None], 0.0, MASKED).astype(f),
        "before": np.triu(np.ones((GT, GT), f), 1), "expert_names": np.tile(np.arange(E, dtype=f), (GT, 1)), "pick": pick,
        "part_rows": np.tile(np.eye(2 * DS, dtype=f), (3, 1))}, rope.reshape(128, 2, CT)


def audio_tower(nc, a, out, probe=None):
    with ExitStack() as ctx:
        sb = lambda name, shape, dt=F32: ctx.enter_context(nc.sbuf_tensor(name, shape, dt))
        psum = ctx.enter_context(nc.psum_tensor("banks", [128, 8, 512], F32))
        banks = [psum[:, b] for b in range(8)]
        stream = sb("stream", [DH, 2, N])
        consts = {name: sb("const_" + name, shape, dt) for name, (shape, dt) in CONSTS.items()}
        spread = sb("const_spread", [6 * DS, 2 * DS, 128], BF16)
        consts["spread"] = spread
        landed = ctx.enter_context(nc.semaphore("constants_landed"))
        made = ctx.enter_context(nc.semaphore("spread_made"))
        with nc.Block() as block:
            @block.sync
            def _(sp):
                for name in CONSTS:
                    sp.dma_start(consts[name][:], a[name]).then_inc(landed, 16)
                sp.wait_ge(landed, 16 * len(CONSTS))

            @block.gpsimd
            def _(pool):
                pool.wait_ge(landed, 16 * len(CONSTS))
                pool.tensor_copy(spread[:], consts["part_rows"][:].unsqueeze(2).broadcast_to([6 * DS, 2 * DS, 128])).then_inc(made, 1)

        def show(tile):
            done = ctx.enter_context(nc.semaphore("probe"))
            with nc.Block() as block:
                @block.sync
                def _(sp):
                    sp.dma_start(out, tile).then_inc(done, 16)
                    sp.wait_ge(done, 16)

        embed(nc, banks, stream, a["x"], a["tok_w"], a["tok_b"])
        if probe == "embed":
            return show(stream[:])
        attention(nc, banks, stream, consts, a["qk_w"], a["qk_b"], a["v_w"], a["v_b"], a["attn_out_w"], a["attn_out_b"], a["rope"])
        if probe == "attn":
            return show(stream[:])
        with ExitStack() as inner:
            isb = lambda name, shape: inner.enter_context(nc.sbuf_tensor(name, shape, F32))
            xf, zn = isb("moe0_x", [DH, 2, N]), isb("moe0_z", [DH, 2, N])
            w_rep, w_t = isb("moe0_weights_rep", [DH, E, N]), isb("moe0_weights_t", [E, N])
            normalise_tokens(nc, "norm0", banks, consts, stream, xf)
            normalise_roots(nc, "roots0", banks, consts, xf, zn)
            route(nc, "route0", banks, consts, xf, a["gate0_w"], None, w_rep, w_t, CAP)
            experts(nc, "moe0", banks, consts, stream, zn, xf, w_rep, w_t, a["moe0_in"], a["moe0_out"], H0, norm_w=a["moe0_norm"])
        if probe == "moe0":
            return show(stream[:])
        with ExitStack() as inner:
            resid = inner.enter_context(nc.sbuf_tensor("resid", [DH, 2, N], F32))
            normalise_tokens(nc, "norm_r", banks, consts, stream, resid)
            state_space(nc, banks, consts, resid, a["p96"], a["p128"], a["dt_w"])
            add_last_norm(nc, banks, consts, stream, resid, a["last_wb"])
        if probe == "mamba":
            return show(stream[:])
        with ExitStack() as inner:
            isb = lambda name, shape: inner.enter_context(nc.sbuf_tensor(name, shape, F32))
            xn = isb("moe1_x", [DH, 2, N])
            w_rep, w_t = isb("moe1_weights_rep", [DH, E, N]), isb("moe1_weights_t", [E, N])
            normalise_tokens(nc, "norm1", banks, consts, stream, xn)
            route(nc, "route1", banks, consts, xn, a["gate1_w"], a["gate1_b"], w_rep, w_t, None)
            experts(nc, "moe1", banks, consts, stream, xn, None, w_rep, w_t, a["moe1_in"], a["moe1_out"], H1, b_in=a["moe1_b_in"], b_out=a["moe1_b_out"])
        if probe == "moe1":
            return show(stream[:])
        store(nc, banks, consts, stream, out)


def halves(w):
    return w.reshape(2, DH, *w.shape[1:]).swapaxes(0, 1)


def tiles(w, n):
    return w.reshape(n, 128, *w.shape[1:]).swapaxes(0, 1)


def laid_out(i):
    a, a["rope"] = constants()
    a["x"] = i["x"]
    a["tok_w"] = i["L0_tok_W"].reshape(D, CHANNELS, PATCH).transpose(1, 2, 0)
    a["tok_b"] = halves(i["L0_tok_b"])
    wqkv, bqkv = i["L0_attn_W_qkv"], i["L0_attn_b_qkv"]
    qk_w, qk_b = np.zeros((D, 2, QT, 4, 32), np.float32), np.zeros((2, QT, 4, 32), np.float32)
    qk_w[..., :HD] = wqkv[:, :2 * D].reshape(D, 2, QT, 4, HD)
    qk_b[..., :HD] = bqkv[:2 * D].reshape(2, QT, 4, HD)
    a["qk_w"] = halves(qk_w.reshape(D, 2 * QT, 128))
    a["qk_b"] = qk_b.reshape(2 * QT, 128).T
    a["v_w"] = halves(wqkv[:, 2 * D:])
    a["v_b"] = np.tile(bqkv[2 * D:], (GT, 1))
    a["attn_out_w"] = halves(i["L0_attn_W_out"])
    a["attn_out_b"] = halves(i["L0_attn_b_out"])
    a["gate0_w"] = halves(i["L0_ffn_gate_w"].T)
    a["moe0_in"] = np.stack([halves(w.T) for w in i["L0_ffn_w13"]])
    a["moe0_out"] = np.stack([tiles(w.T, H0 // 128) for w in i["L0_ffn_w2"]])
    a["moe0_norm"] = np.stack([halves(w) for w in i["L0_ffn_norm_w"]])
    m = {k[len("L1_attn_"):]: v for k, v in i.items() if k.startswith("L1_attn_")}
    a["p96"] = np.stack([np.concatenate([halves(m["in_proj_w"][l].T).reshape(DH, -1), halves(m["norm_w"][l]), halves(m["norm_b"][l])], 1)
                         for l in range(LAYERS)])
    x_w = np.concatenate([m["x_proj_w"][:, DTR:], m["x_proj_w"][:, :DTR]], 1)
    flat = lambda w: tiles(w, DT3).reshape(128, -1)
    a["p128"] = np.stack([np.concatenate([flat(m["conv_w"][l]), flat(m["conv_b"][l]), flat(m["dt_proj_b"][l]), flat(m["D_skip"][l]),
                                          flat(m["A_log"][l]), flat(x_w[l].T), flat(m["out_proj_w"][l].T)], 1) for l in range(LAYERS)])
    a["dt_w"] = m["dt_proj_w"].transpose(0, 2, 1)
    a["last_wb"] = np.stack([halves(m["norm_f_w"]), halves(m["norm_f_b"])], 1)
    a["gate1_w"] = halves(i["L1_ffn_Wg"].T)
    a["gate1_b"] = np.tile(i["L1_ffn_bg"], (GT, 1))
    a["moe1_in"] = np.stack([halves(w) for w in i["L1_ffn_W1"]])
    a["moe1_out"] = np.stack([tiles(w, H1 // 128) for w in i["L1_ffn_W2"]])
    a["moe1_b_in"] = np.stack([tiles(b, H1 // 128) for b in i["L1_ffn_b1"]])
    a["moe1_b_out"] = i["L1_ffn_b2"]
    return {name: np.ascontiguousarray(v) for name, v in a.items()}


def kernel(**inputs):
    import concourse.bacc as bacc
    from concourse.bass_utils import run_bass_kernel_spmd

    arrays = laid_out({name: np.asarray(v) for name, v in inputs.items()})
    nc = bacc.Bacc("TRN2", target_bir_lowering=False, num_devices=1)
    dram = {name: nc.dram_tensor("in_" + name, v.shape, mybir.dt.from_np(v.dtype), kind="ExternalInput").ap() for name, v in arrays.items()}
    out = nc.dram_tensor("out", (SEQS, T, D), F32, kind="ExternalOutput").ap()
    audio_tower(nc, dram, out)
    result = run_bass_kernel_spmd(nc, [{"in_" + name: v for name, v in arrays.items()}], core_ids=[0])
    return result.results[0]["out"]
```

```python
from contextlib import ExitStack

import numpy as np
import concourse.bass as bass
from concourse import mybir

ALU = mybir.AluOpType
ACT = mybir.ActivationFunctionType
AX = mybir.AxisListType
F32 = mybir.dt.float32
BF16 = mybir.dt.bfloat16
U32 = mybir.dt.uint32

SEQS, CHANNELS, SAMPLES, PATCH = 64, 90, 375, 16
T = SAMPLES // PATCH
N = SEQS * T
CHANNEL_ROWS = -(-CHANNELS // 32) * 32
D = 192
DH = D // 2
CB = 16
CT = CB * T
NC = N // CT
GB = 4
GT = GB * T
NG = N // GT
GC = CT // GT
HEADS, HD = 12, 16
QT = 3
E = 8
H0 = 512
H1 = 768
CAP = -(-5 * 2 * N // (4 * E))
LAYERS, DI, DS, DCONV, DTR = 4, 384, 16, 4, 12
DT3 = DI // 128
TAPS = DCONV - 1
SP = CAP // 4
TS = 128
NT = (2 * N + E * (TS - 1)) // TS
NT += NT % 2
MASKED = -1e30
LN_EPS, RMS_EPS = 1e-5, 1e-6


class Semaphores:

    def __init__(self, nc, prefix=""):
        self.nc, self.prefix, self.taken = nc, prefix, []

    def __enter__(self):
        return self

    def __call__(self, name):
        self.taken.append(self.nc.alloc_semaphore(self.prefix + name))
        return self.taken[-1]

    def __exit__(self, *error):
        if error[0] is None:
            self.nc.clear_and_free_semaphores(self.taken)
            self.nc.all_engine_barrier()


def start_at_one(eng, *semaphores):
    for semaphore in semaphores:
        eng.sem_inc(semaphore, 1)


class Norm:

    def __init__(self, nc, sb, sem, name, consts, mean_bank, var_bank, rep_bank, eps, gain=1.0):
        self.nc, self.consts, self.eps, self.gain = nc, consts, eps, gain
        self.mean_bank, self.var_bank, self.rep_bank = mean_bank, var_bank, rep_bank
        self.ve = sb(name + "_var_eps", [GT, GC])
        self.std = sb(name + "_std", [GT, GC])
        self.inv = sb(name + "_inv", [GT, GC])
        if gain != 1.0:
            self.inv_gain = sb(name + "_inv_gain", [GT, GC])
        else:
            self.inv_gain = self.inv
        self.meaned = sem(name + "_meaned")
        self.centred = sem(name + "_centred")
        self.squared = sem(name + "_squared")
        self.summed = sem(name + "_summed")
        self.eps_added = sem(name + "_eps_added")
        self.rooted = sem(name + "_rooted")
        self.inverted = sem(name + "_inverted")
        self.gained = sem(name + "_gained")
        self.spread = sem(name + "_spread")
        self.scaled = sem(name + "_scaled")

    def pe_mean(self, pe, src):
        for k in range(2):
            mm = pe.matmul(self.mean_bank[0:DH, 0:CT], self.consts["mean"][:, 0:DH], src[:, k], start=(k == 0), stop=(k == 1))
        mm.then_inc(self.meaned, 1)

    def pe_square(self, pe, n, sq):
        pe.wait_ge(self.squared, n + 1)
        for g in range(GC):
            for k in range(2):
                mm = pe.matmul(self.var_bank[0:GT, g:g + 1], sq[:, k, g * GT:(g + 1) * GT], self.consts["mean"][:, 0:1],
                               start=(k == 0), stop=(k == 1))
        mm.then_inc(self.summed, 1)

    def pe_spread(self, pe, n):
        pe.wait_ge(self.inverted if self.gain == 1.0 else self.gained, n + 1)
        for g in range(GC):
            mm = pe.matmul(self.rep_bank[0:DH, g * GT:(g + 1) * GT], self.inv_gain[:, g:g + 1].broadcast_to([GT, DH]),
                           self.consts["ident"][0:GT, 0:GT], start=True, stop=True)
        mm.then_inc(self.spread, 1)

    def dve_centre(self, dve, n, xc, src):
        dve.wait_ge(self.meaned, n + 1)
        dve.tensor_tensor(xc, src, self.mean_bank[0:DH, 0:CT].unsqueeze(1).broadcast_to([DH, 2, CT]),
                          ALU.subtract).then_inc(self.centred, 1)

    def act_square(self, act, n, sq, xc):
        act.wait_ge(self.centred, n + 1)
        act.activation(sq, xc, ACT.Square).then_inc(self.squared, 1)

    def dve_eps(self, dve, n):
        dve.wait_ge(self.summed, n + 1)
        dve.tensor_scalar(self.ve[:], self.var_bank[0:GT, 0:GC], self.gain * self.gain, self.eps,
                          ALU.mult, ALU.add).then_inc(self.eps_added, 1)

    def act_root(self, act, n):
        act.wait_ge(self.eps_added, n + 1)
        act.activation(self.std[:], self.ve[:], ACT.Sqrt).then_inc(self.rooted, 1)

    def dve_invert(self, dve, n):
        dve.wait_ge(self.rooted, n + 1)
        dve.reciprocal(self.inv[:], self.std[:]).then_inc(self.inverted, 1)
        if self.gain != 1.0:
            dve.wait_ge(self.inverted, n + 1)
            dve.tensor_scalar(self.inv_gain[:], self.inv[:], self.gain, None, ALU.mult).then_inc(self.gained, 1)

    def dve_scale(self, dve, n, dst, xc):
        dve.wait_ge(self.spread, n + 1)
        dve.tensor_tensor(dst, xc, self.rep_bank[0:DH, 0:CT].unsqueeze(1).broadcast_to([DH, 2, CT]),
                          ALU.mult).then_inc(self.scaled, 1)


def chunk(tile, c):
    return tile[:, :, bass.ds(c * CT, CT)]


def whole_norm(norm, src, xc, sq, dst, centred=True, n0=0, first=None):

    def on_pe(pe):
        for c in range(NC):
            if centred:
                if first is not None:
                    first(pe, c)
                if c >= 1:
                    pe.wait_ge(norm.centred, n0 + c)
                norm.pe_mean(pe, chunk(src, c))
            norm.pe_square(pe, n0 + c, chunk(sq, c))
            norm.pe_spread(pe, n0 + c)

    def on_dve(dve):
        for c in range(NC):
            if centred:
                norm.dve_centre(dve, n0 + c, chunk(xc, c), chunk(src, c))
            norm.dve_eps(dve, n0 + c)
            norm.dve_invert(dve, n0 + c)
            if centred:
                dve.wait_ge(norm.centred, n0 + c + 1)
            norm.dve_scale(dve, n0 + c, chunk(dst, c), chunk(xc, c))

    def on_act(act):
        for c in range(NC):
            if centred:
                norm.act_square(act, n0 + c, chunk(sq, c), chunk(xc, c))
            else:
                act.activation(chunk(sq, c), chunk(xc, c), ACT.Square).then_inc(norm.squared, 1)
            norm.act_root(act, n0 + c)

    return on_pe, on_dve, on_act


def embed(nc, banks, stream, x, tok_w, tok_b, consts, const_srcs, cleared):
    with ExitStack() as ctx:
        sb = lambda name, shape, dt=F32: ctx.enter_context(nc.sbuf_tensor(name, shape, dt))
        sem = ctx.enter_context(Semaphores(nc))
        xs = [sb(f"signal{u}", [CHANNELS, CB, SAMPLES]) for u in range(2)]
        patches = [sb(f"patches{u}", [CHANNEL_ROWS, PATCH, CB, T]) for u in range(2)]
        part_rows = sb("const_part_rows", [6 * DS, 2 * DS])
        w = sb("patch_w", [CHANNEL_ROWS, PATCH, D])
        b = sb("patch_b", [DH, 2])
        WP = 4
        w_landed = [sem(f"patch_w{q}_landed") for q in range(PATCH // WP)]
        b_landed = sem("patch_b_landed")
        const_landed = sem("constants_landed")
        spread_made = sem("spread_made")
        x_landed = [sem(f"signal{u}_landed") for u in range(2)]
        ZR = 32
        zeros = sb("zeros", [128, ZR * D])
        zeroed = sem("zeros_made")
        slots_cleared = sem("slots_cleared")
        padded = sem("patches_padded")
        sorted_in = sem("patches_sorted")
        summed = [sem(f"patch_half{k}_summed") for k in range(2)]
        stored = [sem(f"patch_half{k}_stored") for k in range(2)]
        block = ctx.enter_context(nc.Block())
        K = PATCH // WP

        def load(sp, c):
            sp.dma_start(xs[c % 2][:], x[c * CB:(c + 1) * CB].rearrange("b c t -> c b t")).then_inc(x_landed[c % 2], 16)

        @block.sync
        def _(sp):
            load(sp, 0)
            for q in range(K):
                sp.dma_start(w[:, q * WP:(q + 1) * WP], tok_w[:, q * WP:(q + 1) * WP]).then_inc(w_landed[q], 16)
            sp.dma_start(b[:], tok_b).then_inc(b_landed, 16)
            load(sp, 1)
            for name, src in const_srcs.items():
                sp.dma_start((part_rows if name == "part_rows" else consts[name])[:], src).then_inc(const_landed, 16)
            for c in range(2, NC):
                sp.wait_ge(sorted_in, K * (c - 1))
                load(sp, c)
            sp.wait_ge(const_landed, 16 * len(const_srcs))
            sp.wait_ge(zeroed, 1)
            for slots in cleared:
                sp.dma_start(slots.rearrange("(p r) d -> p (r d)", r=ZR), zeros[0:slots.shape[0] // ZR]).then_inc(slots_cleared, 16)
            sp.wait_ge(slots_cleared, 16 * len(cleared))

        @block.vector
        def _(dve):
            for c in range(NC):
                if c < 2:
                    dve.wait_ge(padded, c + 1)
                dve.wait_ge(x_landed[c % 2], 16 * (c // 2 + 1))
                if c >= 2:
                    dve.wait_ge(summed[1], c - 1)
                signal = xs[c % 2][:, :, 0:PATCH * T].rearrange("c b (t p) -> c p b t", p=PATCH)
                for q in range(K):
                    for p in range(q * WP, (q + 1) * WP):
                        last = dve.tensor_copy(patches[c % 2][0:CHANNELS, p], signal[:, p])
                    last.then_inc(sorted_in, 1)

        @block.gpsimd
        def _(pool):
            for u in range(2):
                pool.memset(patches[u][CHANNEL_ROWS - 32:CHANNEL_ROWS], 0.0).then_inc(padded, 1)
            pool.wait_ge(padded, 2)
            pool.memset(zeros[:], 0.0).then_inc(zeroed, 1)
            pool.wait_ge(zeroed, 1)
            pool.wait_ge(const_landed, 16 * len(const_srcs))
            pool.tensor_copy(consts["spread"][:], part_rows[:].unsqueeze(2).broadcast_to([6 * DS, 2 * DS, 128])).then_inc(spread_made, 1)

        @block.tensor
        def _(pe):
            for c in range(NC):
                for k in range(2):
                    if c >= 1:
                        pe.wait_ge(stored[k], c)
                    for p in range(PATCH):
                        if k == 0 and p % WP == 0:
                            pe.wait_ge(sorted_in, K * c + p // WP + 1)
                            if c == 0:
                                pe.wait_ge(w_landed[p // WP], 16)
                        mm = pe.matmul(banks[k][0:DH, 0:CT], w[:, p, k * DH:(k + 1) * DH],
                                       patches[c % 2][:, p].rearrange("c b t -> c (b t)"), start=(p == 0), stop=(p == PATCH - 1))
                    mm.then_inc(summed[k], 1)

        @block.scalar
        def _(act):
            act.wait_ge(b_landed, 16)
            for c in range(NC):
                for k in range(2):
                    act.wait_ge(summed[k], c + 1)
                    act.activation(stream[:, k, c * CT:(c + 1) * CT], banks[k][0:DH, 0:CT], ACT.Identity,
                                   bias=b[:, k:k + 1]).then_inc(stored[k], 1)


def attention(nc, banks, stream, consts, qk_w, qk_b, v_w, v_b, out_w, out_b, rope):
    with ExitStack() as ctx:
        sb = lambda name, shape, dt=F32: ctx.enter_context(nc.sbuf_tensor(name, shape, dt))
        sem = ctx.enter_context(Semaphores(nc))
        wqk = sb("wqk", [DH, 2, 2 * QT, 128])
        bqk = sb("bqk", [128, 2 * QT])
        wv = sb("wv", [DH, 2, D])
        bv = sb("bv", [GT, D])
        wo = sb("wo", [DH, 2, D])
        bo = sb("bo", [DH, 2])
        cos_sin = sb("cos_sin", [128, 2, CT])
        xc = sb("at_xc", [DH, 2, N])
        sq = sb("at_sq", [DH, 2, N])
        xn = sb("at_xn", [DH, 2, N])
        xl = sb("at_chunk", [DH, 2, CT])
        biased_t = sb("qk_biased", [128, 2, CT])
        t1 = sb("rope_cos_part", [128, 2, CT])
        t2 = sb("rope_sin_part", [128, 2, CT])
        qm = sb("q_one_head", [128, HEADS, CT])
        kt = sb("k_heads", [128, QT, CT])
        va = sb("v_and_one", [GT, GC, HEADS, HD + 1])
        sm = sb("scores", [GT, 2, 4, GT])
        sx = sb("scores_less_max", [GT, 2, 4, GT])
        ex = sb("exps", [GT, 2, 4, GT])
        pt = sb("exps_turned", [GT, 2, 4, GT])
        mx = sb("score_max", [GT, 2, 4])
        rec = sb("inverse_sums", [GT, HEADS])
        cn = sb("context", [GT, HEADS, HD])
        cx = sb("context_turned", [DH, 2, CT])
        norm = Norm(nc, sb, sem, "at", consts, banks[0], banks[1], banks[2], LN_EPS)
        on_pe, on_dve, on_act = whole_norm(norm, stream, xc, sq, xn)
        landed = sem("at_weights_landed")
        zeroed = sem("at_zeroed")
        copied = sem("chunk_copied")
        projected = sem("qk_projected")
        biased = sem("qk_biased_done")
        turned = sem("qk_rotated")
        cos_done = sem("cos_done")
        sin_done = sem("sin_done")
        roped = sem("qk_roped")
        v_summed = sem("v_summed")
        v_stored = sem("v_stored")
        scored = sem("scored")
        masked = sem("scores_masked")
        maxed = sem("scores_maxed")
        lessened = sem("scores_lessened")
        exped = sem("scores_exped")
        exps_turned = sem("exps_turned_done")
        exps_stored = sem("exps_stored")
        mixed = sem("values_mixed")
        inverted = sem("sums_inverted")
        normed = sem("context_normed")
        ctx_turned = sem("context_turned_done")
        ctx_stored = sem("context_stored")
        out_summed = sem("out_summed")
        added = sem("attention_added")
        block = ctx.enter_context(nc.Block())
        U = QT * GC
        J = 2 * QT

        @block.sync
        def _(sp):
            for dst, src in ((wqk, qk_w), (bqk, qk_b), (wv, v_w), (bv, v_b), (wo, out_w), (bo, out_b), (cos_sin, rope)):
                sp.dma_start(dst[:], src).then_inc(landed, 16)

        @block.gpsimd
        def _(pool):
            pool.memset(qm[:], 0.0).then_inc(zeroed, 1)
            pool.memset(va[:], 1.0).then_inc(zeroed, 1)
            pool.wait_ge(landed, 16 * 7)
            with pool.Fori(0, NC) as c:
                for j in range(J):
                    pool.wait_ge(biased, J * c + j + 1)
                    if j >= 2:
                        pool.wait_ge(roped, J * c + j)
                    else:
                        pool.wait_ge(roped, J * c + 1)
                    pool.tensor_tensor(t1[:, j % 2], biased_t[:, j % 2], cos_sin[:, 0], ALU.mult).then_inc(cos_done, 1)
                for u in range(U):
                    b = u % 2
                    pool.wait_ge(maxed, U * c + u + 1)
                    pool.wait_ge(masked, U * c + u + 1)
                    if u >= 2:
                        pool.wait_ge(exped, U * c + u - 1)
                    pool.tensor_tensor(sx[:, b], sm[:, b], mx[:, b].unsqueeze(2).broadcast_to([GT, 4, GT]),
                                       ALU.subtract).then_inc(lessened, 1)

        @block.tensor
        def _(pe):
            start_at_one(pe, v_summed, mixed)
            on_pe(pe)
            pe.wait_ge(landed, 16 * 7)
            with pe.Fori(0, NC) as c:
                pe.wait_ge(copied, c + 1)
                pe.wait_ge(added, 2 * c + 1)

                def rotate(j):
                    pe.wait_ge(biased, J * c + j + 1)
                    if j >= 2:
                        pe.wait_ge(sin_done, J * c + j - 1)
                    pe.matmul(banks[2 + j % 2][:, 0:CT], consts["rotate"][:], biased_t[:, j % 2], start=True,
                              stop=True).then_inc(turned, 1)

                for j in range(J):
                    if j >= 2:
                        pe.wait_ge(biased, J * c + j - 1)
                    for k in range(2):
                        mm = pe.matmul(banks[j % 2][:, 0:CT], wqk[:, k, j], xl[:, k], start=(k == 0), stop=(k == 1))
                    mm.then_inc(projected, 1)
                    if j >= 1:
                        rotate(j - 1)
                rotate(J - 1)
                for g in range(GC):
                    for k in range(2):
                        mm = pe.matmul(banks[4 + g][0:GT, 0:D], xl[:, k, g * GT:(g + 1) * GT], wv[:, k],
                                       start=(k == 0), stop=(k == 1))
                    mm.then_inc(v_summed, 1)
                pe.wait_ge(roped, J * c + J + 1)
                pe.wait_ge(v_stored, GC * c + GC)

                def score(u):
                    g, j = divmod(u, QT)
                    if u >= 2:
                        pe.wait_ge(masked, U * c + u - 1)
                    for i in range(4):
                        mm = pe.matmul(banks[u % 2][0:GT, i * GT:(i + 1) * GT], qm[:, 4 * j + i, g * GT:(g + 1) * GT],
                                       kt[:, j, g * GT:(g + 1) * GT], start=True, stop=True)
                    mm.then_inc(scored, 1)

                def turn(u):
                    pe.wait_ge(exped, U * c + u + 1)
                    if u >= 2:
                        pe.wait_ge(exps_stored, U * c + u - 1)
                    for i in range(4):
                        mm = pe.transpose(banks[2 + u % 2][0:GT, i * GT:(i + 1) * GT], ex[:, u % 2, i], consts["ident"][0:GT, 0:GT])
                    mm.then_inc(exps_turned, 1)

                def mix(u):
                    g, j = divmod(u, QT)
                    pe.wait_ge(exps_stored, U * c + u + 1)
                    if j == 0 and g >= 1:
                        pe.wait_ge(normed, GC * c + g)
                    for i in range(4):
                        h = 4 * j + i
                        mm = pe.matmul(banks[6][0:GT, h * (HD + 1):(h + 1) * (HD + 1)], pt[:, u % 2, i], va[:, g, h],
                                       start=True, stop=True)
                    mm.then_inc(mixed, 1)

                def turn_context(g):
                    pe.wait_ge(normed, GC * c + g + 1)
                    if g >= 1:
                        pe.wait_ge(ctx_stored, GC * c + g)
                    for k in range(2):
                        mm = pe.transpose(banks[7][0:DH, k * GT:(k + 1) * GT],
                                          cn[:].rearrange("p h d -> p (h d)")[:, k * DH:(k + 1) * DH], consts["ident"][0:GT, 0:GT])
                    mm.then_inc(ctx_turned, 1)

                for u in range(U + 4):
                    if u < U:
                        score(u)
                    if 1 <= u <= U:
                        turn(u - 1)
                    if 2 <= u < U + 2:
                        mix(u - 2)
                    if u >= 5 and (u - 5) % QT == 0:
                        turn_context((u - 5) // QT)
                pe.wait_ge(ctx_stored, GC * c + GC)
                for m in range(2):
                    for k in range(2):
                        mm = pe.matmul(banks[4 + m][0:DH, 0:CT], wo[:, k, m * DH:(m + 1) * DH], cx[:, k], start=(k == 0), stop=(k == 1))
                    mm.then_inc(out_summed, 1)

        def store_context(act, c, g):
            act.wait_ge(ctx_turned, GC * c + g + 1)
            act.activation(cx[:, :, g * GT:(g + 1) * GT], banks[7][0:DH, 0:2 * GT].rearrange("p (k t) -> p k t", k=2),
                           ACT.Copy).then_inc(ctx_stored, 1)

        @block.scalar
        def _(act):
            on_act(act)
            act.wait_ge(landed, 16 * 7)
            act.wait_ge(norm.scaled, NC)
            with act.Fori(0, NC) as c:
                act.wait_ge(v_summed, GC * c + 1)
                act.activation(xl[:], chunk(xn, c), ACT.Copy).then_inc(copied, 1)
                for j in range(J):
                    act.wait_ge(projected, J * c + j + 1)
                    if j >= 2:
                        act.wait_ge(turned, J * c + j - 1)
                        act.wait_ge(cos_done, J * c + j - 1)
                    act.activation(biased_t[:, j % 2], banks[j % 2][:, 0:CT], ACT.Identity, bias=bqk[:, j:j + 1]).then_inc(biased, 1)
                for u in range(U + 4):
                    if u < U:
                        act.wait_ge(lessened, U * c + u + 1)
                        if u >= 2:
                            act.wait_ge(exps_turned, U * c + u - 1)
                        act.activation(ex[:, u % 2], sx[:, u % 2], ACT.Exp).then_inc(exped, 1)
                    if 1 <= u <= U:
                        v = u - 1
                        act.wait_ge(exps_turned, U * c + v + 1)
                        if v >= 2:
                            act.wait_ge(mixed, U * c + v)
                        act.activation(pt[:, v % 2].rearrange("p a b -> p (a b)"), banks[2 + v % 2][0:GT, 0:4 * GT], ACT.Copy).then_inc(exps_stored, 1)
                    if u >= 6 and (u - 6) % QT == 0:
                        store_context(act, c, (u - 6) // QT)

        @block.vector
        def _(dve):
            start_at_one(dve, roped, added)
            on_dve(dve)
            dve.wait_ge(landed, 16 * 7)
            dve.wait_ge(zeroed, 2)
            with dve.Fori(0, NC) as c:
                dve.wait_ge(mixed, U * c + 1)
                for j in range(J):
                    b = j % 2
                    dve.wait_ge(turned, J * c + j + 1)
                    dve.tensor_tensor(t2[:, b], banks[2 + b][:, 0:CT], cos_sin[:, 1], ALU.mult).then_inc(sin_done, 1)
                    dve.wait_ge(sin_done, J * c + j + 1)
                    dve.wait_ge(cos_done, J * c + j + 1)
                    if j < QT:
                        for i in range(4):
                            q = slice(32 * i, 32 * i + 32)
                            last = dve.tensor_tensor(qm[q, 4 * j + i], t1[q, b], t2[q, b], ALU.add)
                    else:
                        last = dve.tensor_tensor(kt[:, j - QT], t1[:, b], t2[:, b], ALU.add)
                    last.then_inc(roped, 1)
                for g in range(GC):
                    dve.wait_ge(v_summed, GC * c + g + 2)
                    dve.tensor_tensor(va[:, g, :, 0:HD], banks[4 + g][0:GT, 0:D].rearrange("p (h d) -> p h d", h=HEADS),
                                      bv[:].rearrange("p (h d) -> p h d", h=HEADS), ALU.add).then_inc(v_stored, 1)

                def norm_context(g):
                    dve.wait_ge(mixed, U * c + QT * (g + 1) + 1)
                    heads = banks[6][0:GT, 0:HEADS * (HD + 1)].rearrange("p (h d) -> p h d", h=HEADS)
                    dve.reciprocal(rec[:].unsqueeze(2), heads[:, :, HD:HD + 1]).then_inc(inverted, 1)
                    dve.wait_ge(inverted, GC * c + g + 1)
                    if g >= 1:
                        dve.wait_ge(ctx_turned, GC * c + g)
                    dve.tensor_tensor(cn[:], heads[:, :, 0:HD], rec[:].unsqueeze(2).broadcast_to([GT, HEADS, HD]),
                                      ALU.mult).then_inc(normed, 1)

                for u in range(U):
                    b = u % 2
                    dve.wait_ge(scored, U * c + u + 1)
                    if u >= 2:
                        dve.wait_ge(lessened, U * c + u - 1)
                    dve.scalar_tensor_tensor(sm[:, b], banks[b][0:GT, 0:4 * GT].rearrange("p (i t) -> p i t", i=4), HD ** -0.5,
                                             consts["mask"][:].unsqueeze(1).broadcast_to([GT, 4, GT]),
                                             ALU.mult, ALU.add).then_inc(masked, 1)
                    dve.wait_ge(masked, U * c + u + 1)
                    dve.tensor_reduce(mx[:, b], sm[:, b], AX.X, ALU.max).then_inc(maxed, 1)
                    if u >= 5 and (u - 5) % QT == 0:
                        norm_context((u - 5) // QT)
                for g in range((U - 1 - 5) // QT + 1, GC):
                    norm_context(g)
                for m in range(2):
                    dve.wait_ge(out_summed, 2 * c + m + 1)
                    half = stream[:, m, bass.ds(c * CT, CT)]
                    dve.scalar_tensor_tensor(half, banks[4 + m][0:DH, 0:CT], bo[:, m:m + 1], half, ALU.add, ALU.add).then_inc(added, 1)


def route(nc, tag, banks, consts, stream, xn, gate_w, gate_b, r, slots, tiles_of, capacity):
    with ExitStack() as ctx:
        sb = lambda name, shape, dt=F32: ctx.enter_context(nc.sbuf_tensor(f"{tag}_{name}", shape, dt))
        sem = ctx.enter_context(Semaphores(nc, tag + "_"))
        gw = sb("gate_w", [DH, 2, E])
        gb = sb("gate_b", [GT, E])
        lg = sb("logits", [GT, NG, E])
        top = sb("top_values", [GT, NG, 8])
        ti = sb("top_indices", [GT, NG, 8], U32)
        tf = sb("top_indices_f", [GT, NG, 2])
        is_k = [sb(f"is_expert{k}", [GT, NG, E]) for k in range(2)]
        chosen = sb("chosen", [GT, NG, E])
        less = sb("logits_less_max", [GT, NG, E])
        ex = sb("logit_exps", [GT, NG, E])
        sel = sb("chosen_exps", [GT, NG, E])
        total = sb("exp_total", [GT, NG])
        inv = sb("exp_total_inverse", [GT, NG])
        pre = [sb(f"group_prefix{u}", [GT, NG, E]) for u in range(2)]
        place = sb("place_in_expert", [GT, NG, E])
        slot = sb("slot_in_expert", [GT, NG, E])
        kept = sb("kept", [GT, NG, E])
        picked = [[sb(f"{what}_of_expert{k}", [GT, NG, E]) for k in range(2)] for what in ("slot", "kept", "exp")]
        slot_k = sb("slot_k", [GT, NG, 2])
        kept_k = sb("kept_k", [GT, NG, 2])
        exp_k = sb("exp_k", [GT, NG, 2])
        past = sb("slot_less_own_row", [GT, NG, 2])
        target_f = sb("target_f", [GT, NG, 2])
        source_f = sb("source_f", [GT, NG, 2])
        target = sb("scatter_rows", [GT, NG, 2], U32)
        if capacity is None:
            more = sb("tile_begun", [GT, E, NT])
            need = sb("tiles_needed", [GT, E])
            upto = [sb(f"tiles_upto{u}", [GT, E]) for u in range(2)]
            base = sb("expert_base", [GT, E])
            past_e = sb("tile_past_expert", [1, NT, E])
            tile_f = sb("tile_expert_f", [1, NT])
        else:
            sq = sb("row_squares", [GT, NG, D])
            ms = sb("row_square_sum", [GT, NG])
            root = sb("row_root", [GT, NG])
            rinv = sb("row_root_inverse", [GT, NG])
        landed = sem("gate_landed")
        logits_summed = sem("logits_summed")
        step = sem("routing_step")
        chosen_ready = sem("chosen_ready")
        counted = sem("chosen_counted")
        less_ready = sem("logits_less_max_ready")
        exped = sem("logits_exped")
        row_turned = sem("row_turned")
        row_stored = sem("row_stored")
        squared = sem("rows_squared")
        eps_added = sem("row_eps_added")
        rooted = sem("rows_rooted")
        scaled = sem("rows_scaled")
        targets_ready = sem("targets_ready")
        scattered = sem("rows_scattered")
        block = ctx.enter_context(nc.Block())
        last_of = lambda tile, k: tile[:, :, k:k + 1].broadcast_to([GT, NG, E])
        gated = capacity is not None

        @block.sync
        def _(sp):
            sp.dma_start(gw[:], gate_w).then_inc(landed, 16)
            if gate_b is not None:
                sp.dma_start(gb[:], gate_b).then_inc(landed, 16)

        all_landed = 16 if gate_b is None else 32

        @block.tensor
        def _(pe):
            pe.wait_ge(landed, all_landed)
            for g in range(NG):
                for k in range(2):
                    mm = pe.matmul(banks[0][0:GT, g * E:(g + 1) * E], xn[:, k, g * GT:(g + 1) * GT], gw[:, k], start=(k == 0), stop=(k == 1))
            mm.then_inc(logits_summed, 1)

            def turn(n):
                g = n % NG
                if n >= 4:
                    pe.wait_ge(row_stored, n - 3)
                for k in range(2):
                    mm = pe.transpose(banks[4 + n % 4][0:GT, k * DH:(k + 1) * DH], (xn if n < NG else stream)[:, k, g * GT:(g + 1) * GT],
                                      consts["ident"][0:DH, 0:DH])
                mm.then_inc(row_turned, 1)

            for n in range(NG):
                turn(n)
            pe.wait_ge(chosen_ready, 1)
            flat = chosen[:].rearrange("p g e -> p (g e)")
            pe.matmul(banks[1][0:GT, 0:NG * E], consts["before"][:], flat, start=True, stop=True)
            pe.matmul(banks[2][0:GT, 0:NG * E], consts["ones"][0:GT, 0:GT], flat, start=True, stop=True).then_inc(counted, 1)
            for n in range(NG, 2 * NG):
                turn(n)

        @block.scalar
        def _(act):
            for n in range(2 * NG):
                act.wait_ge(row_turned, n + 1)
                rows = r["x_rows"] if n < NG else r["stream_rows"]
                act.activation(rows[:, n % NG], banks[4 + n % 4][0:GT, 0:D], ACT.Copy).then_inc(row_stored, 1)
                if n == 7:
                    act.wait_ge(less_ready, 1)
                    act.activation(ex[:], less[:], ACT.Exp).then_inc(exped, 1)
                if n == NG - 1 and gated:
                    act.wait_ge(row_stored, NG)
                    act.activation(sq[:], r["x_rows"][:], ACT.Square).then_inc(squared, 1)
                if n == NG + 3 and gated:
                    act.wait_ge(eps_added, 1)
                    act.activation(root[:], ms[:], ACT.Sqrt).then_inc(rooted, 1)

        @block.vector
        def _(dve):
            steps = [0]

            def then(instruction):
                steps[0] += 1
                instruction.then_inc(step, 1)
                dve.wait_ge(step, steps[0])

            dve.wait_ge(landed, all_landed)
            dve.wait_ge(logits_summed, 1)
            summed = banks[0][0:GT, 0:NG * E].rearrange("p (g e) -> p g e", e=E)
            if gate_b is None:
                then(dve.tensor_copy(lg[:], summed))
            else:
                then(dve.tensor_tensor(lg[:], summed, gb[:].unsqueeze(1).broadcast_to([GT, NG, E]), ALU.add))
            for g in range(NG):
                last = dve.max(top[:, g], lg[:, g])
            then(last)
            dve.tensor_tensor(less[:], lg[:], last_of(top, 0), ALU.subtract).then_inc(less_ready, 1)
            for g in range(NG):
                last = dve.max_index(ti[:, g], top[:, g], lg[:, g])
            then(last)
            then(dve.tensor_copy(tf[:], ti[:, :, 0:2]))
            names = consts["counting"][:, 0:E].unsqueeze(1).broadcast_to([GT, NG, E])
            dve.tensor_tensor(is_k[0][:], names, last_of(tf, 0), ALU.is_equal)
            then(dve.tensor_tensor(is_k[1][:], names, last_of(tf, 1), ALU.is_equal))
            dve.tensor_tensor(chosen[:], is_k[0][:], is_k[1][:], ALU.add).then_inc(chosen_ready, 1)
            dve.wait_ge(chosen_ready, 1)
            dve.wait_ge(exped, 1)
            then(dve.tensor_tensor(sel[:], ex[:], chosen[:], ALU.mult))
            then(dve.tensor_reduce(total[:], (sel if gated else ex)[:], AX.X, ALU.add))
            then(dve.reciprocal(inv[:], total[:]))
            dve.wait_ge(counted, 1)
            totals = banks[2][0:GT, 0:NG * E].rearrange("p (g e) -> p g e", e=E)
            dve.memset(pre[0][:, 0:1], 0.0)
            then(dve.tensor_copy(pre[0][:, 1:NG], totals[:, 0:NG - 1]))
            shift, u = 1, 0
            while shift < NG:
                dve.tensor_copy(pre[1 - u][:, 0:shift], pre[u][:, 0:shift])
                then(dve.tensor_tensor(pre[1 - u][:, shift:NG], pre[u][:, shift:NG], pre[u][:, 0:NG - shift], ALU.add))
                shift, u = 2 * shift, 1 - u
            within = banks[1][0:GT, 0:NG * E].rearrange("p (g e) -> p g e", e=E)
            then(dve.tensor_tensor(place[:], pre[u][:], within, ALU.add))
            if gated:
                then(dve.tensor_scalar(kept[:], place[:], float(capacity), None, ALU.is_lt))
                starts = consts["expert_starts"][:].unsqueeze(1)
            else:
                then(dve.tensor_tensor(base[:].unsqueeze(1), pre[u][:, NG - 1:NG], totals[:, NG - 1:NG], ALU.add))
                then(dve.tensor_tensor(more[:], base[:].unsqueeze(2).broadcast_to([GT, E, NT]),
                                       consts["tile_starts"][:].unsqueeze(1).broadcast_to([GT, E, NT]), ALU.is_gt))
                then(dve.tensor_reduce(need[:], more[:], AX.X, ALU.add))
                then(dve.tensor_copy(upto[0][:], need[:]))
                shift, u = 1, 0
                while shift < E:
                    dve.tensor_copy(upto[1 - u][:, 0:shift], upto[u][:, 0:shift])
                    then(dve.tensor_tensor(upto[1 - u][:, shift:E], upto[u][:, shift:E], upto[u][:, 0:E - shift], ALU.add))
                    shift, u = 2 * shift, 1 - u
                dve.tensor_tensor(past_e[:], upto[u][0:1].unsqueeze(1).broadcast_to([1, NT, E]),
                                  consts["counting"][0:1].unsqueeze(2).broadcast_to([1, NT, E]), ALU.is_le)
                then(dve.tensor_tensor(need[:], upto[u][:], need[:], ALU.subtract))
                dve.tensor_reduce(tile_f[:], past_e[:], AX.X, ALU.add)
                then(dve.tensor_scalar(base[:], need[:], float(TS), None, ALU.mult))
                then(dve.tensor_scalar(tile_f[:], tile_f[:], float(E - 1), None, ALU.min))
                dve.tensor_copy(tiles_of[:], tile_f[:])
                starts = base[:].unsqueeze(1)
            then(dve.tensor_tensor(slot[:], place[:], starts.broadcast_to([GT, NG, E]), ALU.add))
            for k in range(2):
                dve.tensor_tensor(picked[0][k][:], slot[:], is_k[k][:], ALU.mult)
                if gated:
                    dve.tensor_tensor(picked[1][k][:], kept[:], is_k[k][:], ALU.mult)
                last = dve.tensor_tensor(picked[2][k][:], sel[:], is_k[k][:], ALU.mult)
            then(last)
            for k in range(2):
                dve.tensor_reduce(slot_k[:, :, k], picked[0][k][:], AX.X, ALU.add)
                if gated:
                    dve.tensor_reduce(kept_k[:, :, k], picked[1][k][:], AX.X, ALU.add)
                last = dve.tensor_reduce(exp_k[:, :, k], picked[2][k][:], AX.X, ALU.add)
            then(last)
            if gated:
                then(dve.tensor_tensor(past[:], slot_k[:], consts["own_rows"][:], ALU.subtract))
                then(dve.tensor_tensor(past[:], past[:], kept_k[:], ALU.mult))
                dve.tensor_tensor(target_f[:], past[:], consts["own_rows"][:], ALU.add)
                then(dve.tensor_tensor(source_f[:], slot_k[:], kept_k[:], ALU.mult))
                then(dve.tensor_copy(target[:], target_f[:]))
                dve.tensor_copy(r["source"][:], source_f[:])
                then(dve.tensor_tensor(exp_k[:], exp_k[:], kept_k[:], ALU.mult))
            else:
                dve.tensor_copy(r["source"][:], slot_k[:])
                then(dve.tensor_copy(target[:], slot_k[:]))
            then(dve.tensor_tensor(r["weights"][:], exp_k[:], inv[:].unsqueeze(2).broadcast_to([GT, NG, 2]), ALU.mult))
            if gated:
                then(dve.tensor_tensor(r["weight_sum"][:].unsqueeze(2), r["weights"][:, :, 0:1], r["weights"][:, :, 1:2], ALU.add))
                dve.wait_ge(squared, 1)
                then(dve.tensor_reduce(ms[:], sq[:], AX.X, ALU.add))
                dve.tensor_scalar(ms[:], ms[:], 4.0 / D, RMS_EPS, ALU.mult, ALU.add).then_inc(eps_added, 1)
                dve.wait_ge(rooted, 1)
                then(dve.reciprocal(rinv[:], root[:]))
                then(dve.tensor_scalar(rinv[:], rinv[:], 2.0, None, ALU.mult))
                for q in range(NC):
                    gs = slice(q * GC, (q + 1) * GC)
                    last = dve.tensor_tensor(sq[:, gs], r["x_rows"][:, gs], rinv[:, gs].unsqueeze(2).broadcast_to([GT, GC, D]), ALU.mult)
                    last.then_inc(scaled, 1)
            dve.wait_ge(step, steps[0])
            dve.sem_inc(targets_ready, 1)

        @block.gpsimd
        def _(pool):
            pool.wait_ge(targets_ready, 1)
            pool.wait_ge(row_stored, NG)
            for g in range(NG):
                if gated and g % GC == 0:
                    pool.wait_ge(scaled, g // GC + 1)
                for k in range(2):
                    pool.indirect_dma_start(slots, bass.IndirectOffsetOnAxis(target[:, g, k:k + 1], 0),
                                            (sq if gated else r["x_rows"])[:, g], None).then_inc(scattered, 16)
            pool.wait_ge(scattered, 16 * 2 * NG)


def gated_experts(nc, banks, consts, slots, results, w_in, w_out, norm_w):
    CG = CAP // SP
    tiles = H0 // 128
    with ExitStack() as ctx:
        sb = lambda name, shape, dt=F32: ctx.enter_context(nc.sbuf_tensor(f"moe0_{name}", shape, dt))
        sem = ctx.enter_context(Semaphores(nc, "moe0_"))
        wi = [sb(f"expert_in{u}", [DH, 2, 2 * H0]) for u in range(2)]
        wo = [sb(f"expert_out{u}", [128, tiles, D]) for u in range(2)]
        nw = sb("expert_norms", [DH, E, 2])
        rows = [sb(f"slot_rows{u}", [SP, CG, D]) for u in range(2)]
        xt = [sb(f"slot_inputs{u}", [DH, 2, CAP]) for u in range(2)]
        silu = sb("gate_silu", [128, 2, CAP])
        hid = [sb(f"expert_hidden{u}", [128, tiles, CAP]) for u in range(2)]
        ys = [sb(f"expert_results{u}", [SP, CG, D]) for u in range(2)]
        norms_landed = sem("expert_norms_landed")
        w_landed = [sem(f"expert{u}_landed") for u in range(2)]
        rows_landed = [sem(f"slot_rows{u}_landed") for u in range(2)]
        turned, inputs_ready = sem("slots_turned"), sem("slot_inputs_ready")
        first_summed, silued, hid_ready = sem("hidden_summed"), sem("gate_silued"), sem("hidden_ready")
        second_summed = sem("results_summed")
        results_stored = sem("results_stored")
        written = [sem(f"results{u}_written") for u in range(2)]
        block = ctx.enter_context(nc.Block())
        PG = 2
        R = CG // PG
        rows_of = lambda ap, e: ap[e * CAP:(e + 1) * CAP].rearrange("(g p) d -> p g d", p=SP)

        @block.sync
        def _(sp):
            sp.dma_start(nw[:], norm_w).then_inc(norms_landed, 16)
            for e in range(E):
                u = e % 2
                if e >= 2:
                    sp.wait_ge(second_summed, R * (e - 1))
                sp.dma_start(rows[u][:], rows_of(slots, e)).then_inc(rows_landed[u], 16)
                sp.dma_start(wi[u][:], w_in[e]).then_inc(w_landed[u], 16)
                sp.dma_start(wo[u][:], w_out[e]).then_inc(w_landed[u], 16)

        @block.tensor
        def _(pe):
            def turn(e):
                pe.wait_ge(rows_landed[e % 2], 16 * (e // 2 + 1))
                for k in range(2):
                    if e >= 1:
                        pe.wait_ge(inputs_ready, 2 * (e - 1) + k + 1)
                    for g in range(CG):
                        mm = pe.transpose(banks[4 + k][0:DH, g * SP:(g + 1) * SP], rows[e % 2][:, g, k * DH:(k + 1) * DH],
                                          consts["ident"][0:SP, 0:SP])
                    mm.then_inc(turned, 1)

            def second(e, r):
                if r == 0:
                    pe.wait_ge(hid_ready, tiles * (e + 1))
                if R * e + r >= 2:
                    pe.wait_ge(results_stored, R * e + r - 1)
                for g in range(r * PG, (r + 1) * PG):
                    for h in range(tiles):
                        mm = pe.matmul(banks[6 + r % 2][0:SP, (g % PG) * D:(g % PG + 1) * D], hid[e % 2][:, h, g * SP:(g + 1) * SP],
                                       wo[e % 2][:, h], start=(h == 0), stop=(h == tiles - 1))
                mm.then_inc(second_summed, 1)

            turn(0)
            for e in range(E):
                pe.wait_ge(inputs_ready, 2 * e + 2)
                pe.wait_ge(w_landed[e % 2], 32 * (e // 2 + 1))
                for h in range(tiles):
                    n = e * tiles + h
                    if n >= 2:
                        pe.wait_ge(hid_ready, n - 1)
                    for part in range(2):
                        o = part * H0 + h * 128
                        for k in range(2):
                            mm = pe.matmul(banks[2 * (n % 2) + part][:, 0:CAP], wi[e % 2][:, k, o:o + 128], xt[e % 2][:, k],
                                           start=(k == 0), stop=(k == 1))
                    mm.then_inc(first_summed, 1)
                    if h == 1 and e >= 1:
                        for r in range(R):
                            second(e - 1, r)
                if e + 1 < E:
                    turn(e + 1)
            for r in range(R):
                second(E - 1, r)

        @block.scalar
        def _(act):
            def inputs(e):
                for k in range(2):
                    act.wait_ge(turned, 2 * e + k + 1)
                    act.activation(xt[e % 2][:, k], banks[4 + k][0:DH, 0:CAP], ACT.Copy, scale=nw[:, e, k:k + 1]).then_inc(inputs_ready, 1)

            act.wait_ge(norms_landed, 16)
            inputs(0)
            for e in range(E):
                for h in range(tiles):
                    n = e * tiles + h
                    act.wait_ge(first_summed, n + 1)
                    if n >= 2:
                        act.wait_ge(hid_ready, n - 1)
                    act.activation(silu[:, n % 2], banks[2 * (n % 2)][:, 0:CAP], ACT.Silu).then_inc(silued, 1)
                if e + 1 < E:
                    inputs(e + 1)

        @block.vector
        def _(dve):
            def keep(e, r):
                dve.wait_ge(second_summed, R * e + r + 1)
                if e >= 2 and r == 0:
                    dve.wait_ge(written[e % 2], 16 * (e // 2))
                dve.tensor_copy(ys[e % 2][:, r * PG:(r + 1) * PG], banks[6 + r % 2][0:SP, 0:PG * D].rearrange("p (g d) -> p g d", g=PG)).then_inc(results_stored, 1)

            for e in range(E):
                for h in range(tiles):
                    n = e * tiles + h
                    if h == 0 and e >= 2:
                        dve.wait_ge(second_summed, R * (e - 1))
                    dve.wait_ge(silued, n + 1)
                    dve.tensor_tensor(hid[e % 2][:, h], silu[:, n % 2], banks[2 * (n % 2) + 1][:, 0:CAP], ALU.mult).then_inc(hid_ready, 1)
                    if h == 2 and e >= 1:
                        for r in range(R):
                            keep(e - 1, r)
            for r in range(R):
                keep(E - 1, r)

        @block.gpsimd
        def _(pool):
            for e in range(E):
                pool.wait_ge(results_stored, R * (e + 1))
                pool.dma_start(rows_of(results, e), ys[e % 2][:]).then_inc(written[e % 2], 16)
            for u in range(2):
                pool.wait_ge(written[u], 16 * E // 2)


def over_tiles(eng, body):
    for t in range(2):
        body(t, t, 0)
    with eng.Fori(0, NT // 2 - 2) as i:
        for u in range(2):
            body(2 * i + 2 + u, u, i + 1)
    for t in range(NT - 2, NT):
        body(t, t % 2, t // 2)


def load_experts(nc, w, landed, w_in, b_in, w_out, b_out):
    with nc.Block() as block:
        @block.sync
        def _(sp):
            for dst, src in ((w["in"], w_in), (w["b_in"], b_in), (w["out"], w_out), (w["b_out"], b_out)):
                sp.dma_start(dst[:], src).then_inc(landed, 16)


def tiled_experts(nc, banks, consts, slots, results, tiles_of, w, weights_landed):
    tiles = H1 // 128
    with ExitStack() as ctx:
        sb = lambda name, shape, dt=F32: ctx.enter_context(nc.sbuf_tensor(f"moe1_{name}", shape, dt))
        sem = ctx.enter_context(Semaphores(nc, "moe1_"))
        two = lambda name, shape: [sb(f"{name}{u}", shape) for u in range(2)]
        wi = two("tile_in", [DH, 2, H1])
        bi = two("tile_b_in", [128, tiles])
        wo = two("tile_out", [128, tiles, D])
        rows, xt = two("slot_rows", [TS, D]), two("slot_inputs", [DH, 2, TS])
        hid, ys = two("tile_hidden", [128, tiles, TS]), two("tile_results", [TS, D])
        rows_landed = [sem(f"slot_rows{u}_landed") for u in range(2)]
        turned, inputs_ready = sem("slots_turned"), sem("slot_inputs_ready")
        in_staged, out_staged = sem("in_weights_staged"), sem("out_weights_staged")
        first_summed, hid_ready = sem("hidden_summed"), sem("hidden_ready")
        second_summed, results_stored = sem("results_summed"), sem("results_stored")
        written = [sem(f"results{u}_written") for u in range(2)]
        block = ctx.enter_context(nc.Block())
        FIRST = 4
        known = lambda t: isinstance(t, int)
        is_last = lambda t: known(t) and t == NT - 1

        @block.sync
        def _(sp):
            def load(t, u):
                sp.dma_start(rows[u][:], slots[bass.ds(t * TS, TS)]).then_inc(rows_landed[u], 16)

            def write(t, u):
                sp.wait_ge(results_stored, t + 2)
                sp.dma_start(results[bass.ds(t * TS, TS)], ys[u][:]).then_inc(written[u], 16)

            def body(t, u, half):
                if not is_last(t):
                    if not (known(t) and t < 1):
                        sp.wait_ge(turned, t)
                    load(t + 1, 1 - u)
                if not (known(t) and t < 1):
                    write(t - 1, 1 - u)

            load(0, 0)
            over_tiles(sp, body)
            write(NT - 1, (NT - 1) % 2)
            for u in range(2):
                sp.wait_ge(written[u], 16 * NT // 2)

        @block.tensor
        def _(pe):
            start_at_one(pe, second_summed)

            def turn(t, u, half):
                pe.wait_ge(rows_landed[u], 16 * half + 16)
                if not (known(t) and t < 2):
                    pe.wait_ge(inputs_ready, t - 1)
                for k in range(2):
                    mm = pe.transpose(banks[4 + u][0:DH, k * TS:(k + 1) * TS], rows[u][:, k * DH:(k + 1) * DH], consts["ident"][:])
                mm.then_inc(turned, 1)

            def second(t, u):
                pe.wait_ge(hid_ready, 2 * t + 2)
                pe.wait_ge(out_staged, t + 1)
                if not (known(t) and t < 2):
                    pe.wait_ge(results_stored, t)
                for h in range(tiles):
                    mm = pe.matmul(banks[6 + u][:, 0:D], hid[u][:, h], wo[u][:, h], start=(h == 0), stop=(h == tiles - 1))
                mm.then_inc(second_summed, 1)

            def body(t, u, half):
                pe.wait_ge(inputs_ready, t + 1)
                pe.wait_ge(in_staged, t + 1)
                if not (known(t) and t < 2):
                    pe.wait_ge(hid_ready, 2 * t - 2)
                for h in range(tiles):
                    for k in range(2):
                        mm = pe.matmul(banks[2 * u + h // FIRST][:, h % FIRST * TS:(h % FIRST + 1) * TS], wi[u][:, k, h * 128:(h + 1) * 128],
                                       xt[u][:, k], start=(k == 0), stop=(k == 1))
                    if h in (FIRST - 1, tiles - 1):
                        mm.then_inc(first_summed, 1)
                if not is_last(t):
                    turn(t + 1, 1 - u, half + u)
                if not (known(t) and t < 1):
                    second(t - 1, 1 - u)

            turn(0, 0, 0)
            over_tiles(pe, body)
            second(NT - 1, (NT - 1) % 2)

        @block.scalar
        def _(act):
            def inputs(t, u):
                act.wait_ge(turned, t + 1)
                act.activation(xt[u][:].rearrange("p k t -> p (k t)"), banks[4 + u][0:DH, 0:2 * TS], ACT.Copy).then_inc(inputs_ready, 1)

            def body(t, u, half):
                for part, hs in enumerate((range(FIRST), range(FIRST, tiles))):
                    act.wait_ge(first_summed, 2 * t + part + 1)
                    if part == 0 and not (known(t) and t < 2):
                        act.wait_ge(second_summed, t)
                    for h in hs:
                        last = act.activation(hid[u][:, h], banks[2 * u + part][:, h % FIRST * TS:(h % FIRST + 1) * TS], ACT.Gelu, bias=bi[u][:, h:h + 1])
                    last.then_inc(hid_ready, 1)
                if not is_last(t):
                    inputs(t + 1, 1 - u)

            inputs(0, 0)
            over_tiles(act, body)

        @block.vector
        def _(dve):
            start_at_one(dve, results_stored)

            def expert_of(t):
                return dve.value_load(tiles_of[0:1, bass.ds(t, 1)], min_val=0, max_val=E - 1)

            def stage_in(t, u, e):
                if not (known(t) and t < 2):
                    dve.wait_ge(first_summed, 2 * t - 2)
                    dve.wait_ge(hid_ready, 2 * t - 2)
                dve.tensor_scalar(bi[u][:].unsqueeze(1), w["b_in"][:, bass.ds(e, 1)], 1.0, None, ALU.mult)
                dve.tensor_scalar(wi[u][:].unsqueeze(1), w["in"][:, bass.ds(e, 1)], 1.0, None, ALU.mult).then_inc(in_staged, 1)

            def stage_out(t, u, e):
                if not (known(t) and t < 2):
                    dve.wait_ge(second_summed, t)
                dve.tensor_scalar(wo[u][:].unsqueeze(1), w["out"][:, bass.ds(e, 1)], 1.0, None, ALU.mult).then_inc(out_staged, 1)

            def keep(t, u, half):
                e = expert_of(t)
                dve.wait_ge(second_summed, t + 2)
                if not (known(t) and t < 2):
                    dve.wait_ge(written[u], 16 * half)
                dve.tensor_tensor(ys[u][:].unsqueeze(1), banks[6 + u][:, 0:D].unsqueeze(1), w["b_out"][:, bass.ds(e, 1)], ALU.add).then_inc(results_stored, 1)

            def body(t, u, half):
                if not is_last(t):
                    e = expert_of(t + 1)
                    stage_in(t + 1, 1 - u, e)
                if not (known(t) and t < 1):
                    keep(t - 1, 1 - u, half if u else half - 1)
                if not is_last(t):
                    stage_out(t + 1, 1 - u, e)

            dve.wait_ge(weights_landed, 16 * 4)
            e = expert_of(0)
            stage_in(0, 0, e)
            stage_out(0, 0, e)
            over_tiles(dve, body)
            keep(NT - 1, (NT - 1) % 2, (NT - 1) // 2)


def combine(nc, tag, banks, consts, stream, r, results, out=None):
    with ExitStack() as ctx:
        sb = lambda name, shape, dt=F32: ctx.enter_context(nc.sbuf_tensor(f"{tag}_{name}", shape, dt))
        sem = ctx.enter_context(Semaphores(nc, tag + "_"))
        got = sb("gathered", [GT, NG, 2, D])
        gathered = [[sem(f"gathered{k}_{g}") for k in range(2)] for g in range(NG)]
        step = sem("combine_step")
        combined = sem("rows_combined")
        turned = sem("combined_turned")
        written = sem("out_written")
        block = ctx.enter_context(nc.Block())

        @block.gpsimd
        def _(pool):
            for g in range(NG):
                for k in range(2):
                    pool.indirect_dma_start(got[:, g, k], None, results, bass.IndirectOffsetOnAxis(r["source"][:, g, k:k + 1], 0)).then_inc(gathered[g][k], 16)

        @block.vector
        def _(dve):
            steps = 0
            for g in range(NG):
                rows = r["stream_rows"][:, g]
                if "weight_sum" in r:
                    dve.scalar_tensor_tensor(rows, r["x_rows"][:, g], r["weight_sum"][:, g:g + 1], rows, ALU.mult, ALU.add).then_inc(step, 1)
                    steps += 1
                    dve.wait_ge(step, steps)
                for k in range(2):
                    dve.wait_ge(gathered[g][k], 16)
                    last = dve.scalar_tensor_tensor(rows, got[:, g, k], r["weights"][:, g, k:k + 1], rows, ALU.mult, ALU.add)
                    if k == 0:
                        last.then_inc(step, 1)
                        steps += 1
                        dve.wait_ge(step, steps)
                last.then_inc(combined, 1)

        if out is None:
            @block.tensor
            def _(pe):
                for g in range(NG):
                    pe.wait_ge(combined, g + 1)
                    for k in range(2):
                        mm = pe.transpose(banks[g // GC + 4 * k][0:DH, (g % GC) * GT:(g % GC + 1) * GT],
                                          r["stream_rows"][:, g, k * DH:(k + 1) * DH], consts["ident"][0:GT, 0:GT])
                    mm.then_inc(turned, 1)

            @block.scalar
            def _(act):
                for c in range(NC):
                    act.wait_ge(turned, GC * (c + 1))
                    for k in range(2):
                        act.activation(stream[:, k, c * CT:(c + 1) * CT], banks[c + 4 * k][0:DH, 0:CT], ACT.Copy)
        else:
            @block.sync
            def _(sp):
                for q in range(NC):
                    sp.wait_ge(combined, GC * (q + 1))
                    sp.dma_start(out.rearrange("b t d -> (b t) d").rearrange("(g p) d -> p g d", p=GT)[:, q * GC:(q + 1) * GC],
                                 r["stream_rows"][:, q * GC:(q + 1) * GC]).then_inc(written, 16)
                sp.wait_ge(written, 16 * NC)


def state_space(nc, banks, consts, resid, params_in, params_conv, dt_w, params_out, a_log):
    with ExitStack() as ctx:
        sb = lambda name, shape, dt=F32: ctx.enter_context(nc.sbuf_tensor(name, shape, dt))
        sem = ctx.enter_context(Semaphores(nc))
        in_p = sb("layer_in", [DH, 2 * 2 * DI + 4])
        in_w = in_p[:, 0:4 * DI].rearrange("p (k e) -> p k e", k=2)
        norm_w, norm_b = in_p[:, 4 * DI:4 * DI + 2], in_p[:, 4 * DI + 2:4 * DI + 4]
        conv_p = sb("layer_conv", [128, DT3 * (DCONV + 2 + 2 * DS + DTR)])
        o = DT3 * DCONV
        conv_w = conv_p[:, 0:o].rearrange("p (d k) -> p d k", d=DT3)
        conv_b, dt_b = conv_p[:, o:o + DT3], conv_p[:, o + DT3:o + 2 * DT3]
        x_w = conv_p[:, o + 2 * DT3:].rearrange("p (d e) -> p d e", d=DT3)
        dtw = sb("layer_dt_w", [64, DI])
        out_p = sb("layer_out", [128, DT3 * (1 + D)])
        skip, out_w = out_p[:, 0:DT3], out_p[:, DT3:].rearrange("p (d e) -> p d e", d=DT3)
        a_exp = sb("a_exp_layers", [128, LAYERS, DT3 * DS])
        a_neg = sb("a_neg", [128, DT3 * DS])
        xc = sb("ss_xc", [DH, 2, CT])
        sq = sb("ss_sq", [DH, 2, CT])
        xn = sb("ss_xn", [DH, 2, CT])
        un = sb("ss_un", [DH, 2, CT])
        padded = sb("conv_in", [128, DT3, CB, T + DCONV - 1])
        conv = sb("conv_sum", [128, DT3, CT])
        xa = sb("conv_silu", [128, 2, DT3, CT])
        zs = sb("gate_silu_z", [128, 2, DT3, CT])
        dtr = sb("dt_low_rank", [64, CT])
        rest = sb("bc_rest", [2 * DS, CT])
        mid = sb("bc_mid", [2 * DS, CT], BF16)
        bc = sb("bc_parts", [3 * 2 * DS, 2, CT], BF16)
        xb = sb("dt_in", [128, DT3, CT])
        eb = sb("dt_exp", [128, DT3, CT])
        ub = conv
        lost = sb("dt_rounding", [128, DT3, CT])
        dt = sb("dt", [128, 2, DT3, CT])
        dtx = sb("dt_x", [128, 2, DT3, CT])
        DEEP = 4
        da = sb("decay", [128, DEEP, DT3, CB, T])
        dbx = sb("state_in", [128, DEEP, DT3 * CT])
        hs = sb("states", [128, DEEP, DT3 * CT])
        cs = sb("c_repeated", [128, DEEP, CT])
        prod = sb("c_states", [128, DEEP, DT3 * CT])
        yg = sb("y", [128, DT3, CT])
        norm = Norm(nc, sb, sem, "ss", consts, banks[6], banks[7], banks[6], LN_EPS)
        in_landed = sem("layer_in_landed")
        out_landed = sem("layer_out_landed")
        a_landed = sem("a_landed")
        a_exped = sem("a_exped")
        a_ready = sem("a_ready")
        zeroed = sem("ss_zeroed")
        affined = sem("norm_affined")
        in_summed = sem("in_summed")
        in_stored = sem("in_stored")
        tap0 = sem("conv_tap0")
        tapped = sem("conv_tapped")
        conv_silued = sem("conv_silued")
        z_silued = sem("z_silued")
        x_summed = sem("x_proj_summed")
        dtr_stored = sem("dt_low_rank_stored")
        bc_step = sem("bc_step")
        bc_mid_stored = sem("bc_mid_stored")
        dt_summed = sem("dt_summed")
        dt_stored = sem("dt_in_stored")
        dt_absed = sem("dt_absed")
        dt_exped = sem("dt_exped")
        dt_one = sem("dt_plus_one")
        dt_lost = sem("dt_rounding_ready")
        dt_logged = sem("dt_logged")
        dt_fixed = sem("dt_log_fixed")
        dt_ready = sem("dt_ready")
        dtx_ready = sem("dtx_ready")
        b_spread = sem("b_spread")
        c_spread = sem("c_spread")
        c_stored = sem("c_stored")
        decayed = sem("decay_ready")
        fed = sem("state_in_ready")
        scanned = sem("scanned")
        produced = sem("c_states_ready")
        reduced = sem("c_states_summed")
        skipped = sem("y_skip_ready")
        gated = sem("y_gated_ready")
        out_summed = sem("mixer_summed")
        added = sem("mixer_added")
        block = ctx.enter_context(nc.Block())
        LAG = 3
        Z = 2 * DT3

        def all_chunks(eng, chunk_program):
            chunk_program(0, 0, 0)
            with eng.Fori(0, LAYERS - 1) as l:
                for c in range(1, NC):
                    chunk_program(NC * l + c, l, c)
                chunk_program(NC * l + NC, l + 1, 0)
            for c in range(1, NC):
                chunk_program(NC * (LAYERS - 1) + c, LAYERS - 1, c)

        def is_first(n):
            return isinstance(n, int) and n == 0

        def is_early(n):
            return isinstance(n, int) and n <= 1

        def is_last(n):
            return isinstance(n, int) and n == NC * LAYERS - 1

        @block.sync
        def _(sp):
            sp.dma_start(in_p[:], params_in[0]).then_inc(in_landed, 16)
            sp.dma_start(conv_p[:], params_conv[0]).then_inc(in_landed, 16)
            sp.dma_start(dtw[2 * DS:2 * DS + DTR, :], dt_w[0]).then_inc(in_landed, 16)
            sp.dma_start(a_exp[:], a_log).then_inc(a_landed, 16)
            sp.dma_start(out_p[:], params_out[0]).then_inc(out_landed, 16)
            with sp.Fori(1, LAYERS) as l:
                layer = lambda w: w[bass.ds(l, 1)].rearrange("a p c -> (a p) c")
                sp.wait_ge(dt_stored, DT3 * NC * l + 1)
                sp.dma_start(in_p[:], layer(params_in)).then_inc(in_landed, 16)
                sp.dma_start(conv_p[:], layer(params_conv)).then_inc(in_landed, 16)
                sp.dma_start(dtw[2 * DS:2 * DS + DTR, :], layer(dt_w)).then_inc(in_landed, 16)
                sp.wait_ge(added, NC * l + 1)
                sp.dma_start(out_p[:], layer(params_out)).then_inc(out_landed, 16)

        @block.tensor
        def _(pe):
            start_at_one(pe, dt_summed, in_summed, out_summed, reduced)

            def project_in(n, l, m):
                if m == 0:
                    pe.wait_ge(in_landed, 48 * l + 48)
                    pe.wait_ge(affined, n + 1)
                if m >= 2:
                    pe.wait_ge(in_stored, Z * n + m - 1)
                for k in range(2):
                    mm = pe.matmul(banks[6 + m % 2][:, 0:CT], in_w[:, k, m * 128:(m + 1) * 128], un[:, k], start=(k == 0), stop=(k == 1))
                mm.then_inc(in_summed, 1)

            def project_x(n, c):
                pe.wait_ge(in_stored, Z * n + Z)
                pe.wait_ge(conv_silued, n + 1)
                for d in range(DT3):
                    mm = pe.matmul(banks[6][0:2 * DS + DTR, 0:CT], x_w[:, d], xa[:, c % 2, d], start=(d == 0), stop=(d == DT3 - 1))
                mm.then_inc(x_summed, 1)

            def project_dt(n, d):
                if d == 0:
                    pe.wait_ge(dtr_stored, n + 1)
                if d == 1:
                    pe.wait_ge(bc_step, 4 * n + 2)
                if d == 2:
                    pe.wait_ge(dt_stored, DT3 * n + 2)
                low = slice(2 * DS, 2 * DS + DTR)
                pe.matmul(banks[7 - d % 2][:, 0:CT], dtw[low, d * 128:(d + 1) * 128], dtr[low, :], start=True,
                          stop=True).then_inc(dt_summed, 1)

            def start(n, l, c, s):
                if s == 0:
                    pe.wait_ge(dt_stored, DT3 * n + 1)
                    if not is_early(n):
                        pe.wait_ge(added, n - 1)
                    norm.pe_mean(pe, chunk(resid, c))
                elif s == 2:
                    norm.pe_square(pe, n, sq)
                elif s == 4:
                    norm.pe_spread(pe, n)
                elif s in (6, 7, 8):
                    project_in(n, l, 2 * (s - 6))
                    project_in(n, l, 2 * (s - 6) + 1)
                elif s == 11:
                    project_x(n, c)
                elif s == 12:
                    for d in range(DT3):
                        project_dt(n, d)

            def project_out(n, l):
                pe.wait_ge(gated, n + 1)
                pe.wait_ge(out_landed, 16 * l + 16)
                if is_last(n) or is_last(n + 1):
                    pe.wait_ge(added, n + 1)
                else:
                    pe.wait_ge(dt_stored, DT3 * (n + 3) + 1)
                for k in range(2):
                    for d in range(DT3):
                        mm = pe.matmul(banks[6 + k][0:DH, 0:CT], out_w[:, d, k * DH:(k + 1) * DH], yg[:, d], start=(d == 0), stop=(d == DT3 - 1))
                mm.then_inc(out_summed, 1)

            def spread_b(n, c, s):
                if s == 0:
                    pe.wait_ge(bc_step, 4 * n + 4)
                    pe.wait_ge(bc_mid_stored, n + 1)
                if not (is_first(n) and s < 2):
                    pe.wait_ge(fed, DS * n + s - 1)
                pe.matmul(banks[3 + s % 2][:, 0:CT], consts["spread"][:, s], bc[:, c % 2], start=True, stop=True).then_inc(b_spread, 1)

            def spread_c(n, c, s):
                if not (is_first(n) and s == 0):
                    pe.wait_ge(c_stored, DS * n + s)
                pe.matmul(banks[5][:, 0:CT], consts["spread"][:, DS + s], bc[:, c % 2], start=True, stop=True).then_inc(c_spread, 1)

            def reduce(n, s):
                if s == 0:
                    pe.wait_ge(skipped, DT3 * n + 1)
                pe.wait_ge(produced, DS * n + s + 1)
                for d in range(DT3):
                    mm = pe.matmul(banks[d][:, 0:CT], consts["ident"][:], prod[:, s % DEEP, d * CT:(d + 1) * CT],
                                   start=(s == 0), stop=(s == DS - 1))
                mm.then_inc(reduced, 1)

            def states(n, l, c):
                for s in range(DS):
                    if s + 1 < DS:
                        spread_b(n, c, s + 1)
                    elif not is_last(n):
                        spread_b(n + 1, c + 1, 0)
                    spread_c(n, c, s)
                    if s >= LAG:
                        reduce(n, s - LAG)
                    elif not is_first(n):
                        reduce(n - 1, DS - LAG + s)
                    if not is_last(n):
                        start(n + 1, l + (c + 1) // NC, (c + 1) % NC, s)
                    if s == 14 and not is_first(n):
                        project_out(n - 1, l if c else l - 1)

            for s in range(DS):
                start(0, 0, 0, s)
            spread_b(0, 0, 0)
            all_chunks(pe, states)
            last = NC * LAYERS - 1
            for s in range(DS - LAG, DS):
                reduce(last, s)
            project_out(last, LAYERS - 1)

        @block.scalar
        def _(act):
            start_at_one(act, dt_stored)
            act.wait_ge(a_landed, 16)
            act.activation(a_exp[:], a_exp[:], ACT.Exp).then_inc(a_exped, 1)
            act.wait_ge(a_exped, 1)

            def affine(n, l):
                act.wait_ge(norm.scaled, n + 1)
                act.wait_ge(in_landed, 48 * l + 48)
                act.wait_ge(in_summed, Z * n + 1)
                for k in range(2):
                    last = act.activation(un[:, k], xn[:, k], ACT.Identity, bias=norm_b[:, k:k + 1], scale=norm_w[:, k:k + 1])
                last.then_inc(affined, 1)

            def store_in(n, c, m):
                act.wait_ge(in_summed, Z * n + m + 2)
                bank = banks[6 + m % 2][:, 0:CT]
                if m < DT3:
                    if m == 0:
                        act.wait_ge(tapped, TAPS * DT3 * n + 1)
                    act.activation(padded[:, m, :, DCONV - 1:], bank.rearrange("p (b t) -> p b t", t=T), ACT.Copy).then_inc(in_stored, 1)
                else:
                    if m == DT3 and not is_early(n):
                        act.wait_ge(gated, n - 1)
                    act.activation(zs[:, c % 2, m - DT3], bank, ACT.Copy).then_inc(in_stored, 1)

            def first_tap(n, d):
                act.wait_ge(in_stored, Z * n + d + 1)
                if d == 0:
                    act.wait_ge(dt_fixed, n + 1)
                act.activation(conv[:, d].rearrange("p (b t) -> p b t", t=T), padded[:, d, :, 0:T], ACT.Identity,
                               bias=conv_b[:, d:d + 1], scale=conv_w[:, d, 0:1]).then_inc(tap0, 1)

            def silus(n, c):
                act.wait_ge(in_stored, Z * n + Z)
                act.activation(zs[:, c % 2], zs[:, c % 2], ACT.Silu).then_inc(z_silued, 1)
                act.wait_ge(tapped, TAPS * DT3 * (n + 1) + 1)
                act.activation(xa[:, c % 2], conv[:], ACT.Silu).then_inc(conv_silued, 1)

            def low_rank(n):
                low = slice(2 * DS, 2 * DS + DTR)
                act.wait_ge(x_summed, n + 1)
                act.wait_ge(dt_summed, DT3 * n + 1)
                act.activation(dtr[low, :], banks[6][low, 0:CT], ACT.Copy).then_inc(dtr_stored, 1)

            def store_mid(n, c):
                act.wait_ge(bc_step, 4 * n + 3)
                act.activation(bc[2 * DS:4 * DS, c % 2], mid[:], ACT.Copy).then_inc(bc_mid_stored, 1)

            def soften(n):
                if not is_first(n):
                    act.wait_ge(dt_ready, n)
                for d in range(DT3):
                    act.wait_ge(dt_summed, DT3 * n + d + 2)
                    act.activation(xb[:, d], banks[7 - d % 2][:, 0:CT], ACT.Identity, bias=dt_b[:, d:d + 1]).then_inc(dt_stored, 1)
                act.wait_ge(dt_stored, DT3 * (n + 1) + 1)
                act.activation(eb[:], xb[:], ACT.Abs).then_inc(dt_absed, 1)
                act.wait_ge(dt_absed, n + 1)
                act.activation(eb[:], eb[:], ACT.Exp, scale=-1.0).then_inc(dt_exped, 1)

            def soften_log(n):
                act.wait_ge(dt_lost, n + 1)
                act.activation(ub[:], ub[:], ACT.Ln).then_inc(dt_logged, 1)

            def start(n, l, c, s):
                if s == 1:
                    norm.act_square(act, n, sq[:], xc[:])
                elif s == 3:
                    norm.act_root(act, n)
                elif s == 4:
                    affine(n, l)
                elif s in (6, 7, 8):
                    store_in(n, c, 2 * (s - 6))
                    store_in(n, c, 2 * (s - 6) + 1)
                    if s == 7:
                        for d in range(DT3):
                            first_tap(n, d)
                elif s == 10:
                    silus(n, c)
                elif s == 11:
                    low_rank(n)
                elif s == 12:
                    store_mid(n, c)
                    soften(n)
                elif s == 14:
                    soften_log(n)

            def states(n, l, c):
                if c == 0:
                    if not is_first(n):
                        act.wait_ge(decayed, DS * n)
                    act.activation(a_neg[:], a_exp[:, bass.ds(l, 1)].rearrange("p a k -> p (a k)"), ACT.Copy, scale=-1.0).then_inc(a_ready, 1)
                    act.wait_ge(a_ready, l + 1)
                act.wait_ge(dt_ready, n + 1)
                for s in range(DS):
                    i = DS * n + s
                    early = is_first(n) and s < DEEP
                    if not early:
                        act.wait_ge(scanned, i - DEEP + 1)
                    for d in range(DT3):
                        last = act.activation(da[:, s % DEEP, d, :, 1:], dt[:, c % 2, d].rearrange("p (b t) -> p b t", t=T)[:, :, 1:],
                                              ACT.Exp, scale=a_neg[:, d * DS + s:d * DS + s + 1])
                    last.then_inc(decayed, 1)
                    act.wait_ge(c_spread, i + 1)
                    if not early:
                        act.wait_ge(produced, i - DEEP + 1)
                    act.activation(cs[:, s % DEEP], banks[5][:, 0:CT], ACT.Copy).then_inc(c_stored, 1)
                    if not is_last(n):
                        start(n + 1, l + (c + 1) // NC, (c + 1) % NC, s)

            for s in range(DS):
                start(0, 0, 0, s)
            all_chunks(act, states)

        @block.vector
        def _(dve):
            start_at_one(dve, added, skipped, tapped, dt_fixed)
            dve.memset(da[:, :, :, :, 0:1], 0.0)
            dve.memset(padded[:, :, :, 0:DCONV - 1], 0.0).then_inc(zeroed, 1)
            dve.wait_ge(zeroed, 1)

            def convolve(n, d):
                dve.wait_ge(tap0, DT3 * n + d + 1)
                out = conv[:, d].rearrange("p (b t) -> p b t", t=T)
                for k in range(1, DCONV):
                    if k > 1:
                        dve.wait_ge(tapped, TAPS * (DT3 * n + d) + k)
                    dve.scalar_tensor_tensor(out, padded[:, d, :, k:k + T], conv_w[:, d, k:k + 1], out, ALU.mult,
                                             ALU.add).then_inc(tapped, 1)

            def split_bc(n, c):
                dve.wait_ge(x_summed, n + 1)
                if not is_first(n):
                    dve.wait_ge(bc_mid_stored, n)
                summed = banks[6][0:2 * DS, 0:CT]
                high = bc[0:2 * DS, c % 2]
                dve.tensor_copy(high, summed).then_inc(bc_step, 1)
                dve.wait_ge(bc_step, 4 * n + 1)
                dve.tensor_tensor(rest[:], summed, high, ALU.subtract).then_inc(bc_step, 1)
                dve.wait_ge(bc_step, 4 * n + 2)
                dve.tensor_copy(mid[:], rest[:]).then_inc(bc_step, 1)
                dve.wait_ge(bc_step, 4 * n + 3)
                dve.tensor_tensor(bc[4 * DS:6 * DS, c % 2], rest[:], mid[:], ALU.subtract).then_inc(bc_step, 1)

            def soften(n):
                dve.wait_ge(dt_exped, n + 1)
                dve.tensor_scalar(ub[:], eb[:], 1.0, None, ALU.add).then_inc(dt_one, 1)
                dve.wait_ge(dt_one, n + 1)
                dve.scalar_tensor_tensor(lost[:], ub[:], -1.0, eb[:], ALU.add, ALU.subtract).then_inc(dt_lost, 1)

            def finish_dt(n, c):
                dve.wait_ge(dt_logged, n + 1)
                dve.tensor_tensor(lost[:], ub[:], lost[:], ALU.subtract).then_inc(dt_fixed, 1)
                dve.wait_ge(dt_fixed, n + 2)
                dve.scalar_tensor_tensor(dt[:, c % 2], xb[:], 0.0, lost[:], ALU.max, ALU.add).then_inc(dt_ready, 1)
                dve.wait_ge(dt_ready, n + 1)
                dve.wait_ge(conv_silued, n + 1)
                dve.tensor_tensor(dtx[:, c % 2], dt[:, c % 2], xa[:, c % 2], ALU.mult).then_inc(dtx_ready, 1)

            def start(n, c, s):
                if s == 0:
                    norm.dve_centre(dve, n, xc[:], chunk(resid, c))
                elif s == 2:
                    norm.dve_eps(dve, n)
                elif s == 3:
                    norm.dve_invert(dve, n)
                elif s == 4:
                    if not is_first(n):
                        dve.wait_ge(affined, n)
                    norm.dve_scale(dve, n, xn[:], xc[:])
                elif s in (7, 8, 9):
                    convolve(n, s - 7)
                elif s == 11:
                    split_bc(n, c)
                elif s == 13:
                    soften(n)
                elif s == 14:
                    finish_dt(n, c)

            def add_skip(n, l, c):
                dve.wait_ge(reduced, DS * (n + 1) + 1)
                dve.wait_ge(out_landed, 16 * l + 16)
                dve.wait_ge(out_summed, n + 1)
                for d in range(DT3):
                    dve.scalar_tensor_tensor(yg[:, d], xa[:, c % 2, d], skip[:, d:d + 1], banks[d][:, 0:CT],
                                             ALU.mult, ALU.add).then_inc(skipped, 1)

            def add_mixed(n, c):
                dve.wait_ge(out_summed, n + 2)
                for k in range(2):
                    last = dve.tensor_tensor(resid[:, k, c * CT:(c + 1) * CT], resid[:, k, c * CT:(c + 1) * CT],
                                             banks[6 + k][0:DH, 0:CT], ALU.add)
                last.then_inc(added, 1)

            def feed(n, c, s):
                i = DS * n + s
                dve.wait_ge(b_spread, i + 1)
                if s == 0:
                    dve.wait_ge(dtx_ready, n + 1)
                if not (is_first(n) and s < DEEP):
                    dve.wait_ge(scanned, i - DEEP + 1)
                dve.tensor_tensor(dbx[:, s % DEEP].rearrange("p (d t) -> p d t", d=DT3), dtx[:, c % 2],
                                  banks[3 + s % 2][:, 0:CT].unsqueeze(1).broadcast_to([128, DT3, CT]), ALU.mult).then_inc(fed, 1)

            def states(n, l, c):
                for s in range(DS):
                    i = DS * n + s
                    if s + 1 < DS:
                        feed(n, c, s + 1)
                    elif not is_last(n):
                        feed(n + 1, c + 1, 0)
                    dve.wait_ge(fed, i + 1)
                    dve.wait_ge(decayed, i + 1)
                    if not (is_first(n) and s < DEEP):
                        dve.wait_ge(produced, i - DEEP + 1)
                    dve.tensor_tensor_scan(hs[:, s % DEEP], da[:, s % DEEP].rearrange("p d b t -> p (d b t)"), dbx[:, s % DEEP], 0.0,
                                           ALU.mult, ALU.add).then_inc(scanned, 1)
                    if not is_last(n):
                        start(n + 1, (c + 1) % NC, s)
                    if not is_first(n):
                        if s == LAG - 1:
                            add_skip(n - 1, l if c else l - 1, (c - 1) % NC)
                        elif s == 15:
                            add_mixed(n - 1, (c - 1) % NC)

            for s in range(DS):
                start(0, 0, s)
            feed(0, 0, 0)
            all_chunks(dve, states)
            last = NC * LAYERS - 1
            add_skip(last, LAYERS - 1, NC - 1)
            add_mixed(last, NC - 1)

        @block.gpsimd
        def _(pool):
            def gate(n, c):
                pool.wait_ge(skipped, DT3 * (n + 1) + 1)
                pool.wait_ge(z_silued, n + 1)
                pool.tensor_tensor(yg[:], yg[:], zs[:, c % 2], ALU.mult).then_inc(gated, 1)

            def states(n, l, c):
                for s in range(DS):
                    i = DS * n + s
                    pool.wait_ge(scanned, i + 1)
                    pool.wait_ge(c_stored, i + 1)
                    if not (is_first(n) and s < DEEP):
                        pool.wait_ge(reduced, i - DEEP + 2)
                    pool.tensor_tensor(prod[:, s % DEEP].rearrange("p (d t) -> p d t", d=DT3),
                                       hs[:, s % DEEP].rearrange("p (d t) -> p d t", d=DT3),
                                       cs[:, s % DEEP].unsqueeze(1).broadcast_to([128, DT3, CT]), ALU.mult).then_inc(produced, 1)
                    if s == LAG + 1 and not is_first(n):
                        gate(n - 1, (c - 1) % NC)

            all_chunks(pool, states)
            gate(NC * LAYERS - 1, NC - 1)


def normalise_tokens(nc, tag, banks, consts, src, dst, eps=LN_EPS):
    with ExitStack() as ctx:
        sb = lambda name, shape, dt=F32: ctx.enter_context(nc.sbuf_tensor(f"{tag}_{name}", shape, dt))
        sem = ctx.enter_context(Semaphores(nc, tag + "_"))
        xc, sq = sb("nt_xc", [DH, 2, N]), sb("nt_sq", [DH, 2, N])
        norm = Norm(nc, sb, sem, "nt", consts, banks[0], banks[1], banks[2], eps)
        on_pe, on_dve, on_act = whole_norm(norm, src, xc, sq, dst)
        block = ctx.enter_context(nc.Block())
        block.tensor(on_pe)
        block.vector(on_dve)
        block.scalar(on_act)


def add_last_norm(nc, banks, consts, stream, resid, last_wb):
    with ExitStack() as ctx:
        sb = lambda name, shape, dt=F32: ctx.enter_context(nc.sbuf_tensor(name, shape, dt))
        sem = ctx.enter_context(Semaphores(nc))
        xc, sq, xn = sb("ln_xc", [DH, 2, N]), sb("ln_sq", [DH, 2, N]), sb("ln_xn", [DH, 2, N])
        wb = sb("ln_wb", [DH, 2, 2])
        wb_landed, affined = sem("last_wb_landed"), sem("last_affined")
        norm = Norm(nc, sb, sem, "ln", consts, banks[0], banks[1], banks[2], LN_EPS)
        on_pe, on_dve, on_act = whole_norm(norm, resid, xc, sq, xn)
        block = ctx.enter_context(nc.Block())
        block.tensor(on_pe)
        block.scalar(on_act)

        @block.sync
        def _(sp):
            sp.dma_start(wb[:], last_wb).then_inc(wb_landed, 16)

        @block.vector
        def _(dve):
            on_dve(dve)
            dve.wait_ge(norm.scaled, NC)
            dve.wait_ge(wb_landed, 16)
            for k in range(2):
                dve.tensor_scalar(xn[:, k], xn[:, k], wb[:, 0, k:k + 1], wb[:, 1, k:k + 1], ALU.mult, ALU.add).then_inc(affined, 1)
                dve.wait_ge(affined, k + 1)
                dve.tensor_tensor(stream[:, k], stream[:, k], xn[:, k], ALU.add)


CONSTS = {"mean": ([DH, DH], F32), "ident": ([128, 128], F32), "ones": ([128, 128], F32), "rotate": ([128, 128], F32),
          "mask": ([GT, GT], F32), "before": ([GT, GT], F32), "counting": ([GT, NT], F32), "tile_starts": ([GT, NT], F32),
          "expert_starts": ([GT, E], F32), "own_rows": ([GT, NG, 2], F32)}


def constants():
    f = np.float32
    rotate = np.zeros((128, 128), f)
    for h in range(4):
        for i in range(0, HD, 2):
            rotate[32 * h + i + 1, 32 * h + i] = -1.0
            rotate[32 * h + i, 32 * h + i + 1] = 1.0
    seq = np.arange(GT) // T
    freq = (1.0 / 10000.0 ** (np.arange(0, HD, 2, dtype=f) / f(HD))).astype(f)
    angle = np.arange(T, dtype=f)[:, None] * freq[None]
    angle = np.concatenate([angle, angle], -1).T
    rope = np.zeros((128, 2, CB, T), f)
    for h in range(4):
        rope[32 * h:32 * h + HD, 0] = np.cos(angle)[:, None]
        rope[32 * h:32 * h + HD, 1] = np.sin(angle)[:, None]
    return {
        "mean": np.full((DH, DH), 1.0 / D, f), "ident": np.eye(128, dtype=f), "ones": np.ones((128, 128), f), "rotate": rotate,
        "mask": np.where(seq[:, None] == seq[None], 0.0, MASKED).astype(f),
        "before": np.triu(np.ones((GT, GT), f), 1), "counting": np.tile(np.arange(NT, dtype=f), (GT, 1)),
        "tile_starts": np.tile(np.arange(NT, dtype=f) * TS, (GT, 1)), "expert_starts": np.tile(np.arange(E, dtype=f) * CAP, (GT, 1)),
        "own_rows": (E * CAP + np.arange(2 * N, dtype=f)).reshape(NG, GT, 2).swapaxes(0, 1),
        "part_rows": np.tile(np.eye(2 * DS, dtype=f), (3, 1))}, rope.reshape(128, 2, CT)


def audio_tower(nc, a, out, probe=None):
    with ExitStack() as ctx:
        sb = lambda name, shape, dt=F32: ctx.enter_context(nc.sbuf_tensor(name, shape, dt))
        psum = ctx.enter_context(nc.psum_tensor("banks", [128, 8, 512], F32))
        banks = [psum[:, b] for b in range(8)]
        stream = sb("stream", [DH, 2, N])
        consts = {name: sb("const_" + name, shape, dt) for name, (shape, dt) in CONSTS.items()}
        consts["spread"] = sb("const_spread", [6 * DS, 2 * DS, 128], BF16)

        def show(tile):
            done = ctx.enter_context(nc.semaphore("probe"))
            with nc.Block() as block:
                @block.sync
                def _(sp):
                    sp.dma_start(out, tile).then_inc(done, 16)
                    sp.wait_ge(done, 16)

        dram = lambda name, rows: nc.dram_tensor(name, (rows, D), F32, kind="Internal").ap()
        slots0, results0 = dram("slots0", E * CAP + 2 * N), dram("results0", E * CAP)
        slots1, results1 = dram("slots1", NT * TS), dram("results1", NT * TS)

        embed(nc, banks, stream, a["x"], a["tok_w"], a["tok_b"], consts, {name: a[name] for name in (*CONSTS, "part_rows")},
              (slots0[0:E * CAP], slots1))
        if probe == "embed":
            return show(stream[:])
        attention(nc, banks, stream, consts, a["qk_w"], a["qk_b"], a["v_w"], a["v_b"], a["attn_out_w"], a["attn_out_b"], a["rope"])
        if probe == "attn":
            return show(stream[:])
        with ExitStack() as inner:
            isb = lambda name, shape, dt=F32: inner.enter_context(nc.sbuf_tensor("moe0_" + name, shape, dt))
            xf = isb("x", [DH, 2, N])
            r = routed_rows(isb)
            r["weight_sum"] = isb("weight_sum", [GT, NG])
            normalise_tokens(nc, "norm0", banks, consts, stream, xf)
            route(nc, "route0", banks, consts, stream, xf, a["gate0_w"], None, r, slots0, None, CAP)
            gated_experts(nc, banks, consts, slots0, results0, a["moe0_in"], a["moe0_out"], a["moe0_norm"])
            combine(nc, "combine0", banks, consts, stream, r, results0)
        if probe == "moe0":
            return show(stream[:])
        with ExitStack() as inner:
            resid = inner.enter_context(nc.sbuf_tensor("resid", [DH, 2, N], F32))
            normalise_tokens(nc, "norm_r", banks, consts, stream, resid)
            state_space(nc, banks, consts, resid, a["ss_in"], a["ss_conv"], a["ss_dt_w"], a["ss_out"], a["ss_a_log"])
            add_last_norm(nc, banks, consts, stream, resid, a["last_wb"])
        if probe == "mamba":
            return show(stream[:])
        with ExitStack() as inner:
            isb = lambda name, shape, dt=F32: inner.enter_context(nc.sbuf_tensor("moe1_" + name, shape, dt))
            xn = isb("x", [DH, 2, N])
            r = routed_rows(isb)
            tiles_of = isb("tile_expert", [1, NT], U32)
            w = {"in": isb("all_in", [DH, E, 2, H1]), "b_in": isb("all_b_in", [128, E, H1 // 128]),
                 "out": isb("all_out", [128, E, H1 // 128, D]), "b_out": isb("all_b_out", [TS, E, D])}
            weights_landed = inner.enter_context(nc.semaphore("moe1_weights_landed"))
            load_experts(nc, w, weights_landed, a["moe1_in"], a["moe1_b_in"], a["moe1_out"], a["moe1_b_out"])
            normalise_tokens(nc, "norm1", banks, consts, stream, xn)
            route(nc, "route1", banks, consts, stream, xn, a["gate1_w"], a["gate1_b"], r, slots1, tiles_of, None)
            tiled_experts(nc, banks, consts, slots1, results1, tiles_of, w, weights_landed)
            combine(nc, "combine1", banks, consts, stream, r, results1, out)


def routed_rows(sb):
    return {"x_rows": sb("x_rows", [GT, NG, D]), "stream_rows": sb("stream_rows", [GT, NG, D]),
            "weights": sb("pair_weights", [GT, NG, 2]), "source": sb("gather_rows", [GT, NG, 2], U32)}


def halves(w):
    return w.reshape(2, DH, *w.shape[1:]).swapaxes(0, 1)


def tiles(w, n):
    return w.reshape(n, 128, *w.shape[1:]).swapaxes(0, 1)


def laid_out(i):
    a, a["rope"] = constants()
    a["x"] = i["x"]
    a["tok_w"] = np.zeros((CHANNEL_ROWS, PATCH, D), np.float32)
    a["tok_w"][:CHANNELS] = i["L0_tok_W"].reshape(D, CHANNELS, PATCH).transpose(1, 2, 0)
    a["tok_b"] = halves(i["L0_tok_b"])
    wqkv, bqkv = i["L0_attn_W_qkv"], i["L0_attn_b_qkv"]
    qk_w, qk_b = np.zeros((D, 2, QT, 4, 32), np.float32), np.zeros((2, QT, 4, 32), np.float32)
    qk_w[..., :HD] = wqkv[:, :2 * D].reshape(D, 2, QT, 4, HD)
    qk_b[..., :HD] = bqkv[:2 * D].reshape(2, QT, 4, HD)
    a["qk_w"] = halves(qk_w.reshape(D, 2 * QT, 128))
    a["qk_b"] = qk_b.reshape(2 * QT, 128).T
    a["v_w"] = halves(wqkv[:, 2 * D:])
    a["v_b"] = np.tile(bqkv[2 * D:], (GT, 1))
    a["attn_out_w"] = halves(i["L0_attn_W_out"])
    a["attn_out_b"] = halves(i["L0_attn_b_out"])
    a["gate0_w"] = halves(i["L0_ffn_gate_w"].T)
    a["moe0_in"] = np.stack([halves(w.T) for w in i["L0_ffn_w13"]])
    a["moe0_out"] = np.stack([tiles(w.T, H0 // 128) for w in i["L0_ffn_w2"]])
    a["moe0_norm"] = np.stack([halves(w) for w in i["L0_ffn_norm_w"]], 1)
    m = {k[len("L1_attn_"):]: v for k, v in i.items() if k.startswith("L1_attn_")}
    a["ss_in"] = np.stack([np.concatenate([halves(m["in_proj_w"][l].T).reshape(DH, -1), halves(m["norm_w"][l]), halves(m["norm_b"][l])], 1)
                           for l in range(LAYERS)])
    x_w = np.concatenate([m["x_proj_w"][:, DTR:], m["x_proj_w"][:, :DTR]], 1)
    flat = lambda w: tiles(w, DT3).reshape(128, -1)
    a["ss_conv"] = np.stack([np.concatenate([flat(m["conv_w"][l]), flat(m["conv_b"][l]), flat(m["dt_proj_b"][l]), flat(x_w[l].T)], 1)
                             for l in range(LAYERS)])
    a["ss_dt_w"] = m["dt_proj_w"].transpose(0, 2, 1)
    a["ss_out"] = np.stack([np.concatenate([flat(m["D_skip"][l]), flat(m["out_proj_w"][l].T)], 1) for l in range(LAYERS)])
    a["ss_a_log"] = np.stack([flat(w) for w in m["A_log"]], 1)
    a["last_wb"] = np.stack([halves(m["norm_f_w"]), halves(m["norm_f_b"])], 1)
    a["gate1_w"] = halves(i["L1_ffn_Wg"].T)
    a["gate1_b"] = np.tile(i["L1_ffn_bg"], (GT, 1))
    a["moe1_in"] = np.stack([halves(w) for w in i["L1_ffn_W1"]], 1)
    a["moe1_out"] = np.stack([tiles(w, H1 // 128) for w in i["L1_ffn_W2"]], 1)
    a["moe1_b_in"] = np.stack([tiles(b, H1 // 128) for b in i["L1_ffn_b1"]], 1)
    a["moe1_b_out"] = np.tile(i["L1_ffn_b2"], (TS, 1, 1))
    return {name: np.ascontiguousarray(v) for name, v in a.items()}


def kernel(**inputs):
    import concourse.bacc as bacc
    from concourse.bass_utils import run_bass_kernel_spmd

    arrays = laid_out({name: np.asarray(v) for name, v in inputs.items()})
    nc = bacc.Bacc("TRN2", target_bir_lowering=False, num_devices=1)
    dram = {name: nc.dram_tensor("in_" + name, v.shape, mybir.dt.from_np(v.dtype), kind="ExternalInput").ap() for name, v in arrays.items()}
    out = nc.dram_tensor("out", (SEQS, T, D), F32, kind="ExternalOutput").ap()
    audio_tower(nc, dram, out)
    result = run_bass_kernel_spmd(nc, [{"in_" + name: v for name, v in arrays.items()}], core_ids=[0])
    return result.results[0]["out"]
```

```python
from contextlib import ExitStack

import numpy as np
import concourse.bass as bass
from concourse import mybir

ALU = mybir.AluOpType
ACT = mybir.ActivationFunctionType
AX = mybir.AxisListType
F32 = mybir.dt.float32
BF16 = mybir.dt.bfloat16
U32 = mybir.dt.uint32

SEQS, CHANNELS, SAMPLES, PATCH = 64, 90, 375, 16
T = SAMPLES // PATCH
N = SEQS * T
CHANNEL_ROWS = -(-CHANNELS // 32) * 32
D = 192
DH = D // 2
CB = 16
CT = CB * T
NC = N // CT
GB = 4
GT = GB * T
NG = N // GT
GP = -(-GT // 32) * 32
GC = CT // GT
RT = 128
RG = -(-N // RT)
RQ = 3
HEADS, HD = 12, 16
QT = 3
E = 8
H0 = 512
H1 = 768
CAP = -(-5 * 2 * N // (4 * E))
LAYERS, DI, DS, DCONV, DTR = 4, 384, 16, 4, 12
DT3 = DI // 128
TAPS = DCONV - 1
SP = CAP // 4
TS = 128
NT = (2 * N + E * (TS - 1)) // TS
NT += NT % 2
MASKED = -1e30
LN_EPS, RMS_EPS = 1e-5, 1e-6


class Semaphores:

    def __init__(self, nc, prefix=""):
        self.nc, self.prefix, self.taken = nc, prefix, []

    def __enter__(self):
        return self

    def __call__(self, name):
        self.taken.append(self.nc.alloc_semaphore(self.prefix + name))
        return self.taken[-1]

    def __exit__(self, *error):
        if error[0] is None:
            self.nc.clear_and_free_semaphores(self.taken)
            self.nc.all_engine_barrier()


def start_at_one(eng, *semaphores):
    for semaphore in semaphores:
        eng.sem_inc(semaphore, 1)


class Norm:

    def __init__(self, nc, sb, sem, name, consts, mean_bank, var_bank, rep_bank):
        self.nc, self.consts = nc, consts
        self.mean_bank, self.var_bank, self.rep_bank = mean_bank, var_bank, rep_bank
        self.ve = sb(name + "_var_eps", [GT, GC])
        self.log = sb(name + "_log", [GT, GC])
        self.inv = sb(name + "_inv", [GT, GC])
        self.meaned = sem(name + "_meaned")
        self.centred = sem(name + "_centred")
        self.squared = sem(name + "_squared")
        self.summed = sem(name + "_summed")
        self.eps_added = sem(name + "_eps_added")
        self.logged = sem(name + "_logged")
        self.inverted = sem(name + "_inverted")
        self.spread = sem(name + "_spread")
        self.scaled = sem(name + "_scaled")

    def pe_mean(self, pe, src):
        for k in range(2):
            mm = pe.matmul(self.mean_bank[0:DH, 0:CT], self.consts["mean"][:, 0:DH], src[:, k], start=(k == 0), stop=(k == 1))
        mm.then_inc(self.meaned, 1)

    def pe_square(self, pe, n, sq):
        pe.wait_ge(self.squared, n + 1)
        for g in range(GC):
            for k in range(2):
                mm = pe.matmul(self.var_bank[0:GT, g:g + 1], sq[:, k, g * GT:(g + 1) * GT], self.consts["mean"][:, 0:1],
                               start=(k == 0), stop=(k == 1))
        mm.then_inc(self.summed, 1)

    def pe_spread(self, pe, n):
        pe.wait_ge(self.inverted, n + 1)
        for g in range(GC):
            mm = pe.matmul(self.rep_bank[0:DH, g * GT:(g + 1) * GT], self.inv[:, g:g + 1].broadcast_to([GT, DH]),
                           self.consts["ident"][0:GT, 0:GT], start=True, stop=True)
        mm.then_inc(self.spread, 1)

    def dve_centre(self, dve, n, xc, src):
        dve.wait_ge(self.meaned, n + 1)
        dve.tensor_tensor(xc, src, self.mean_bank[0:DH, 0:CT].unsqueeze(1).broadcast_to([DH, 2, CT]),
                          ALU.subtract).then_inc(self.centred, 1)

    def act_square(self, act, n, sq, xc):
        act.wait_ge(self.centred, n + 1)
        act.activation(sq, xc, ACT.Square).then_inc(self.squared, 1)

    def dve_eps(self, dve, n):
        dve.wait_ge(self.summed, n + 1)
        dve.tensor_scalar(self.ve[:], self.var_bank[0:GT, 0:GC], 1.0, LN_EPS,
                          ALU.mult, ALU.add).then_inc(self.eps_added, 1)

    def act_invert_root(self, act, n):
        act.wait_ge(self.eps_added, n + 1)
        act.activation(self.log[:], self.ve[:], ACT.Ln).then_inc(self.logged, 1)
        act.wait_ge(self.logged, n + 1)
        act.activation(self.inv[:], self.log[:], ACT.Exp, scale=-0.5).then_inc(self.inverted, 1)

    def dve_scale(self, dve, n, dst, xc):
        dve.wait_ge(self.spread, n + 1)
        dve.tensor_tensor(dst, xc, self.rep_bank[0:DH, 0:CT].unsqueeze(1).broadcast_to([DH, 2, CT]),
                          ALU.mult).then_inc(self.scaled, 1)


def chunk(tile, c):
    return tile[:, :, bass.ds(c * CT, CT)]


def whole_norm(sb, sem, name, banks, consts, src, xc, sq, dst):
    ve = sb(name + "_var_eps", [GT, NG])
    std = sb(name + "_std", [GT, NG])
    inv = sb(name + "_inv", [GT, NG])
    meaned, centred, squared = sem(name + "_meaned"), sem(name + "_centred"), sem(name + "_squared")
    summed, eps_added, rooted = sem(name + "_summed"), sem(name + "_eps_added"), sem(name + "_rooted")
    inverted, spread, scaled = sem(name + "_inverted"), sem(name + "_spread"), sem(name + "_scaled")
    over_halves = lambda bank: bank[0:DH, 0:CT].unsqueeze(1).broadcast_to([DH, 2, CT])

    def on_pe(pe):
        for c in range(NC):
            for k in range(2):
                mm = pe.matmul(banks[c][0:DH, 0:CT], consts["mean"][:, 0:DH], src[:, k, c * CT:(c + 1) * CT], start=(k == 0), stop=(k == 1))
            mm.then_inc(meaned, 1)
        for g in range(NG):
            if g % GC == 0:
                pe.wait_ge(squared, g // GC + 1)
            for k in range(2):
                mm = pe.matmul(banks[NC][0:GT, g:g + 1], sq[:, k, g * GT:(g + 1) * GT], consts["mean"][:, 0:1], start=(k == 0), stop=(k == 1))
        mm.then_inc(summed, 1)
        pe.wait_ge(inverted, 1)
        for g in range(NG):
            mm = pe.matmul(banks[g // GC][0:DH, (g % GC) * GT:(g % GC + 1) * GT], inv[:, g:g + 1].broadcast_to([GT, DH]),
                           consts["ident"][0:GT, 0:GT], start=True, stop=True)
            if g % GC == GC - 1:
                mm.then_inc(spread, 1)

    def on_dve(dve):
        for c in range(NC):
            dve.wait_ge(meaned, c + 1)
            dve.tensor_tensor(chunk(xc, c), chunk(src, c), over_halves(banks[c]), ALU.subtract).then_inc(centred, 1)
        dve.wait_ge(summed, 1)
        dve.tensor_scalar(ve[:], banks[NC][0:GT, 0:NG], 1.0, LN_EPS, ALU.mult, ALU.add).then_inc(eps_added, 1)
        dve.wait_ge(rooted, 1)
        dve.reciprocal(inv[:], std[:]).then_inc(inverted, 1)
        dve.wait_ge(centred, NC)
        for c in range(NC):
            dve.wait_ge(spread, c + 1)
            dve.tensor_tensor(chunk(dst, c), chunk(xc, c), over_halves(banks[c]), ALU.mult).then_inc(scaled, 1)

    def on_act(act):
        for c in range(NC):
            act.wait_ge(centred, c + 1)
            act.activation(chunk(sq, c), chunk(xc, c), ACT.Square).then_inc(squared, 1)
        act.wait_ge(eps_added, 1)
        act.activation(std[:], ve[:], ACT.Sqrt).then_inc(rooted, 1)

    return on_pe, on_dve, on_act, scaled


def embed(nc, banks, stream, x, tok_w, tok_b, consts, const_srcs, cleared):
    with ExitStack() as ctx:
        sb = lambda name, shape, dt=F32: ctx.enter_context(nc.sbuf_tensor(name, shape, dt))
        sem = ctx.enter_context(Semaphores(nc))
        xs = [sb(f"signal{u}", [CHANNELS, CB, SAMPLES]) for u in range(2)]
        patches = [sb(f"patches{u}", [CHANNEL_ROWS, PATCH, CB, T]) for u in range(2)]
        part_rows = sb("const_part_rows", [6 * DS, 2 * DS])
        w = sb("patch_w", [CHANNEL_ROWS, PATCH, D])
        b = sb("patch_b", [DH, 2])
        WP = 4
        w_landed = [sem(f"patch_w{q}_landed") for q in range(PATCH // WP)]
        b_landed = sem("patch_b_landed")
        const_landed = sem("constants_landed")
        spread_made = sem("spread_made")
        x_landed = [sem(f"signal{u}_landed") for u in range(2)]
        ZR = 32
        zeros = sb("zeros", [128, ZR * D])
        zeroed = sem("zeros_made")
        slots_cleared = sem("slots_cleared")
        padded = sem("patches_padded")
        sorted_in = sem("patches_sorted")
        summed = [sem(f"patch_half{k}_summed") for k in range(2)]
        stored = [sem(f"patch_half{k}_stored") for k in range(2)]
        block = ctx.enter_context(nc.Block())
        K = PATCH // WP

        def load(sp, c):
            sp.dma_start(xs[c % 2][:], x[c * CB:(c + 1) * CB].rearrange("b c t -> c b t")).then_inc(x_landed[c % 2], 16)

        @block.sync
        def _(sp):
            load(sp, 0)
            for q in range(K):
                sp.dma_start(w[:, q * WP:(q + 1) * WP], tok_w[:, q * WP:(q + 1) * WP]).then_inc(w_landed[q], 16)
            sp.dma_start(b[:], tok_b).then_inc(b_landed, 16)
            load(sp, 1)
            for name, src in const_srcs.items():
                sp.dma_start((part_rows if name == "part_rows" else consts[name])[:], src).then_inc(const_landed, 16)
            for c in range(2, NC):
                sp.wait_ge(sorted_in, K * (c - 1))
                load(sp, c)
            sp.wait_ge(const_landed, 16 * len(const_srcs))
            sp.wait_ge(zeroed, 1)
            for slots in cleared:
                sp.dma_start(slots.rearrange("(p r) d -> p (r d)", r=ZR), zeros[0:slots.shape[0] // ZR]).then_inc(slots_cleared, 16)
            sp.wait_ge(slots_cleared, 16 * len(cleared))

        @block.vector
        def _(dve):
            for c in range(NC):
                if c < 2:
                    dve.wait_ge(padded, c + 1)
                dve.wait_ge(x_landed[c % 2], 16 * (c // 2 + 1))
                if c >= 2:
                    dve.wait_ge(summed[1], c - 1)
                signal = xs[c % 2][:, :, 0:PATCH * T].rearrange("c b (t p) -> c p b t", p=PATCH)
                for q in range(K):
                    for p in range(q * WP, (q + 1) * WP):
                        last = dve.tensor_copy(patches[c % 2][0:CHANNELS, p], signal[:, p])
                    last.then_inc(sorted_in, 1)

        @block.gpsimd
        def _(pool):
            for u in range(2):
                pool.memset(patches[u][CHANNEL_ROWS - 32:CHANNEL_ROWS], 0.0).then_inc(padded, 1)
            pool.wait_ge(padded, 2)
            pool.memset(zeros[:], 0.0).then_inc(zeroed, 1)
            pool.wait_ge(zeroed, 1)
            pool.wait_ge(const_landed, 16 * len(const_srcs))
            pool.tensor_copy(consts["spread"][:], part_rows[:].unsqueeze(2).broadcast_to([6 * DS, 2 * DS, 128])).then_inc(spread_made, 1)

        @block.tensor
        def _(pe):
            for c in range(NC):
                for k in range(2):
                    if c >= 1:
                        pe.wait_ge(stored[k], c)
                    for p in range(PATCH):
                        if k == 0 and p % WP == 0:
                            pe.wait_ge(sorted_in, K * c + p // WP + 1)
                            if c == 0:
                                pe.wait_ge(w_landed[p // WP], 16)
                        mm = pe.matmul(banks[k][0:DH, 0:CT], w[:, p, k * DH:(k + 1) * DH],
                                       patches[c % 2][:, p].rearrange("c b t -> c (b t)"), start=(p == 0), stop=(p == PATCH - 1))
                    mm.then_inc(summed[k], 1)

        @block.scalar
        def _(act):
            act.wait_ge(b_landed, 16)
            for c in range(NC):
                for k in range(2):
                    act.wait_ge(summed[k], c + 1)
                    act.activation(stream[:, k, c * CT:(c + 1) * CT], banks[k][0:DH, 0:CT], ACT.Identity,
                                   bias=b[:, k:k + 1]).then_inc(stored[k], 1)


def attention(nc, banks, stream, consts, qk_w, qk_b, v_w, v_b, out_w, out_b, rope):
    with ExitStack() as ctx:
        sb = lambda name, shape, dt=F32: ctx.enter_context(nc.sbuf_tensor(name, shape, dt))
        sem = ctx.enter_context(Semaphores(nc))
        DEPTH = 4
        wqk = sb("wqk", [DH, 2, 2 * QT, 128])
        bqk = sb("bqk", [128, 2 * QT])
        wv = sb("wv", [DH, 2, D])
        bv = sb("bv", [GT, D])
        wo = sb("wo", [DH, 2, D])
        bo = sb("bo", [DH, 2])
        cos_sin = sb("cos_sin", [128, 2, CT])
        xc = sb("at_xc", [DH, 2, N])
        sq = sb("at_sq", [DH, 2, N])
        xn = sb("at_xn", [DH, 2, N])
        xl = sb("at_chunk", [DH, 2, CT])
        biased_t = sb("qk_biased", [128, 2, CT])
        t1 = sb("rope_cos_part", [128, 2, CT])
        t2 = sb("rope_sin_part", [128, 2, CT])
        qm = sb("q_one_head", [128, HEADS, CT])
        kt = sb("k_heads", [128, QT, CT])
        va = sb("v_and_one", [GP, GC, HEADS, HD + 1])
        sm = sb("scores", [GT, DEPTH, 4, GT])
        sx = sb("scores_less_max", [GT, DEPTH, 4, GT])
        ex = sb("exps", [GP, DEPTH, 4, GT])
        pt = sb("exps_turned", [GP, DEPTH, 4, GT])
        mx = sb("score_max", [GT, DEPTH, 4])
        rec = sb("inverse_sums", [GT, 2, HEADS])
        cn = sb("context", [GP, 2, HEADS, HD])
        cx = sb("context_turned", [DH, 2, CT])
        on_pe, on_dve, on_act, scaled = whole_norm(sb, sem, "at", banks, consts, stream, xc, sq, xn)
        landed = sem("at_weights_landed")
        zeroed = sem("at_zeroed")
        copied = sem("chunk_copied")
        projected = sem("qk_projected")
        biased = sem("qk_biased_done")
        turned = sem("qk_rotated")
        cos_done = sem("cos_done")
        sin_done = sem("sin_done")
        roped = sem("qk_roped")
        v_summed = sem("v_summed")
        v_stored = sem("v_stored")
        scored = sem("scored")
        masked = sem("scores_masked")
        maxed = sem("scores_maxed")
        lessened = sem("scores_lessened")
        exped = sem("scores_exped")
        exps_turned = sem("exps_turned_done")
        exps_stored = sem("exps_stored")
        mixed = sem("values_mixed")
        inverted = sem("sums_inverted")
        normed = sem("context_normed")
        ctx_turned = sem("context_turned_done")
        ctx_stored = sem("context_stored")
        out_summed = sem("out_summed")
        added = sem("attention_added")
        block = ctx.enter_context(nc.Block())
        U = QT * GC
        J = 2 * QT
        TURN, MIX, NORM, CONTEXT = 2, 3, 6, 8

        @block.sync
        def _(sp):
            for dst, src in ((wqk, qk_w), (bqk, qk_b), (wv, v_w), (bv, v_b), (wo, out_w), (bo, out_b), (cos_sin, rope)):
                sp.dma_start(dst[:], src).then_inc(landed, 16)

        @block.gpsimd
        def _(pool):
            pool.memset(qm[:], 0.0).then_inc(zeroed, 1)
            pool.memset(va[:], 1.0).then_inc(zeroed, 1)
            pool.wait_ge(zeroed, 2)
            for n, tile in enumerate((ex, pt, cn)):
                pool.memset(tile[:], 0.0).then_inc(zeroed, 1)
                pool.wait_ge(zeroed, n + 3)
            pool.wait_ge(landed, 16 * 7)
            with pool.Fori(0, NC) as c:
                for j in range(J):
                    pool.wait_ge(biased, J * c + j + 1)
                    if j >= 2:
                        pool.wait_ge(roped, J * c + j)
                    else:
                        pool.wait_ge(roped, J * c + 1)
                    pool.tensor_tensor(t1[:, j % 2], biased_t[:, j % 2], cos_sin[:, 0], ALU.mult).then_inc(cos_done, 1)
                for u in range(U):
                    b = u % DEPTH
                    pool.wait_ge(maxed, U * c + u + 1)
                    pool.wait_ge(masked, U * c + u + 1)
                    if u >= DEPTH:
                        pool.wait_ge(exped, U * c + u - DEPTH + 1)
                    pool.tensor_tensor(sx[:, b], sm[:, b], mx[:, b].unsqueeze(2).broadcast_to([GT, 4, GT]),
                                       ALU.subtract).then_inc(lessened, 1)

        @block.tensor
        def _(pe):
            start_at_one(pe, v_summed, mixed)
            on_pe(pe)
            pe.wait_ge(landed, 16 * 7)
            with pe.Fori(0, NC) as c:
                pe.wait_ge(copied, c + 1)

                def rotate(j):
                    pe.wait_ge(biased, J * c + j + 1)
                    if j >= 2:
                        pe.wait_ge(sin_done, J * c + j - 1)
                    pe.matmul(banks[2 + j % 2][:, 0:CT], consts["rotate"][:], biased_t[:, j % 2], start=True,
                              stop=True).then_inc(turned, 1)

                for j in range(J):
                    if j >= 2:
                        pe.wait_ge(biased, J * c + j - 1)
                    for k in range(2):
                        mm = pe.matmul(banks[j % 2][:, 0:CT], wqk[:, k, j], xl[:, k], start=(k == 0), stop=(k == 1))
                    mm.then_inc(projected, 1)
                    if j >= 1:
                        rotate(j - 1)
                rotate(J - 1)
                pe.wait_ge(added, 2 * c + 1)
                for g in range(GC):
                    for k in range(2):
                        mm = pe.matmul(banks[4 + g][0:GT, 0:D], xl[:, k, g * GT:(g + 1) * GT], wv[:, k],
                                       start=(k == 0), stop=(k == 1))
                    mm.then_inc(v_summed, 1)
                pe.wait_ge(roped, J * c + J + 1)
                pe.wait_ge(v_stored, GC * c + GC)

                def score(u):
                    g, j = divmod(u, QT)
                    if u >= 2:
                        pe.wait_ge(masked, U * c + u - 1)
                    for i in range(4):
                        mm = pe.matmul(banks[u % 2][0:GT, i * GT:(i + 1) * GT], qm[:, 4 * j + i, g * GT:(g + 1) * GT],
                                       kt[:, j, g * GT:(g + 1) * GT], start=True, stop=True)
                    mm.then_inc(scored, 1)

                def turn(u):
                    pe.wait_ge(exped, U * c + u + 1)
                    if u >= 2:
                        pe.wait_ge(exps_stored, U * c + u - 1)
                    for i in range(4):
                        mm = pe.matmul(banks[2 + u % 2][0:GT, i * GT:(i + 1) * GT], ex[:, u % DEPTH, i], consts["ident"][0:GP, 0:GT],
                                       start=True, stop=True)
                    mm.then_inc(exps_turned, 1)

                def mix(u):
                    g, j = divmod(u, QT)
                    pe.wait_ge(exps_stored, U * c + u + 1)
                    if j == 0 and g >= 2:
                        pe.wait_ge(normed, GC * c + g - 1)
                    for i in range(4):
                        h = 4 * j + i
                        mm = pe.matmul(banks[6 + g % 2][0:GT, h * (HD + 1):(h + 1) * (HD + 1)], pt[:, u % DEPTH, i], va[:, g, h],
                                       start=True, stop=True)
                    mm.then_inc(mixed, 1)

                def turn_context(g):
                    pe.wait_ge(normed, GC * c + g + 1)
                    if g >= 2:
                        pe.wait_ge(ctx_stored, GC * c + g - 1)
                    for k in range(2):
                        mm = pe.matmul(banks[4 + g % 2][0:DH, k * GT:(k + 1) * GT],
                                       cn[:, g % 2].rearrange("p h d -> p (h d)")[:, k * DH:(k + 1) * DH], consts["ident"][0:GP, 0:GT],
                                       start=True, stop=True)
                    mm.then_inc(ctx_turned, 1)

                for u in range(U + QT + 3):
                    if u < U:
                        score(u)
                    if TURN <= u < U + TURN:
                        turn(u - TURN)
                    if MIX <= u < U + MIX:
                        mix(u - MIX)
                    if u >= CONTEXT and (u - CONTEXT) % QT == 0:
                        turn_context((u - CONTEXT) // QT)
                pe.wait_ge(ctx_stored, GC * c + GC)
                for m in range(2):
                    for k in range(2):
                        mm = pe.matmul(banks[4 + m][0:DH, 0:CT], wo[:, k, m * DH:(m + 1) * DH], cx[:, k], start=(k == 0), stop=(k == 1))
                    mm.then_inc(out_summed, 1)

        def store_context(act, c, g):
            act.wait_ge(ctx_turned, GC * c + g + 1)
            act.activation(cx[:, :, g * GT:(g + 1) * GT], banks[4 + g % 2][0:DH, 0:2 * GT].rearrange("p (k t) -> p k t", k=2),
                           ACT.Copy).then_inc(ctx_stored, 1)

        @block.scalar
        def _(act):
            on_act(act)
            act.wait_ge(landed, 16 * 7)
            act.wait_ge(scaled, NC)
            with act.Fori(0, NC) as c:
                act.wait_ge(v_summed, GC * c + 1)
                act.activation(xl[:], chunk(xn, c), ACT.Copy).then_inc(copied, 1)
                for j in range(J):
                    act.wait_ge(projected, J * c + j + 1)
                    if j >= 2:
                        act.wait_ge(turned, J * c + j - 1)
                        act.wait_ge(cos_done, J * c + j - 1)
                    act.activation(biased_t[:, j % 2], banks[j % 2][:, 0:CT], ACT.Identity, bias=bqk[:, j:j + 1]).then_inc(biased, 1)
                for u in range(U + QT + 3):
                    if u < U:
                        act.wait_ge(lessened, U * c + u + 1)
                        if u >= DEPTH:
                            act.wait_ge(exps_turned, U * c + u - DEPTH + 1)
                        act.activation(ex[0:GT, u % DEPTH], sx[:, u % DEPTH], ACT.Exp).then_inc(exped, 1)
                    if TURN <= u < U + TURN:
                        v = u - TURN
                        act.wait_ge(exps_turned, U * c + v + 1)
                        if v >= DEPTH:
                            act.wait_ge(mixed, U * c + v - DEPTH + 2)
                        act.activation(pt[0:GT, v % DEPTH].rearrange("p a b -> p (a b)"), banks[2 + v % 2][0:GT, 0:4 * GT], ACT.Copy).then_inc(exps_stored, 1)
                    if u >= CONTEXT and (u - CONTEXT) % QT == 0:
                        store_context(act, c, (u - CONTEXT) // QT)

        @block.vector
        def _(dve):
            start_at_one(dve, roped, added)
            on_dve(dve)
            dve.wait_ge(landed, 16 * 7)
            dve.wait_ge(zeroed, 5)
            with dve.Fori(0, NC) as c:
                dve.wait_ge(mixed, U * c + 1)
                for j in range(J):
                    b = j % 2
                    dve.wait_ge(turned, J * c + j + 1)
                    dve.tensor_tensor(t2[:, b], banks[2 + b][:, 0:CT], cos_sin[:, 1], ALU.mult).then_inc(sin_done, 1)
                    dve.wait_ge(sin_done, J * c + j + 1)
                    dve.wait_ge(cos_done, J * c + j + 1)
                    if j < QT:
                        for i in range(4):
                            q = slice(32 * i, 32 * i + 32)
                            last = dve.tensor_tensor(qm[q, 4 * j + i], t1[q, b], t2[q, b], ALU.add)
                    else:
                        last = dve.tensor_tensor(kt[:, j - QT], t1[:, b], t2[:, b], ALU.add)
                    last.then_inc(roped, 1)
                for g in range(GC):
                    dve.wait_ge(v_summed, GC * c + g + 2)
                    dve.tensor_tensor(va[0:GT, g, :, 0:HD], banks[4 + g][0:GT, 0:D].rearrange("p (h d) -> p h d", h=HEADS),
                                      bv[:].rearrange("p (h d) -> p h d", h=HEADS), ALU.add).then_inc(v_stored, 1)

                def norm_context(g):
                    dve.wait_ge(mixed, U * c + QT * (g + 1) + 1)
                    heads = banks[6 + g % 2][0:GT, 0:HEADS * (HD + 1)].rearrange("p (h d) -> p h d", h=HEADS)
                    if g >= 2:
                        dve.wait_ge(ctx_turned, GC * c + g - 1)
                    dve.reciprocal(rec[:, g % 2].unsqueeze(2), heads[:, :, HD:HD + 1]).then_inc(inverted, 1)
                    dve.wait_ge(inverted, GC * c + g + 1)
                    dve.tensor_tensor(cn[0:GT, g % 2], heads[:, :, 0:HD], rec[:, g % 2].unsqueeze(2).broadcast_to([GT, HEADS, HD]),
                                      ALU.mult).then_inc(normed, 1)

                for u in range(U):
                    b = u % DEPTH
                    dve.wait_ge(scored, U * c + u + 1)
                    if u >= DEPTH:
                        dve.wait_ge(lessened, U * c + u - DEPTH + 1)
                    dve.scalar_tensor_tensor(sm[:, b], banks[u % 2][0:GT, 0:4 * GT].rearrange("p (i t) -> p i t", i=4), HD ** -0.5,
                                             consts["mask"][:].unsqueeze(1).broadcast_to([GT, 4, GT]),
                                             ALU.mult, ALU.add).then_inc(masked, 1)
                    dve.wait_ge(masked, U * c + u + 1)
                    dve.tensor_reduce(mx[:, b], sm[:, b], AX.X, ALU.max).then_inc(maxed, 1)
                    if u >= NORM and (u - NORM) % QT == 0:
                        norm_context((u - NORM) // QT)
                for g in range((U - 1 - NORM) // QT + 1, GC):
                    norm_context(g)
                for m in range(2):
                    dve.wait_ge(out_summed, 2 * c + m + 1)
                    half = stream[:, m, bass.ds(c * CT, CT)]
                    dve.scalar_tensor_tensor(half, banks[4 + m][0:DH, 0:CT], bo[:, m:m + 1], half, ALU.add, ALU.add).then_inc(added, 1)


def tokens(g):
    return slice(g * RT, min(N, (g + 1) * RT))


def size(g):
    return tokens(g).stop - tokens(g).start


def route(nc, tag, banks, consts, stream, xn, gw, gb, landed, r, slots, tiles_of, capacity):
    with ExitStack() as ctx:
        sb = lambda name, shape, dt=F32: ctx.enter_context(nc.sbuf_tensor(f"{tag}_{name}", shape, dt))
        sem = ctx.enter_context(Semaphores(nc, tag + "_"))
        lg = sb("logits", [RT, RG, E])
        top = sb("top_values", [RT, RG, 8])
        ti = sb("top_indices", [RT, RG, 8], U32)
        tf = sb("top_indices_f", [RT, RG, 2])
        is_k = [sb(f"is_expert{k}", [RT, RG, E]) for k in range(2)]
        chosen = sb("chosen", [RT, RG, E])
        less = sb("logits_less_max", [RT, RG, E])
        ex = sb("logit_exps", [RT, RG, E])
        sel = sb("chosen_exps", [RT, RG, E])
        total = sb("exp_total", [RT, RG])
        inv = sb("exp_total_inverse", [RT, RG])
        pre = [sb(f"group_prefix{u}", [RT, RG, E]) for u in range(2)]
        place = sb("place_in_expert", [RT, RG, E])
        slot = sb("slot_in_expert", [RT, RG, E])
        kept = sb("kept", [RT, RG, E])
        picked = [[sb(f"{what}_of_expert{k}", [RT, RG, E]) for k in range(2)] for what in ("slot", "kept", "exp")]
        slot_k = sb("slot_k", [RT, RG, 2])
        kept_k = sb("kept_k", [RT, RG, 2])
        exp_k = sb("exp_k", [RT, RG, 2])
        past = sb("slot_less_own_row", [RT, RG, 2])
        target_f = sb("target_f", [RT, RG, 2])
        source_f = sb("source_f", [RT, RG, 2])
        target = sb("scatter_rows", [RT, RG, 2], U32)
        if capacity is None:
            more = sb("tile_begun", [RT, E, NT])
            need = sb("tiles_needed", [RT, E])
            upto = [sb(f"tiles_upto{u}", [RT, E]) for u in range(2)]
            base = sb("expert_base", [RT, E])
            past_e = sb("tile_past_expert", [1, NT, E])
            tile_f = sb("tile_expert_f", [1, NT])
        else:
            sq = sb("row_squares", [RT, RG, D])
            ms = sb("row_square_sum", [RT, RG])
            root = sb("row_root", [RT, RG])
            rinv = sb("row_root_inverse", [RT, RG])
        logits_summed = sem("logits_summed")
        step = sem("routing_step")
        chosen_ready = sem("chosen_ready")
        counted = sem("chosen_counted")
        less_ready = sem("logits_less_max_ready")
        exped = sem("logits_exped")
        pad_zeroed = sem("row_padding_zeroed")
        row_turned = sem("row_turned")
        row_stored = sem("row_stored")
        squared = sem("rows_squared")
        eps_added = sem("row_eps_added")
        rooted = sem("rows_rooted")
        inverted = sem("row_roots_inverted")
        scaled = sem("rows_scaled")
        targets_ready = sem("targets_ready")
        scattered = sem("rows_scattered")
        block = ctx.enter_context(nc.Block())
        last_of = lambda tile, k: tile[:, :, k:k + 1].broadcast_to([RT, RG, E])
        gated = capacity is not None

        all_landed = 16 if gb is None else 32

        @block.tensor
        def _(pe):
            def turn(n):
                g = n % RG
                if n >= 4:
                    pe.wait_ge(row_stored, n - 3)
                for k in range(2):
                    mm = pe.transpose(banks[4 + n % 4][0:size(g), k * DH:(k + 1) * DH], (xn if n < RG else stream)[:, k, tokens(g)],
                                      consts["ident"][0:DH, 0:DH])
                mm.then_inc(row_turned, 1)

            def logits():
                pe.wait_ge(landed, all_landed)
                for g in range(RG):
                    for k in range(2):
                        mm = pe.matmul(banks[0][0:size(g), g * E:(g + 1) * E], xn[:, k, tokens(g)], gw[:, k], start=(k == 0), stop=(k == 1))
                mm.then_inc(logits_summed, 1)

            if not gated:
                logits()
            for n in range(RG):
                turn(n)
            if gated:
                logits()
                for n in range(RG, 2 * RG):
                    turn(n)
            pe.wait_ge(chosen_ready, 1)
            flat = chosen[:].rearrange("p g e -> p (g e)")
            pe.matmul(banks[1][0:RT, 0:RG * E], consts["before"][:], flat, start=True, stop=True)
            pe.matmul(banks[2][0:RT, 0:RG * E], consts["ones"][0:RT, 0:RT], flat, start=True, stop=True).then_inc(counted, 1)
            if not gated:
                for n in range(RG, 2 * RG):
                    turn(n)

        @block.scalar
        def _(act):
            for n in range(2 * RG):
                act.wait_ge(row_turned, n + 1)
                rows = r["x_rows"] if n < RG else r["stream_rows"]
                m = size(n % RG)
                act.activation(rows[0:m, n % RG], banks[4 + n % 4][0:m, 0:D], ACT.Copy).then_inc(row_stored, 1)
                if n == RG - 1 and gated:
                    act.wait_ge(row_stored, RG)
                    act.wait_ge(pad_zeroed, 1)
                    act.activation(sq[:], r["x_rows"][:], ACT.Square).then_inc(squared, 1)
                    act.wait_ge(eps_added, 1)
                    act.activation(root[:], ms[:], ACT.Sqrt).then_inc(rooted, 1)
                if n == (2 * RG if gated else RG) - 1:
                    act.wait_ge(less_ready, 1)
                    act.activation(ex[:], less[:], ACT.Exp).then_inc(exped, 1)
            if gated:
                act.wait_ge(inverted, 1)
                for g in range(RG):
                    act.activation(sq[:, g], r["x_rows"][:, g], ACT.Copy, scale=rinv[:, g:g + 1]).then_inc(scaled, 1)

        @block.vector
        def _(dve):
            steps = [0]

            def then(instruction):
                steps[0] += 1
                instruction.then_inc(step, 1)
                dve.wait_ge(step, steps[0])

            pad = slice(size(RG - 1), RT)
            dve.memset(r["x_rows"][pad, RG - 1], 0.0).then_inc(pad_zeroed, 1)
            then(dve.memset(lg[pad, RG - 1], 0.0))
            if gated:
                dve.wait_ge(squared, 1)
                then(dve.tensor_reduce(ms[:], sq[:], AX.X, ALU.add))
                dve.tensor_scalar(ms[:], ms[:], 4.0 / D, RMS_EPS, ALU.mult, ALU.add).then_inc(eps_added, 1)
                dve.wait_ge(rooted, 1)
                then(dve.reciprocal(rinv[:], root[:]))
                dve.tensor_scalar(rinv[:], rinv[:], 2.0, None, ALU.mult).then_inc(inverted, 1)
            dve.wait_ge(landed, all_landed)
            dve.wait_ge(logits_summed, 1)
            for rows, gs in ((slice(0, RT), slice(0, RG - 1)), (slice(0, size(RG - 1)), slice(RG - 1, RG))):
                summed = banks[0][rows, gs.start * E:gs.stop * E].rearrange("p (g e) -> p g e", e=E)
                if gb is None:
                    last = dve.tensor_copy(lg[rows, gs], summed)
                else:
                    bias = gb[rows].unsqueeze(1).broadcast_to([rows.stop, gs.stop - gs.start, E])
                    last = dve.tensor_tensor(lg[rows, gs], summed, bias, ALU.add)
            then(last)
            for g in range(RG):
                last = dve.max(top[:, g], lg[:, g])
            then(last)
            dve.tensor_tensor(less[:], lg[:], last_of(top, 0), ALU.subtract).then_inc(less_ready, 1)
            for g in range(RG):
                last = dve.max_index(ti[:, g], top[:, g], lg[:, g])
            then(last)
            then(dve.tensor_copy(tf[:], ti[:, :, 0:2]))
            names = consts["counting"][:, 0:E].unsqueeze(1).broadcast_to([RT, RG, E])
            dve.tensor_tensor(is_k[0][:], names, last_of(tf, 0), ALU.is_equal)
            then(dve.tensor_tensor(is_k[1][:], names, last_of(tf, 1), ALU.is_equal))
            then(dve.tensor_tensor(chosen[:], is_k[0][:], is_k[1][:], ALU.add))
            dve.memset(chosen[pad, RG - 1], 0.0).then_inc(chosen_ready, 1)
            dve.wait_ge(chosen_ready, 1)
            dve.wait_ge(exped, 1)
            then(dve.tensor_tensor(sel[:], ex[:], chosen[:], ALU.mult))
            then(dve.tensor_reduce(total[:], (sel if gated else ex)[:], AX.X, ALU.add))
            then(dve.memset(total[pad, RG - 1:RG], 1.0))
            then(dve.reciprocal(inv[:], total[:]))
            dve.wait_ge(counted, 1)
            totals = banks[2][0:RT, 0:RG * E].rearrange("p (g e) -> p g e", e=E)
            dve.memset(pre[0][:, 0:1], 0.0)
            then(dve.tensor_copy(pre[0][:, 1:RG], totals[:, 0:RG - 1]))
            shift, u = 1, 0
            while shift < RG:
                dve.tensor_copy(pre[1 - u][:, 0:shift], pre[u][:, 0:shift])
                then(dve.tensor_tensor(pre[1 - u][:, shift:RG], pre[u][:, shift:RG], pre[u][:, 0:RG - shift], ALU.add))
                shift, u = 2 * shift, 1 - u
            within = banks[1][0:RT, 0:RG * E].rearrange("p (g e) -> p g e", e=E)
            then(dve.tensor_tensor(place[:], pre[u][:], within, ALU.add))
            if gated:
                then(dve.tensor_scalar(kept[:], place[:], float(capacity), None, ALU.is_lt))
                starts = consts["expert_starts"][:].unsqueeze(1)
            else:
                then(dve.tensor_tensor(base[:].unsqueeze(1), pre[u][:, RG - 1:RG], totals[:, RG - 1:RG], ALU.add))
                then(dve.tensor_tensor(more[:], base[:].unsqueeze(2).broadcast_to([RT, E, NT]),
                                       consts["tile_starts"][:].unsqueeze(1).broadcast_to([RT, E, NT]), ALU.is_gt))
                then(dve.tensor_reduce(need[:], more[:], AX.X, ALU.add))
                then(dve.tensor_copy(upto[0][:], need[:]))
                shift, u = 1, 0
                while shift < E:
                    dve.tensor_copy(upto[1 - u][:, 0:shift], upto[u][:, 0:shift])
                    then(dve.tensor_tensor(upto[1 - u][:, shift:E], upto[u][:, shift:E], upto[u][:, 0:E - shift], ALU.add))
                    shift, u = 2 * shift, 1 - u
                dve.tensor_tensor(past_e[:], upto[u][0:1].unsqueeze(1).broadcast_to([1, NT, E]),
                                  consts["counting"][0:1].unsqueeze(2).broadcast_to([1, NT, E]), ALU.is_le)
                then(dve.tensor_tensor(need[:], upto[u][:], need[:], ALU.subtract))
                dve.tensor_reduce(tile_f[:], past_e[:], AX.X, ALU.add)
                then(dve.tensor_scalar(base[:], need[:], float(TS), None, ALU.mult))
                then(dve.tensor_scalar(tile_f[:], tile_f[:], float(E - 1), None, ALU.min))
                dve.tensor_copy(tiles_of[:], tile_f[:])
                starts = base[:].unsqueeze(1)
            then(dve.tensor_tensor(slot[:], place[:], starts.broadcast_to([RT, RG, E]), ALU.add))
            for k in range(2):
                dve.tensor_tensor(picked[0][k][:], slot[:], is_k[k][:], ALU.mult)
                if gated:
                    dve.tensor_tensor(picked[1][k][:], kept[:], is_k[k][:], ALU.mult)
                last = dve.tensor_tensor(picked[2][k][:], sel[:], is_k[k][:], ALU.mult)
            then(last)
            for k in range(2):
                dve.tensor_reduce(slot_k[:, :, k], picked[0][k][:], AX.X, ALU.add)
                if gated:
                    dve.tensor_reduce(kept_k[:, :, k], picked[1][k][:], AX.X, ALU.add)
                last = dve.tensor_reduce(exp_k[:, :, k], picked[2][k][:], AX.X, ALU.add)
            then(last)
            if gated:
                then(dve.tensor_tensor(past[:], slot_k[:], consts["own_rows"][:], ALU.subtract))
                then(dve.tensor_tensor(past[:], past[:], kept_k[:], ALU.mult))
                dve.tensor_tensor(target_f[:], past[:], consts["own_rows"][:], ALU.add)
                then(dve.tensor_tensor(source_f[:], slot_k[:], kept_k[:], ALU.mult))
                then(dve.tensor_copy(target[:], target_f[:]))
                dve.tensor_copy(r["source"][:], source_f[:])
                then(dve.tensor_tensor(exp_k[:], exp_k[:], kept_k[:], ALU.mult))
            else:
                dve.tensor_copy(r["source"][:], slot_k[:])
                then(dve.tensor_copy(target[:], slot_k[:]))
            then(dve.tensor_tensor(r["weights"][:], exp_k[:], inv[:].unsqueeze(2).broadcast_to([RT, RG, 2]), ALU.mult))
            if gated:
                then(dve.tensor_tensor(r["weight_sum"][:].unsqueeze(2), r["weights"][:, :, 0:1], r["weights"][:, :, 1:2], ALU.add))
            dve.wait_ge(step, steps[0])
            dve.sem_inc(targets_ready, 1)

        @block.gpsimd
        def _(pool):
            pool.wait_ge(targets_ready, 1)
            pool.wait_ge(row_stored, RG)
            for g in range(RG):
                if gated:
                    pool.wait_ge(scaled, g + 1)
                for k in range(2):
                    pool.indirect_dma_start(slots, bass.IndirectOffsetOnAxis(target[0:size(g), g, k:k + 1], 0),
                                            (sq if gated else r["x_rows"])[0:size(g), g], None).then_inc(scattered, 16)
            pool.wait_ge(scattered, 16 * 2 * RG)


def gated_experts(nc, banks, consts, slots, results, w_in, w_out, norm_w):
    CG = CAP // SP
    tiles = H0 // 128
    with ExitStack() as ctx:
        sb = lambda name, shape, dt=F32: ctx.enter_context(nc.sbuf_tensor(f"moe0_{name}", shape, dt))
        sem = ctx.enter_context(Semaphores(nc, "moe0_"))
        wi = [sb(f"expert_in{u}", [DH, 2, 2 * H0]) for u in range(2)]
        wo = [sb(f"expert_out{u}", [128, tiles, D]) for u in range(2)]
        nw = sb("expert_norms", [DH, E, 2])
        rows = [sb(f"slot_rows{u}", [SP, CG, D]) for u in range(2)]
        xt = [sb(f"slot_inputs{u}", [DH, 2, CAP]) for u in range(2)]
        silu = sb("gate_silu", [128, 2, CAP])
        hid = [sb(f"expert_hidden{u}", [128, tiles, CAP]) for u in range(2)]
        ys = [sb(f"expert_results{u}", [SP, CG, D]) for u in range(2)]
        norms_landed = sem("expert_norms_landed")
        w_landed = [sem(f"expert{u}_landed") for u in range(2)]
        rows_landed = [sem(f"slot_rows{u}_landed") for u in range(2)]
        turned, inputs_ready = sem("slots_turned"), sem("slot_inputs_ready")
        first_summed, silued, hid_ready = sem("hidden_summed"), sem("gate_silued"), sem("hidden_ready")
        second_summed = sem("results_summed")
        results_stored = sem("results_stored")
        written = [sem(f"results{u}_written") for u in range(2)]
        block = ctx.enter_context(nc.Block())
        PG = 2
        R = CG // PG
        rows_of = lambda ap, e: ap[e * CAP:(e + 1) * CAP].rearrange("(g p) d -> p g d", p=SP)

        @block.sync
        def _(sp):
            sp.dma_start(nw[:], norm_w).then_inc(norms_landed, 16)
            for e in range(E):
                u = e % 2
                if e >= 2:
                    sp.wait_ge(second_summed, R * (e - 1))
                sp.dma_start(rows[u][:], rows_of(slots, e)).then_inc(rows_landed[u], 16)
                sp.dma_start(wi[u][:], w_in[e]).then_inc(w_landed[u], 16)
                sp.dma_start(wo[u][:], w_out[e]).then_inc(w_landed[u], 16)

        @block.tensor
        def _(pe):
            def turn(e):
                pe.wait_ge(rows_landed[e % 2], 16 * (e // 2 + 1))
                for k in range(2):
                    if e >= 1:
                        pe.wait_ge(inputs_ready, 2 * (e - 1) + k + 1)
                    for g in range(CG):
                        mm = pe.transpose(banks[4 + k][0:DH, g * SP:(g + 1) * SP], rows[e % 2][:, g, k * DH:(k + 1) * DH],
                                          consts["ident"][0:SP, 0:SP])
                    mm.then_inc(turned, 1)

            def second(e, r):
                if r == 0:
                    pe.wait_ge(hid_ready, tiles * (e + 1))
                if R * e + r >= 2:
                    pe.wait_ge(results_stored, R * e + r - 1)
                for g in range(r * PG, (r + 1) * PG):
                    for h in range(tiles):
                        mm = pe.matmul(banks[6 + r % 2][0:SP, (g % PG) * D:(g % PG + 1) * D], hid[e % 2][:, h, g * SP:(g + 1) * SP],
                                       wo[e % 2][:, h], start=(h == 0), stop=(h == tiles - 1))
                mm.then_inc(second_summed, 1)

            turn(0)
            for e in range(E):
                pe.wait_ge(inputs_ready, 2 * e + 2)
                pe.wait_ge(w_landed[e % 2], 32 * (e // 2 + 1))
                for h in range(tiles):
                    n = e * tiles + h
                    if n >= 2:
                        pe.wait_ge(hid_ready, n - 1)
                    for part in range(2):
                        o = part * H0 + h * 128
                        for k in range(2):
                            mm = pe.matmul(banks[2 * (n % 2) + part][:, 0:CAP], wi[e % 2][:, k, o:o + 128], xt[e % 2][:, k],
                                           start=(k == 0), stop=(k == 1))
                    mm.then_inc(first_summed, 1)
                    if h == 1 and e >= 1:
                        for r in range(R):
                            second(e - 1, r)
                if e + 1 < E:
                    turn(e + 1)
            for r in range(R):
                second(E - 1, r)

        @block.scalar
        def _(act):
            def inputs(e):
                for k in range(2):
                    act.wait_ge(turned, 2 * e + k + 1)
                    act.activation(xt[e % 2][:, k], banks[4 + k][0:DH, 0:CAP], ACT.Copy, scale=nw[:, e, k:k + 1]).then_inc(inputs_ready, 1)

            act.wait_ge(norms_landed, 16)
            inputs(0)
            for e in range(E):
                for h in range(tiles):
                    n = e * tiles + h
                    act.wait_ge(first_summed, n + 1)
                    if n >= 2:
                        act.wait_ge(hid_ready, n - 1)
                    act.activation(silu[:, n % 2], banks[2 * (n % 2)][:, 0:CAP], ACT.Silu).then_inc(silued, 1)
                if e + 1 < E:
                    inputs(e + 1)

        @block.vector
        def _(dve):
            def keep(e, r):
                dve.wait_ge(second_summed, R * e + r + 1)
                if e >= 2 and r == 0:
                    dve.wait_ge(written[e % 2], 16 * (e // 2))
                dve.tensor_copy(ys[e % 2][:, r * PG:(r + 1) * PG], banks[6 + r % 2][0:SP, 0:PG * D].rearrange("p (g d) -> p g d", g=PG)).then_inc(results_stored, 1)

            for e in range(E):
                for h in range(tiles):
                    n = e * tiles + h
                    if h == 0 and e >= 2:
                        dve.wait_ge(second_summed, R * (e - 1))
                    dve.wait_ge(silued, n + 1)
                    dve.tensor_tensor(hid[e % 2][:, h], silu[:, n % 2], banks[2 * (n % 2) + 1][:, 0:CAP], ALU.mult).then_inc(hid_ready, 1)
                    if h == 2 and e >= 1:
                        for r in range(R):
                            keep(e - 1, r)
            for r in range(R):
                keep(E - 1, r)

        @block.gpsimd
        def _(pool):
            for e in range(E):
                pool.wait_ge(results_stored, R * (e + 1))
                pool.dma_start(rows_of(results, e), ys[e % 2][:]).then_inc(written[e % 2], 16)
            for u in range(2):
                pool.wait_ge(written[u], 16 * E // 2)


def over_tiles(eng, body):
    for t in range(2):
        body(t, t, 0)
    with eng.Fori(0, NT // 2 - 2) as i:
        for u in range(2):
            body(2 * i + 2 + u, u, i + 1)
    for t in range(NT - 2, NT):
        body(t, t % 2, t // 2)


def start_loads(nc, loads):
    with nc.Block() as block:
        @block.sync
        def _(sp):
            for dst, src, landed in loads:
                sp.dma_start(dst[:], src).then_inc(landed, 16)


def tiled_experts(nc, banks, consts, slots, results, tiles_of, w, weights_landed):
    tiles = H1 // 128
    with ExitStack() as ctx:
        sb = lambda name, shape, dt=F32: ctx.enter_context(nc.sbuf_tensor(f"moe1_{name}", shape, dt))
        sem = ctx.enter_context(Semaphores(nc, "moe1_"))
        two = lambda name, shape: [sb(f"{name}{u}", shape) for u in range(2)]
        wi = two("tile_in", [DH, 2, H1])
        bi = two("tile_b_in", [128, tiles])
        wo = two("tile_out", [128, tiles, D])
        rows, xt = two("slot_rows", [TS, D]), two("slot_inputs", [DH, 2, TS])
        hid, ys = two("tile_hidden", [128, tiles, TS]), two("tile_results", [TS, D])
        rows_landed = [sem(f"slot_rows{u}_landed") for u in range(2)]
        turned, inputs_ready = sem("slots_turned"), sem("slot_inputs_ready")
        in_staged, out_staged = sem("in_weights_staged"), sem("out_weights_staged")
        first_summed, hid_ready = sem("hidden_summed"), sem("hidden_ready")
        second_summed, results_stored = sem("results_summed"), sem("results_stored")
        written = [sem(f"results{u}_written") for u in range(2)]
        block = ctx.enter_context(nc.Block())
        FIRST = 4
        known = lambda t: isinstance(t, int)
        is_last = lambda t: known(t) and t == NT - 1

        @block.sync
        def _(sp):
            def load(t, u):
                sp.dma_start(rows[u][:], slots[bass.ds(t * TS, TS)]).then_inc(rows_landed[u], 16)

            def write(t, u):
                sp.wait_ge(results_stored, t + 2)
                sp.dma_start(results[bass.ds(t * TS, TS)], ys[u][:]).then_inc(written[u], 16)

            def body(t, u, half):
                if not is_last(t):
                    if not (known(t) and t < 1):
                        sp.wait_ge(turned, t)
                    load(t + 1, 1 - u)
                if not (known(t) and t < 2):
                    write(t - 2, u)

            load(0, 0)
            over_tiles(sp, body)
            for t in range(NT - 2, NT):
                write(t, t % 2)
            for u in range(2):
                sp.wait_ge(written[u], 16 * NT // 2)

        @block.tensor
        def _(pe):
            start_at_one(pe, second_summed)

            def turn(t, u, half):
                pe.wait_ge(rows_landed[u], 16 * half + 16)
                if not (known(t) and t < 2):
                    pe.wait_ge(inputs_ready, t - 1)
                for k in range(2):
                    mm = pe.transpose(banks[4 + u][0:DH, k * TS:(k + 1) * TS], rows[u][:, k * DH:(k + 1) * DH], consts["ident"][:])
                mm.then_inc(turned, 1)

            def second(t, u):
                pe.wait_ge(hid_ready, 2 * t + 2)
                pe.wait_ge(out_staged, t + 1)
                if not (known(t) and t < 2):
                    pe.wait_ge(results_stored, t)
                for h in range(tiles):
                    mm = pe.matmul(banks[6 + u][:, 0:D], hid[u][:, h], wo[u][:, h], start=(h == 0), stop=(h == tiles - 1))
                mm.then_inc(second_summed, 1)

            def body(t, u, half):
                pe.wait_ge(inputs_ready, t + 1)
                pe.wait_ge(in_staged, t + 1)
                if not (known(t) and t < 2):
                    pe.wait_ge(hid_ready, 2 * t - 2)
                for h in range(tiles):
                    for k in range(2):
                        mm = pe.matmul(banks[2 * u + h // FIRST][:, h % FIRST * TS:(h % FIRST + 1) * TS], wi[u][:, k, h * 128:(h + 1) * 128],
                                       xt[u][:, k], start=(k == 0), stop=(k == 1))
                    if h in (FIRST - 1, tiles - 1):
                        mm.then_inc(first_summed, 1)
                if not is_last(t):
                    turn(t + 1, 1 - u, half + u)
                if not (known(t) and t < 1):
                    second(t - 1, 1 - u)

            turn(0, 0, 0)
            over_tiles(pe, body)
            second(NT - 1, (NT - 1) % 2)

        @block.scalar
        def _(act):
            def inputs(t, u):
                act.wait_ge(turned, t + 1)
                act.activation(xt[u][:].rearrange("p k t -> p (k t)"), banks[4 + u][0:DH, 0:2 * TS], ACT.Copy).then_inc(inputs_ready, 1)

            def body(t, u, half):
                for part, hs in enumerate((range(FIRST), range(FIRST, tiles))):
                    act.wait_ge(first_summed, 2 * t + part + 1)
                    if part == 0 and not (known(t) and t < 2):
                        act.wait_ge(second_summed, t)
                    for h in hs:
                        last = act.activation(hid[u][:, h], banks[2 * u + part][:, h % FIRST * TS:(h % FIRST + 1) * TS], ACT.Gelu, bias=bi[u][:, h:h + 1])
                    last.then_inc(hid_ready, 1)
                if not is_last(t):
                    inputs(t + 1, 1 - u)

            inputs(0, 0)
            over_tiles(act, body)

        @block.vector
        def _(dve):
            start_at_one(dve, results_stored)

            def expert_of(t):
                return dve.value_load(tiles_of[0:1, bass.ds(t, 1)], min_val=0, max_val=E - 1)

            def stage_in(t, u, e):
                if not (known(t) and t < 2):
                    dve.wait_ge(first_summed, 2 * t - 2)
                    dve.wait_ge(hid_ready, 2 * t - 2)
                dve.tensor_scalar(bi[u][:].unsqueeze(1), w["b_in"][:, bass.ds(e, 1)], 1.0, None, ALU.mult)
                dve.tensor_scalar(wi[u][:].unsqueeze(1), w["in"][:, bass.ds(e, 1)], 1.0, None, ALU.mult).then_inc(in_staged, 1)

            def stage_out(t, u, e):
                if not (known(t) and t < 2):
                    dve.wait_ge(second_summed, t)
                dve.tensor_scalar(wo[u][:].unsqueeze(1), w["out"][:, bass.ds(e, 1)], 1.0, None, ALU.mult).then_inc(out_staged, 1)

            def keep(t, u, half):
                e = expert_of(t)
                dve.wait_ge(second_summed, t + 2)
                if not (known(t) and t < 2):
                    dve.wait_ge(written[u], 16 * half)
                dve.tensor_tensor(ys[u][:].unsqueeze(1), banks[6 + u][:, 0:D].unsqueeze(1), w["b_out"][:, bass.ds(e, 1)], ALU.add).then_inc(results_stored, 1)

            def body(t, u, half):
                if not is_last(t):
                    e = expert_of(t + 1)
                    stage_in(t + 1, 1 - u, e)
                if not (known(t) and t < 1):
                    keep(t - 1, 1 - u, half if u else half - 1)
                if not is_last(t):
                    stage_out(t + 1, 1 - u, e)

            dve.wait_ge(weights_landed, 16 * 4)
            e = expert_of(0)
            stage_in(0, 0, e)
            stage_out(0, 0, e)
            over_tiles(dve, body)
            keep(NT - 1, (NT - 1) % 2, (NT - 1) // 2)


def combine(nc, tag, banks, consts, stream, r, results, resid=None, out=None):
    with ExitStack() as ctx:
        sb = lambda name, shape, dt=F32: ctx.enter_context(nc.sbuf_tensor(f"{tag}_{name}", shape, dt))
        sem = ctx.enter_context(Semaphores(nc, tag + "_"))
        got = sb("gathered", [RT, RG, 2, D])
        gathered = [[sem(f"gathered{k}_{g}") for k in range(2)] for g in range(RG)]
        step = sem("combine_step")
        combined = sem("rows_combined")
        written = sem("out_written")
        if out is None:
            stats = sb("row_stats", [RT, RG, 6])
            moments = sb("row_moments", [RT, RG, 2])
            ve = sb("row_var_eps", [RT, RG])
            root = sb("row_root", [RT, RG])
            inv = sb("row_root_inverse", [RT, RG])
            rows_normed = sb("rows_normed", [RT, RG, D])
            eps_added, rooted, normed = sem("row_eps_added"), sem("rows_rooted"), sem("rows_normed_ready")
            turned, stream_stored = sem("combined_turned"), sem("stream_stored")
        block = ctx.enter_context(nc.Block())

        @block.gpsimd
        def _(pool):
            for g in range(RG):
                for k in range(2):
                    pool.indirect_dma_start(got[0:size(g), g, k], None, results, bass.IndirectOffsetOnAxis(r["source"][0:size(g), g, k:k + 1], 0)).then_inc(gathered[g][k], 16)

        @block.vector
        def _(dve):
            steps = [0]

            def then(instruction):
                steps[0] += 1
                instruction.then_inc(step, 1)
                dve.wait_ge(step, steps[0])

            def normalise(g):
                m = size(g)
                dve.wait_ge(rooted, g + 1)
                then(dve.reciprocal(inv[0:m, g:g + 1], root[0:m, g:g + 1]))
                dve.tensor_scalar(rows_normed[0:m, g], r["stream_rows"][0:m, g], moments[0:m, g, 0:1], inv[0:m, g:g + 1],
                                  ALU.subtract, ALU.mult).then_inc(normed, 1)

            for g in range(RG):
                m = size(g)
                rows = r["stream_rows"][0:m, g]
                if "weight_sum" in r:
                    then(dve.scalar_tensor_tensor(rows, r["x_rows"][0:m, g], r["weight_sum"][0:m, g:g + 1], rows, ALU.mult, ALU.add))
                dve.wait_ge(gathered[g][0], 16)
                then(dve.scalar_tensor_tensor(rows, got[0:m, g, 0], r["weights"][0:m, g, 0:1], rows, ALU.mult, ALU.add))
                dve.wait_ge(gathered[g][1], 16)
                dve.scalar_tensor_tensor(rows, got[0:m, g, 1], r["weights"][0:m, g, 1:2], rows, ALU.mult, ALU.add).then_inc(combined, 1)
                if out is None:
                    dve.wait_ge(combined, g + 1)
                    then(dve.bn_stats(stats[0:m, g], rows))
                    then(dve.bn_aggr(moments[0:m, g], stats[0:m, g]))
                    dve.tensor_scalar(ve[0:m, g:g + 1], moments[0:m, g, 1:2], LN_EPS, None, ALU.add).then_inc(eps_added, 1)
                    if g >= 1:
                        normalise(g - 1)
            if out is None:
                normalise(RG - 1)

        if out is None:
            def piece(q):
                return slice(q * RQ * RT, min(N, (q + 1) * RQ * RT))

            @block.tensor
            def _(pe):
                def turn(q, rows, ready):
                    for g in range(q * RQ, (q + 1) * RQ):
                        pe.wait_ge(ready, g + 1)
                        m = size(g)
                        for k in range(2):
                            mm = pe.transpose(banks[q + 4 * k][0:DH, (g % RQ) * RT:(g % RQ) * RT + m], rows[0:m, g, k * DH:(k + 1) * DH],
                                              consts["ident"][0:m, 0:m])
                    mm.then_inc(turned, 1)

                for q in range(RG // RQ):
                    turn(q, r["stream_rows"], combined)
                    if q >= 1:
                        pe.wait_ge(stream_stored, q)
                        turn(q - 1, rows_normed, normed)
                pe.wait_ge(stream_stored, RG // RQ)
                turn(RG // RQ - 1, rows_normed, normed)

            @block.scalar
            def _(act):
                def keep(q, n, dst):
                    act.wait_ge(turned, n + 1)
                    for k in range(2):
                        last = act.activation(dst[:, k, piece(q)], banks[q + 4 * k][0:DH, 0:piece(q).stop - piece(q).start], ACT.Copy)
                    return last

                Q = RG // RQ
                for q in range(Q):
                    for g in range(q * RQ, (q + 1) * RQ):
                        m = size(g)
                        act.wait_ge(eps_added, g + 1)
                        act.activation(root[0:m, g:g + 1], ve[0:m, g:g + 1], ACT.Sqrt).then_inc(rooted, 1)
                    keep(q, max(0, 2 * q - 1), stream).then_inc(stream_stored, 1)
                    if q >= 1:
                        keep(q - 1, 2 * q, resid)
                keep(Q - 1, 2 * Q - 1, resid)
        else:
            @block.sync
            def _(sp):
                flat = out.rearrange("b t d -> (b t) d")
                for q in range(RG // RQ):
                    sp.wait_ge(combined, RQ * (q + 1))
                    whole = range(q * RQ, min(RG - 1, (q + 1) * RQ))
                    sp.dma_start(flat[whole.start * RT:whole.stop * RT].rearrange("(g p) d -> p g d", p=RT),
                                 r["stream_rows"][:, whole.start:whole.stop]).then_inc(written, 16)
                sp.dma_start(flat[tokens(RG - 1)], r["stream_rows"][0:size(RG - 1), RG - 1]).then_inc(written, 16)
                sp.wait_ge(written, 16 * (RG // RQ + 1))


AT = {
    "mean": 0, "sum squares": 1, "spread": 4, "project": (7, 7, 8, 9, 9, 10), "x": 11, "dt": (11, 12, 12),
    "project out": 14,
    "square": 1, "root": 3, "affine": 6, "store": (7, 7, 8, 9, 9, 10), "first tap": (7, 8, 8), "silus": 10,
    "low rank": 10, "store mid": 13, "soften": 12, "log": 14,
    "centre": 0, "eps": 2, "scale": 5, "convolve": (8, 8, 9), "split": 10, "plus one": 13,
    "finish": 14, "mixed": 15, "skip": 2,
    "gate": 5,
}


def state_space(nc, banks, consts, resid, params_in, params_conv, dt_w, params_out, a_log):
    with ExitStack() as ctx:
        sb = lambda name, shape, dt=F32: ctx.enter_context(nc.sbuf_tensor(name, shape, dt))
        sem = ctx.enter_context(Semaphores(nc))
        in_p = sb("layer_in", [DH, 2 * 2 * DI + 4])
        in_w = in_p[:, 0:4 * DI].rearrange("p (k e) -> p k e", k=2)
        norm_w, norm_b = in_p[:, 4 * DI:4 * DI + 2], in_p[:, 4 * DI + 2:4 * DI + 4]
        conv_p = sb("layer_conv", [128, DT3 * (DCONV + 2 + 2 * DS + DTR)])
        o = DT3 * DCONV
        conv_w = conv_p[:, 0:o].rearrange("p (d k) -> p d k", d=DT3)
        conv_b, dt_b = conv_p[:, o:o + DT3], conv_p[:, o + DT3:o + 2 * DT3]
        x_w = conv_p[:, o + 2 * DT3:].rearrange("p (d e) -> p d e", d=DT3)
        dtw = sb("layer_dt_w", [DH, DI])
        out_p = sb("layer_out", [128, DT3 * (1 + D)])
        skip, out_w = out_p[:, 0:DT3], out_p[:, DT3:].rearrange("p (d e) -> p d e", d=DT3)
        a_exp = sb("a_exp_layers", [128, LAYERS, DT3 * DS])
        a_neg = sb("a_neg", [128, DT3 * DS])
        xc = sb("ss_xc", [DH, 2, CT])
        sq = sb("ss_sq", [DH, 2, CT])
        xn = sb("ss_xn", [DH, 2, CT])
        un = sb("ss_un", [DH, 2, CT])
        padded = sb("conv_in", [128, DT3, CB, T + DCONV - 1])
        conv = sb("conv_sum", [128, DT3, CT])
        xa = sb("conv_silu", [128, 2, DT3, CT])
        zs = sb("gate_silu_z", [128, 2, DT3, CT])
        dtr = sb("dt_low_rank", [DH, CT])
        rest = sb("bc_rest", [2 * DS, CT])
        mid = sb("bc_mid", [2 * DS, CT], BF16)
        bc = sb("bc_parts", [3 * 2 * DS, 2, CT], BF16)
        xb = sb("dt_in", [128, DT3, CT])
        eb = sb("dt_exp", [128, DT3, CT])
        ub = conv
        lost = sb("dt_rounding", [128, DT3, CT])
        dt = sb("dt", [128, 2, DT3, CT])
        dtx = sb("dt_x", [128, 2, DT3, CT])
        DEEP = 4
        da = sb("decay", [128, DEEP, DT3, CB, T])
        dbx = sb("state_in", [128, DEEP, DT3 * CT])
        hs = sb("states", [128, DEEP, DT3 * CT])
        cs = sb("c_repeated", [128, DEEP, CT])
        prod = sb("c_states", [128, DEEP, DT3 * CT])
        yg = sb("y", [128, DT3, CT])
        norm = Norm(nc, sb, sem, "ss", consts, banks[6], banks[7], banks[6])
        in_landed = sem("layer_in_landed")
        out_landed = sem("layer_out_landed")
        a_landed = sem("a_landed")
        a_exped = sem("a_exped")
        a_ready = sem("a_ready")
        zeroed = sem("ss_zeroed")
        affined = sem("norm_affined")
        in_summed = sem("in_summed")
        in_stored = sem("in_stored")
        tap0 = sem("conv_tap0")
        tapped = sem("conv_tapped")
        conv_silued = sem("conv_silued")
        z_silued = sem("z_silued")
        x_summed = sem("x_proj_summed")
        dtr_stored = sem("dt_low_rank_stored")
        bc_step = sem("bc_step")
        bc_mid_stored = sem("bc_mid_stored")
        low_rank_zeroed = sem("low_rank_zeroed")
        dt_summed = sem("dt_summed")
        dt_stored = sem("dt_in_stored")
        dt_absed = sem("dt_absed")
        dt_exped = sem("dt_exped")
        dt_one = sem("dt_plus_one")
        dt_lost = sem("dt_rounding_ready")
        dt_logged = sem("dt_logged")
        dt_fixed = sem("dt_log_fixed")
        dt_ready = sem("dt_ready")
        dtx_ready = sem("dtx_ready")
        b_spread = sem("b_spread")
        c_spread = sem("c_spread")
        c_stored = sem("c_stored")
        decayed = sem("decay_ready")
        fed = sem("state_in_ready")
        scanned = sem("scanned")
        produced = sem("c_states_ready")
        reduced = sem("c_states_summed")
        skipped = sem("y_skip_ready")
        gated = sem("y_gated_ready")
        out_summed = sem("mixer_summed")
        added = sem("mixer_added")
        block = ctx.enter_context(nc.Block())
        LAG = 3
        LEAD = 1
        Z = 2 * DT3

        def all_chunks(eng, chunk_program):
            chunk_program(0, 0, 0)
            with eng.Fori(0, LAYERS - 1) as l:
                for c in range(1, NC):
                    chunk_program(NC * l + c, l, c)
                chunk_program(NC * l + NC, l + 1, 0)
            for c in range(1, NC):
                chunk_program(NC * (LAYERS - 1) + c, LAYERS - 1, c)

        def is_first(n):
            return isinstance(n, int) and n == 0

        def is_early(n):
            return isinstance(n, int) and n <= 1

        def is_last(n):
            return isinstance(n, int) and n == NC * LAYERS - 1

        @block.sync
        def _(sp):
            sp.dma_start(in_p[:], params_in[0]).then_inc(in_landed, 16)
            sp.dma_start(conv_p[:], params_conv[0]).then_inc(in_landed, 16)
            sp.wait_ge(low_rank_zeroed, 2)
            sp.dma_start(dtw[2 * DS:2 * DS + DTR, :], dt_w[0]).then_inc(in_landed, 16)
            sp.dma_start(a_exp[:], a_log).then_inc(a_landed, 16)
            sp.dma_start(out_p[:], params_out[0]).then_inc(out_landed, 16)
            with sp.Fori(1, LAYERS) as l:
                layer = lambda w: w[bass.ds(l, 1)].rearrange("a p c -> (a p) c")
                sp.wait_ge(dt_stored, DT3 * NC * l + 1)
                sp.dma_start(in_p[:], layer(params_in)).then_inc(in_landed, 16)
                sp.dma_start(conv_p[:], layer(params_conv)).then_inc(in_landed, 16)
                sp.dma_start(dtw[2 * DS:2 * DS + DTR, :], layer(dt_w)).then_inc(in_landed, 16)
                sp.wait_ge(added, NC * l + 1)
                sp.dma_start(out_p[:], layer(params_out)).then_inc(out_landed, 16)

        @block.tensor
        def _(pe):
            start_at_one(pe, dt_summed, in_summed, out_summed, reduced)

            def project_in(n, l, m):
                if m == 0:
                    pe.wait_ge(in_landed, 48 * l + 48)
                    pe.wait_ge(affined, n + 1)
                if m >= 2:
                    pe.wait_ge(in_stored, Z * n + m - 1)
                for k in range(2):
                    mm = pe.matmul(banks[6 + m % 2][:, 0:CT], in_w[:, k, m * 128:(m + 1) * 128], un[:, k], start=(k == 0), stop=(k == 1))
                mm.then_inc(in_summed, 1)

            def project_x(n, c):
                pe.wait_ge(in_stored, Z * n + Z)
                pe.wait_ge(conv_silued, n + 1)
                for d in range(DT3):
                    mm = pe.matmul(banks[6][0:2 * DS + DTR, 0:CT], x_w[:, d], xa[:, c % 2, d], start=(d == 0), stop=(d == DT3 - 1))
                mm.then_inc(x_summed, 1)

            def project_dt(n, d):
                if d == 0:
                    pe.wait_ge(dtr_stored, n + 1)
                if d == 1:
                    pe.wait_ge(bc_step, 4 * n + 2)
                if d == 2:
                    pe.wait_ge(dt_stored, DT3 * n + 2)
                pe.matmul(banks[7 - d % 2][:, 0:CT], dtw[:, d * 128:(d + 1) * 128], dtr[:], start=True,
                          stop=True).then_inc(dt_summed, 1)

            def start(n, l, c, s):
                if s == AT["mean"]:
                    pe.wait_ge(dt_stored, DT3 * n + 1)
                    if not is_early(n):
                        pe.wait_ge(added, n - 1)
                    norm.pe_mean(pe, chunk(resid, c))
                if s == AT["sum squares"]:
                    norm.pe_square(pe, n, sq)
                if s == AT["spread"]:
                    norm.pe_spread(pe, n)
                for m in range(Z):
                    if s == AT["project"][m]:
                        project_in(n, l, m)
                if s == AT["x"]:
                    project_x(n, c)
                for d in range(DT3):
                    if s == AT["dt"][d]:
                        project_dt(n, d)

            def project_out(n, l):
                pe.wait_ge(gated, n + 1)
                pe.wait_ge(out_landed, 16 * l + 16)
                if is_last(n) or is_last(n + 1):
                    pe.wait_ge(added, n + 1)
                else:
                    pe.wait_ge(dt_stored, DT3 * (n + 3) + 1)
                for k in range(2):
                    for d in range(DT3):
                        mm = pe.matmul(banks[6 + k][0:DH, 0:CT], out_w[:, d, k * DH:(k + 1) * DH], yg[:, d], start=(d == 0), stop=(d == DT3 - 1))
                mm.then_inc(out_summed, 1)

            def spread_b(n, c, s):
                if s == 0:
                    pe.wait_ge(bc_step, 4 * n + 4)
                    pe.wait_ge(bc_mid_stored, n + 1)
                if not (is_first(n) and s < 2):
                    pe.wait_ge(fed, DS * n + s - 1)
                pe.matmul(banks[3 + s % 2][:, 0:CT], consts["spread"][:, s], bc[:, c % 2], start=True, stop=True).then_inc(b_spread, 1)

            def spread_c(n, c, s):
                if not (is_first(n) and s == 0):
                    pe.wait_ge(c_stored, DS * n + s)
                pe.matmul(banks[5][:, 0:CT], consts["spread"][:, DS + s], bc[:, c % 2], start=True, stop=True).then_inc(c_spread, 1)

            def reduce(n, s):
                if s == 0:
                    pe.wait_ge(skipped, DT3 * n + 1)
                pe.wait_ge(produced, DS * n + s + 1)
                for d in range(DT3):
                    mm = pe.matmul(banks[d][:, 0:CT], consts["ident"][:], prod[:, s % DEEP, d * CT:(d + 1) * CT],
                                   start=(s == 0), stop=(s == DS - 1))
                mm.then_inc(reduced, 1)

            def states(n, l, c):
                for s in range(DS):
                    if s + LEAD < DS:
                        spread_b(n, c, s + LEAD)
                    elif not is_last(n):
                        spread_b(n + 1, c + 1, s + LEAD - DS)
                    spread_c(n, c, s)
                    if s >= LAG:
                        reduce(n, s - LAG)
                    elif not is_first(n):
                        reduce(n - 1, DS - LAG + s)
                    if not is_last(n):
                        start(n + 1, l + (c + 1) // NC, (c + 1) % NC, s)
                    if s == AT["project out"] and not is_first(n):
                        project_out(n - 1, l if c else l - 1)

            for s in range(DS):
                start(0, 0, 0, s)
            for s in range(LEAD):
                spread_b(0, 0, s)
            all_chunks(pe, states)
            last = NC * LAYERS - 1
            for s in range(DS - LAG, DS):
                reduce(last, s)
            project_out(last, LAYERS - 1)

        @block.scalar
        def _(act):
            start_at_one(act, dt_stored)
            act.preload_act_table_set("natural_log_exp_and_others")
            act.wait_ge(a_landed, 16)
            act.wait_ge(low_rank_zeroed, 2)
            act.activation(a_exp[:], a_exp[:], ACT.Exp).then_inc(a_exped, 1)
            act.wait_ge(a_exped, 1)

            def affine(n, l):
                act.wait_ge(norm.scaled, n + 1)
                act.wait_ge(in_landed, 48 * l + 48)
                act.wait_ge(in_summed, Z * n + 1)
                for k in range(2):
                    last = act.activation(un[:, k], xn[:, k], ACT.Identity, bias=norm_b[:, k:k + 1], scale=norm_w[:, k:k + 1])
                last.then_inc(affined, 1)

            def store_in(n, c, m):
                act.wait_ge(in_summed, Z * n + m + 2)
                bank = banks[6 + m % 2][:, 0:CT]
                if m < DT3:
                    if m == 0:
                        act.wait_ge(tapped, TAPS * DT3 * n + 1)
                    act.activation(padded[:, m, :, DCONV - 1:], bank.rearrange("p (b t) -> p b t", t=T), ACT.Copy).then_inc(in_stored, 1)
                else:
                    if m == DT3 and not is_early(n):
                        act.wait_ge(gated, n - 1)
                    act.activation(zs[:, c % 2, m - DT3], bank, ACT.Copy).then_inc(in_stored, 1)

            def first_tap(n, d):
                act.wait_ge(in_stored, Z * n + d + 1)
                if d == 0:
                    act.wait_ge(dt_fixed, n + 1)
                act.activation(conv[:, d].rearrange("p (b t) -> p b t", t=T), padded[:, d, :, 0:T], ACT.Identity,
                               bias=conv_b[:, d:d + 1], scale=conv_w[:, d, 0:1]).then_inc(tap0, 1)

            def silus(n, c):
                act.wait_ge(in_stored, Z * n + Z)
                act.activation(zs[:, c % 2], zs[:, c % 2], ACT.Silu).then_inc(z_silued, 1)
                act.wait_ge(tapped, TAPS * DT3 * (n + 1) + 1)
                act.activation(xa[:, c % 2], conv[:], ACT.Silu).then_inc(conv_silued, 1)
                act.preload_act_table_set("natural_log_exp_and_others")

            def low_rank(n):
                low = slice(2 * DS, 2 * DS + DTR)
                act.wait_ge(x_summed, n + 1)
                act.wait_ge(dt_summed, DT3 * n + 1)
                act.activation(dtr[low, :], banks[6][low, 0:CT], ACT.Copy).then_inc(dtr_stored, 1)

            def store_mid(n, c):
                act.wait_ge(bc_step, 4 * n + 3)
                act.activation(bc[2 * DS:4 * DS, c % 2], mid[:], ACT.Copy).then_inc(bc_mid_stored, 1)

            def soften(n):
                if not is_first(n):
                    act.wait_ge(dt_ready, n)
                for d in range(DT3):
                    act.wait_ge(dt_summed, DT3 * n + d + 2)
                    act.activation(xb[:, d], banks[7 - d % 2][:, 0:CT], ACT.Identity, bias=dt_b[:, d:d + 1]).then_inc(dt_stored, 1)
                act.wait_ge(dt_stored, DT3 * (n + 1) + 1)
                act.activation(eb[:], xb[:], ACT.Abs).then_inc(dt_absed, 1)
                act.wait_ge(dt_absed, n + 1)
                act.activation(eb[:], eb[:], ACT.Exp, scale=-1.0).then_inc(dt_exped, 1)

            def soften_log(n):
                act.wait_ge(dt_lost, n + 1)
                act.activation(ub[:], ub[:], ACT.Ln).then_inc(dt_logged, 1)

            def start(n, l, c, s):
                if s == AT["square"]:
                    norm.act_square(act, n, sq[:], xc[:])
                if s == AT["root"]:
                    norm.act_invert_root(act, n)
                if s == AT["affine"]:
                    affine(n, l)
                for m in range(Z):
                    if s == AT["store"][m]:
                        store_in(n, c, m)
                for d in range(DT3):
                    if s == AT["first tap"][d]:
                        first_tap(n, d)
                if s == AT["silus"]:
                    silus(n, c)
                if s == AT["low rank"]:
                    low_rank(n)
                if s == AT["store mid"]:
                    store_mid(n, c)
                if s == AT["soften"]:
                    soften(n)
                if s == AT["log"]:
                    soften_log(n)

            def states(n, l, c):
                if c == 0:
                    if not is_first(n):
                        act.wait_ge(decayed, DS * n)
                    act.activation(a_neg[:], a_exp[:, bass.ds(l, 1)].rearrange("p a k -> p (a k)"), ACT.Copy, scale=-1.0).then_inc(a_ready, 1)
                    act.wait_ge(a_ready, l + 1)
                act.wait_ge(dt_ready, n + 1)
                for s in range(DS):
                    i = DS * n + s
                    early = is_first(n) and s < DEEP
                    if not early:
                        act.wait_ge(scanned, i - DEEP + 1)
                    for d in range(DT3):
                        last = act.activation(da[:, s % DEEP, d, :, 1:], dt[:, c % 2, d].rearrange("p (b t) -> p b t", t=T)[:, :, 1:],
                                              ACT.Exp, scale=a_neg[:, d * DS + s:d * DS + s + 1])
                    last.then_inc(decayed, 1)
                    act.wait_ge(c_spread, i + 1)
                    if not early:
                        act.wait_ge(produced, i - DEEP + 1)
                    act.activation(cs[:, s % DEEP], banks[5][:, 0:CT], ACT.Copy).then_inc(c_stored, 1)
                    if not is_last(n):
                        start(n + 1, l + (c + 1) // NC, (c + 1) % NC, s)

            for s in range(DS):
                start(0, 0, 0, s)
            all_chunks(act, states)

        @block.vector
        def _(dve):
            start_at_one(dve, added, skipped, tapped, dt_fixed)
            dve.memset(da[:, :, :, :, 0:1], 0.0)
            dve.memset(padded[:, :, :, 0:DCONV - 1], 0.0).then_inc(zeroed, 1)
            dve.wait_ge(zeroed, 1)

            def convolve(n, d):
                dve.wait_ge(tap0, DT3 * n + d + 1)
                out = conv[:, d].rearrange("p (b t) -> p b t", t=T)
                for k in range(1, DCONV):
                    if k > 1:
                        dve.wait_ge(tapped, TAPS * (DT3 * n + d) + k)
                    dve.scalar_tensor_tensor(out, padded[:, d, :, k:k + T], conv_w[:, d, k:k + 1], out, ALU.mult,
                                             ALU.add).then_inc(tapped, 1)

            def split_bc(n, c):
                dve.wait_ge(x_summed, n + 1)
                if not is_first(n):
                    dve.wait_ge(bc_mid_stored, n)
                summed = banks[6][0:2 * DS, 0:CT]
                high = bc[0:2 * DS, c % 2]
                dve.tensor_copy(high, summed).then_inc(bc_step, 1)
                dve.wait_ge(bc_step, 4 * n + 1)
                dve.tensor_tensor(rest[:], summed, high, ALU.subtract).then_inc(bc_step, 1)
                dve.wait_ge(bc_step, 4 * n + 2)
                dve.tensor_copy(mid[:], rest[:]).then_inc(bc_step, 1)
                dve.wait_ge(bc_step, 4 * n + 3)
                dve.tensor_tensor(bc[4 * DS:6 * DS, c % 2], rest[:], mid[:], ALU.subtract).then_inc(bc_step, 1)

            def soften(n):
                dve.wait_ge(dt_exped, n + 1)
                dve.tensor_scalar(ub[:], eb[:], 1.0, None, ALU.add).then_inc(dt_one, 1)
                dve.wait_ge(dt_one, n + 1)
                dve.scalar_tensor_tensor(lost[:], ub[:], -1.0, eb[:], ALU.add, ALU.subtract).then_inc(dt_lost, 1)

            def finish_dt(n, c):
                dve.wait_ge(dt_logged, n + 1)
                dve.tensor_tensor(lost[:], ub[:], lost[:], ALU.subtract).then_inc(dt_fixed, 1)
                dve.wait_ge(dt_fixed, n + 2)
                dve.scalar_tensor_tensor(dt[:, c % 2], xb[:], 0.0, lost[:], ALU.max, ALU.add).then_inc(dt_ready, 1)
                dve.wait_ge(dt_ready, n + 1)
                dve.wait_ge(conv_silued, n + 1)
                dve.tensor_tensor(dtx[:, c % 2], dt[:, c % 2], xa[:, c % 2], ALU.mult).then_inc(dtx_ready, 1)

            def start(n, c, s):
                if s == AT["centre"]:
                    norm.dve_centre(dve, n, xc[:], chunk(resid, c))
                if s == AT["eps"]:
                    norm.dve_eps(dve, n)
                if s == AT["scale"]:
                    if not is_first(n):
                        dve.wait_ge(affined, n)
                    norm.dve_scale(dve, n, xn[:], xc[:])
                for d in range(DT3):
                    if s == AT["convolve"][d]:
                        convolve(n, d)
                if s == AT["split"]:
                    split_bc(n, c)
                if s == AT["plus one"]:
                    soften(n)
                if s == AT["finish"]:
                    finish_dt(n, c)

            def add_skip(n, l, c):
                dve.wait_ge(reduced, DS * (n + 1) + 1)
                dve.wait_ge(out_landed, 16 * l + 16)
                dve.wait_ge(out_summed, n + 1)
                for d in range(DT3):
                    dve.scalar_tensor_tensor(yg[:, d], xa[:, c % 2, d], skip[:, d:d + 1], banks[d][:, 0:CT],
                                             ALU.mult, ALU.add).then_inc(skipped, 1)

            def add_mixed(n, c):
                dve.wait_ge(out_summed, n + 2)
                for k in range(2):
                    last = dve.tensor_tensor(resid[:, k, c * CT:(c + 1) * CT], resid[:, k, c * CT:(c + 1) * CT],
                                             banks[6 + k][0:DH, 0:CT], ALU.add)
                last.then_inc(added, 1)

            def feed(n, c, s):
                i = DS * n + s
                dve.wait_ge(b_spread, i + 1)
                if s == 0:
                    dve.wait_ge(dtx_ready, n + 1)
                if not (is_first(n) and s < DEEP):
                    dve.wait_ge(scanned, i - DEEP + 1)
                dve.tensor_tensor(dbx[:, s % DEEP].rearrange("p (d t) -> p d t", d=DT3), dtx[:, c % 2],
                                  banks[3 + s % 2][:, 0:CT].unsqueeze(1).broadcast_to([128, DT3, CT]), ALU.mult).then_inc(fed, 1)

            def states(n, l, c):
                for s in range(DS):
                    i = DS * n + s
                    if s + 1 < DS:
                        feed(n, c, s + 1)
                    elif not is_last(n):
                        feed(n + 1, c + 1, 0)
                    dve.wait_ge(fed, i + 1)
                    dve.wait_ge(decayed, i + 1)
                    if not (is_first(n) and s < DEEP):
                        dve.wait_ge(produced, i - DEEP + 1)
                    dve.tensor_tensor_scan(hs[:, s % DEEP], da[:, s % DEEP].rearrange("p d b t -> p (d b t)"), dbx[:, s % DEEP], 0.0,
                                           ALU.mult, ALU.add).then_inc(scanned, 1)
                    if not is_last(n):
                        start(n + 1, (c + 1) % NC, s)
                    if not is_first(n):
                        if s == AT["skip"]:
                            add_skip(n - 1, l if c else l - 1, (c - 1) % NC)
                        elif s == AT["mixed"]:
                            add_mixed(n - 1, (c - 1) % NC)

            for s in range(DS):
                start(0, 0, s)
            feed(0, 0, 0)
            all_chunks(dve, states)
            last = NC * LAYERS - 1
            add_skip(last, LAYERS - 1, NC - 1)
            add_mixed(last, NC - 1)

        @block.gpsimd
        def _(pool):
            pool.memset(dtw[:], 0.0).then_inc(low_rank_zeroed, 1)
            pool.wait_ge(low_rank_zeroed, 1)
            pool.memset(dtr[:], 0.0).then_inc(low_rank_zeroed, 1)
            pool.wait_ge(low_rank_zeroed, 2)

            def gate(n, c):
                pool.wait_ge(skipped, DT3 * (n + 1) + 1)
                pool.wait_ge(z_silued, n + 1)
                pool.tensor_tensor(yg[:], yg[:], zs[:, c % 2], ALU.mult).then_inc(gated, 1)

            def states(n, l, c):
                for s in range(DS):
                    i = DS * n + s
                    pool.wait_ge(scanned, i + 1)
                    pool.wait_ge(c_stored, i + 1)
                    if not (is_first(n) and s < DEEP):
                        pool.wait_ge(reduced, i - DEEP + 2)
                    pool.tensor_tensor(prod[:, s % DEEP].rearrange("p (d t) -> p d t", d=DT3),
                                       hs[:, s % DEEP].rearrange("p (d t) -> p d t", d=DT3),
                                       cs[:, s % DEEP].unsqueeze(1).broadcast_to([128, DT3, CT]), ALU.mult).then_inc(produced, 1)
                    if s == AT["gate"] and not is_first(n):
                        gate(n - 1, (c - 1) % NC)

            all_chunks(pool, states)
            gate(NC * LAYERS - 1, NC - 1)


def normalise_tokens(nc, tag, banks, consts, src, dst):
    with ExitStack() as ctx:
        sb = lambda name, shape, dt=F32: ctx.enter_context(nc.sbuf_tensor(f"{tag}_{name}", shape, dt))
        sem = ctx.enter_context(Semaphores(nc, tag + "_"))
        xc, sq = sb("nt_xc", [DH, 2, N]), sb("nt_sq", [DH, 2, N])
        on_pe, on_dve, on_act, _ = whole_norm(sb, sem, "nt", banks, consts, src, xc, sq, dst)
        block = ctx.enter_context(nc.Block())
        block.tensor(on_pe)
        block.vector(on_dve)
        block.scalar(on_act)


def add_last_norm(nc, banks, consts, stream, resid, last_wb):
    with ExitStack() as ctx:
        sb = lambda name, shape, dt=F32: ctx.enter_context(nc.sbuf_tensor(name, shape, dt))
        sem = ctx.enter_context(Semaphores(nc))
        xc, sq, xn = sb("ln_xc", [DH, 2, N]), sb("ln_sq", [DH, 2, N]), sb("ln_xn", [DH, 2, N])
        wb = sb("ln_wb", [DH, 2, 2])
        wb_landed, affined = sem("last_wb_landed"), sem("last_affined")
        on_pe, on_dve, on_act, scaled = whole_norm(sb, sem, "ln", banks, consts, resid, xc, sq, xn)
        block = ctx.enter_context(nc.Block())
        block.tensor(on_pe)

        @block.sync
        def _(sp):
            sp.dma_start(wb[:], last_wb).then_inc(wb_landed, 16)

        @block.scalar
        def _(act):
            on_act(act)
            act.wait_ge(wb_landed, 16)
            for c in range(NC):
                act.wait_ge(scaled, c + 1)
                for k in range(2):
                    last = act.activation(xn[:, k, c * CT:(c + 1) * CT], xn[:, k, c * CT:(c + 1) * CT], ACT.Identity,
                                          bias=wb[:, 1, k:k + 1], scale=wb[:, 0, k:k + 1])
                last.then_inc(affined, 1)

        @block.vector
        def _(dve):
            on_dve(dve)
            for c in range(NC):
                dve.wait_ge(affined, c + 1)
                dve.tensor_tensor(chunk(stream, c), chunk(stream, c), chunk(xn, c), ALU.add)


CONSTS = {"mean": ([DH, DH], F32), "ident": ([128, 128], F32), "ones": ([128, 128], F32), "rotate": ([128, 128], F32),
          "mask": ([GT, GT], F32), "before": ([RT, RT], F32), "counting": ([RT, NT], F32), "tile_starts": ([RT, NT], F32),
          "expert_starts": ([RT, E], F32), "own_rows": ([RT, RG, 2], F32)}


def constants():
    f = np.float32
    rotate = np.zeros((128, 128), f)
    for h in range(4):
        for i in range(0, HD, 2):
            rotate[32 * h + i + 1, 32 * h + i] = -1.0
            rotate[32 * h + i, 32 * h + i + 1] = 1.0
    seq = np.arange(GT) // T
    freq = (1.0 / 10000.0 ** (np.arange(0, HD, 2, dtype=f) / f(HD))).astype(f)
    angle = np.arange(T, dtype=f)[:, None] * freq[None]
    angle = np.concatenate([angle, angle], -1).T
    rope = np.zeros((128, 2, CB, T), f)
    for h in range(4):
        rope[32 * h:32 * h + HD, 0] = np.cos(angle)[:, None]
        rope[32 * h:32 * h + HD, 1] = np.sin(angle)[:, None]
    return {
        "mean": np.full((DH, DH), 1.0 / D, f), "ident": np.eye(128, dtype=f), "ones": np.ones((128, 128), f), "rotate": rotate,
        "mask": np.where(seq[:, None] == seq[None], 0.0, MASKED).astype(f),
        "before": np.triu(np.ones((RT, RT), f), 1), "counting": np.tile(np.arange(NT, dtype=f), (RT, 1)),
        "tile_starts": np.tile(np.arange(NT, dtype=f) * TS, (RT, 1)), "expert_starts": np.tile(np.arange(E, dtype=f) * CAP, (RT, 1)),
        "own_rows": (E * CAP + np.arange(2 * RG * RT, dtype=f)).reshape(RG, RT, 2).swapaxes(0, 1),
        "part_rows": np.tile(np.eye(2 * DS, dtype=f), (3, 1))}, rope.reshape(128, 2, CT)


def audio_tower(nc, a, out, probe=None):
    with ExitStack() as ctx:
        sb = lambda name, shape, dt=F32: ctx.enter_context(nc.sbuf_tensor(name, shape, dt))
        psum = ctx.enter_context(nc.psum_tensor("banks", [128, 8, 512], F32))
        banks = [psum[:, b] for b in range(8)]
        stream = sb("stream", [DH, 2, N])
        resid = sb("resid", [DH, 2, N])
        consts = {name: sb("const_" + name, shape, dt) for name, (shape, dt) in CONSTS.items()}
        consts["spread"] = sb("const_spread", [6 * DS, 2 * DS, 128], BF16)

        def show(tile):
            done = ctx.enter_context(nc.semaphore("probe"))
            with nc.Block() as block:
                @block.sync
                def _(sp):
                    sp.dma_start(out, tile).then_inc(done, 16)
                    sp.wait_ge(done, 16)

        dram = lambda name, rows: nc.dram_tensor(name, (rows, D), F32, kind="Internal").ap()
        slots0, results0 = dram("slots0", E * CAP + 2 * N), dram("results0", E * CAP)
        slots1, results1 = dram("slots1", NT * TS), dram("results1", NT * TS)

        embed(nc, banks, stream, a["x"], a["tok_w"], a["tok_b"], consts, {name: a[name] for name in (*CONSTS, "part_rows")},
              (slots0[0:E * CAP], slots1))
        if probe == "embed":
            return show(stream[:])
        attention(nc, banks, stream, consts, a["qk_w"], a["qk_b"], a["v_w"], a["v_b"], a["attn_out_w"], a["attn_out_b"], a["rope"])
        if probe == "attn":
            return show(stream[:])
        with ExitStack() as inner:
            isb = lambda name, shape, dt=F32: inner.enter_context(nc.sbuf_tensor("moe0_" + name, shape, dt))
            xf = isb("x", [DH, 2, N])
            r = routed_rows(isb)
            r["weight_sum"] = isb("weight_sum", [RT, RG])
            gw, gate_landed = isb("gate_w", [DH, 2, E]), inner.enter_context(nc.semaphore("moe0_gate_landed"))
            start_loads(nc, [(gw, a["gate0_w"], gate_landed)])
            normalise_tokens(nc, "norm0", banks, consts, stream, xf)
            route(nc, "route0", banks, consts, stream, xf, gw, None, gate_landed, r, slots0, None, CAP)
            gated_experts(nc, banks, consts, slots0, results0, a["moe0_in"], a["moe0_out"], a["moe0_norm"])
            combine(nc, "combine0", banks, consts, stream, r, results0, resid=resid)
        if probe == "moe0":
            return show(stream[:])
        state_space(nc, banks, consts, resid, a["ss_in"], a["ss_conv"], a["ss_dt_w"], a["ss_out"], a["ss_a_log"])
        add_last_norm(nc, banks, consts, stream, resid, a["last_wb"])
        if probe == "mamba":
            return show(stream[:])
        with ExitStack() as inner:
            isb = lambda name, shape, dt=F32: inner.enter_context(nc.sbuf_tensor("moe1_" + name, shape, dt))
            xn = isb("x", [DH, 2, N])
            r = routed_rows(isb)
            tiles_of = isb("tile_expert", [1, NT], U32)
            w = {"in": isb("all_in", [DH, E, 2, H1]), "b_in": isb("all_b_in", [128, E, H1 // 128]),
                 "out": isb("all_out", [128, E, H1 // 128, D]), "b_out": isb("all_b_out", [TS, E, D])}
            weights_landed = inner.enter_context(nc.semaphore("moe1_weights_landed"))
            gw, gb, gate_landed = isb("gate_w", [DH, 2, E]), isb("gate_b", [RT, E]), inner.enter_context(nc.semaphore("moe1_gate_landed"))
            start_loads(nc, [(gw, a["gate1_w"], gate_landed), (gb, a["gate1_b"], gate_landed)]
                        + [(w[name], a["moe1_" + name], weights_landed) for name in ("in", "b_in", "out", "b_out")])
            normalise_tokens(nc, "norm1", banks, consts, stream, xn)
            route(nc, "route1", banks, consts, stream, xn, gw, gb, gate_landed, r, slots1, tiles_of, None)
            tiled_experts(nc, banks, consts, slots1, results1, tiles_of, w, weights_landed)
            combine(nc, "combine1", banks, consts, stream, r, results1, out=out)


def routed_rows(sb):
    return {"x_rows": sb("x_rows", [RT, RG, D]), "stream_rows": sb("stream_rows", [RT, RG, D]),
            "weights": sb("pair_weights", [RT, RG, 2]), "source": sb("gather_rows", [RT, RG, 2], U32)}


def halves(w):
    return w.reshape(2, DH, *w.shape[1:]).swapaxes(0, 1)


def tiles(w, n):
    return w.reshape(n, 128, *w.shape[1:]).swapaxes(0, 1)


def laid_out(i):
    a, a["rope"] = constants()
    a["x"] = i["x"]
    a["tok_w"] = np.zeros((CHANNEL_ROWS, PATCH, D), np.float32)
    a["tok_w"][:CHANNELS] = i["L0_tok_W"].reshape(D, CHANNELS, PATCH).transpose(1, 2, 0)
    a["tok_b"] = halves(i["L0_tok_b"])
    wqkv, bqkv = i["L0_attn_W_qkv"], i["L0_attn_b_qkv"]
    qk_w, qk_b = np.zeros((D, 2, QT, 4, 32), np.float32), np.zeros((2, QT, 4, 32), np.float32)
    qk_w[..., :HD] = wqkv[:, :2 * D].reshape(D, 2, QT, 4, HD)
    qk_b[..., :HD] = bqkv[:2 * D].reshape(2, QT, 4, HD)
    a["qk_w"] = halves(qk_w.reshape(D, 2 * QT, 128))
    a["qk_b"] = qk_b.reshape(2 * QT, 128).T
    a["v_w"] = halves(wqkv[:, 2 * D:])
    a["v_b"] = np.tile(bqkv[2 * D:], (GT, 1))
    a["attn_out_w"] = halves(i["L0_attn_W_out"])
    a["attn_out_b"] = halves(i["L0_attn_b_out"])
    a["gate0_w"] = halves(i["L0_ffn_gate_w"].T)
    a["moe0_in"] = np.stack([halves(w.T) for w in i["L0_ffn_w13"]])
    a["moe0_out"] = np.stack([tiles(w.T, H0 // 128) for w in i["L0_ffn_w2"]])
    a["moe0_norm"] = np.stack([halves(w) for w in i["L0_ffn_norm_w"]], 1)
    m = {k[len("L1_attn_"):]: v for k, v in i.items() if k.startswith("L1_attn_")}
    a["ss_in"] = np.stack([np.concatenate([halves(m["in_proj_w"][l].T).reshape(DH, -1), halves(m["norm_w"][l]), halves(m["norm_b"][l])], 1)
                           for l in range(LAYERS)])
    x_w = np.concatenate([m["x_proj_w"][:, DTR:], m["x_proj_w"][:, :DTR]], 1)
    flat = lambda w: tiles(w, DT3).reshape(128, -1)
    a["ss_conv"] = np.stack([np.concatenate([flat(m["conv_w"][l]), flat(m["conv_b"][l]), flat(m["dt_proj_b"][l]), flat(x_w[l].T)], 1)
                             for l in range(LAYERS)])
    a["ss_dt_w"] = m["dt_proj_w"].transpose(0, 2, 1)
    a["ss_out"] = np.stack([np.concatenate([flat(m["D_skip"][l]), flat(m["out_proj_w"][l].T)], 1) for l in range(LAYERS)])
    a["ss_a_log"] = np.stack([flat(w) for w in m["A_log"]], 1)
    a["last_wb"] = np.stack([halves(m["norm_f_w"]), halves(m["norm_f_b"])], 1)
    a["gate1_w"] = halves(i["L1_ffn_Wg"].T)
    a["gate1_b"] = np.tile(i["L1_ffn_bg"], (RT, 1))
    a["moe1_in"] = np.stack([halves(w) for w in i["L1_ffn_W1"]], 1)
    a["moe1_out"] = np.stack([tiles(w, H1 // 128) for w in i["L1_ffn_W2"]], 1)
    a["moe1_b_in"] = np.stack([tiles(b, H1 // 128) for b in i["L1_ffn_b1"]], 1)
    a["moe1_b_out"] = np.tile(i["L1_ffn_b2"], (TS, 1, 1))
    return {name: np.ascontiguousarray(v) for name, v in a.items()}


def kernel(**inputs):
    import concourse.bacc as bacc
    from concourse.bass_utils import run_bass_kernel_spmd

    arrays = laid_out({name: np.asarray(v) for name, v in inputs.items()})
    nc = bacc.Bacc("TRN2", target_bir_lowering=False, num_devices=1)
    dram = {name: nc.dram_tensor("in_" + name, v.shape, mybir.dt.from_np(v.dtype), kind="ExternalInput").ap() for name, v in arrays.items()}
    out = nc.dram_tensor("out", (SEQS, T, D), F32, kind="ExternalOutput").ap()
    audio_tower(nc, dram, out)
    result = run_bass_kernel_spmd(nc, [{"in_" + name: v for name, v in arrays.items()}], core_ids=[0])
    return result.results[0]["out"]
```
